# Optimizing a Trainium2 kernel written in Bass

```python
import numpy as np
import jax
import jax.numpy as jnp

def _softmax(x, axis=-1):
    return jax.nn.softmax(x, axis=axis)

def _gelu(x):
    return jax.nn.gelu(x, approximate=True)

def _silu(x):
    return jax.nn.silu(x)

def _sigmoid(x):
    return jax.nn.sigmoid(x)

def _layernorm(x, axis=-1, eps=1e-05):
    m = jnp.mean(x, axis=axis, keepdims=True)
    v = jnp.var(x, axis=axis, keepdims=True)
    return (x - m) / jnp.sqrt(v + eps)

def _scatter_add(tgt, idx, src, axis=0):
    return tgt.at[idx].add(src)

def _segment_sum(src, seg, n):
    return jax.ops.segment_sum(src, seg, n)
kernel_name = 'mk_hybrid_d1_jaxref_r8_6f90a3'

def setup_inputs(seed: int=0):
    np.random.seed(seed)
    _w = jnp.asarray

    def _L0_attn_a_setup():
        import math
        import jax, jax.numpy as jnp
        import numpy as np
        N_EMBD = 128
        N_HEAD = 16
        B, T = (2, 256)

        def _heads(t):
            b, s, d = t.shape
            return t.reshape(b, s, N_HEAD, d // N_HEAD).transpose(0, 2, 1, 3)
        key = jax.random.key(seed)
        ks = jax.random.split(key, 7)
        D = N_EMBD
        s = 0.02
        return {'x': jax.random.normal(ks[0], (B, T, D), dtype=jnp.float32), 'w_attn': jax.random.normal(ks[1], (2 * D, D), dtype=jnp.float32) * s, 'b_attn': jnp.zeros((2 * D,), dtype=jnp.float32), 'w_k2': jax.random.normal(ks[2], (D, D), dtype=jnp.float32) * s, 'b_k2': jnp.zeros((D,), dtype=jnp.float32), 'w_proj': jax.random.normal(ks[3], (D, D), dtype=jnp.float32) * s, 'b_proj': jnp.zeros((D,), dtype=jnp.float32)}
    _L0_attn_a_in = _L0_attn_a_setup()

    def _L0_attn_b_setup():
        import jax, jax.numpy as jnp
        import numpy as np
        from jax import lax
        D_MODEL, D_STATE, D_CONV, D_INNER, DT_RANK = (128, 16, 4, 256, 64)
        B_SZ, SEQ = (2, 128)

        def silu(v):
            return v * jax.nn.sigmoid(v)

        def _mamba_fwd(x, W_in, conv_w, conv_b, W_x, W_dt, b_dt, A_log, D, W_out):
            b, l, _ = x.shape
            xz = x @ W_in
            x_e, z = jnp.split(xz, 2, axis=-1)
            xc = lax.conv_general_dilated(x_e.transpose(0, 2, 1), conv_w, window_strides=(1,), padding=[(D_CONV - 1, 0)], dimension_numbers=('NCH', 'OIH', 'NCH'), feature_group_count=D_INNER)
            xc = (xc + conv_b[None, :, None]).transpose(0, 2, 1)
            xc = silu(xc)
            x_dbl = xc @ W_x
            delta_r = x_dbl[..., :DT_RANK]
            Bmat = x_dbl[..., DT_RANK:DT_RANK + D_STATE]
            Cmat = x_dbl[..., DT_RANK + D_STATE:]
            delta = jax.nn.softplus(delta_r @ W_dt + b_dt)
            A = -jnp.exp(A_log)
            deltaA = jnp.exp(delta[..., None] * A[None, None])
            deltaB_x = delta[..., None] * Bmat[:, :, None, :] * xc[..., None]

            def combine(left, right):
                a_l, b_l = left
                a_r, b_r = right
                return (a_r * a_l, a_r * b_l + b_r)
            _, H = lax.associative_scan(combine, (deltaA, deltaB_x), axis=1)
            y = jnp.einsum('bldn,bln->bld', H, Cmat) + xc * D[None, None, :]
            y = y * silu(z)
            return y @ W_out
        key = jax.random.key(seed)
        ks = jax.random.split(key, 10)
        s = lambda fan: 1.0 / np.sqrt(fan)
        x = jax.random.normal(ks[0], (B_SZ, SEQ, D_MODEL), jnp.float32)
        W_in = jax.random.normal(ks[1], (D_MODEL, 2 * D_INNER), jnp.float32) * s(D_MODEL)
        conv_w = jax.random.normal(ks[2], (D_INNER, 1, D_CONV), jnp.float32) * s(D_CONV)
        conv_b = jax.random.normal(ks[3], (D_INNER,), jnp.float32) * 0.01
        W_x = jax.random.normal(ks[4], (D_INNER, DT_RANK + 2 * D_STATE), jnp.float32) * s(D_INNER)
        W_dt = jax.random.normal(ks[5], (DT_RANK, D_INNER), jnp.float32) * s(DT_RANK)
        b_dt = jax.random.normal(ks[6], (D_INNER,), jnp.float32) * 0.01
        A_log = jnp.log(jnp.tile(jnp.arange(1, D_STATE + 1, dtype=jnp.float32), (D_INNER, 1)))
        Dparam = jnp.ones((D_INNER,), jnp.float32)
        W_out = jax.random.normal(ks[7], (D_INNER, D_MODEL), jnp.float32) * s(D_INNER)
        return {'x': x, 'W_in': W_in, 'conv_w': conv_w, 'conv_b': conv_b, 'W_x': W_x, 'W_dt': W_dt, 'b_dt': b_dt, 'A_log': A_log, 'D': Dparam, 'W_out': W_out}
    _L0_attn_b_in = _L0_attn_b_setup()

    def _L0_ffn_setup():
        import jax, jax.numpy as jnp
        import numpy as np
        D_MODEL = 128
        HIDDEN = 256
        N_EXPERTS = 8
        TOP_K = 2
        key = jax.random.key(seed)
        ks = jax.random.split(key, 9)
        s = 0.02
        x = jax.random.normal(ks[0], (4, 256, D_MODEL), dtype=jnp.float32)
        sw1 = jax.random.normal(ks[1], (D_MODEL, HIDDEN), dtype=jnp.float32) * s
        sw2 = jax.random.normal(ks[2], (D_MODEL, HIDDEN), dtype=jnp.float32) * s
        sw3 = jax.random.normal(ks[3], (HIDDEN, D_MODEL), dtype=jnp.float32) * s
        ew1 = jax.random.normal(ks[4], (N_EXPERTS, D_MODEL, HIDDEN), dtype=jnp.float32) * s
        ew2 = jax.random.normal(ks[5], (N_EXPERTS, D_MODEL, HIDDEN), dtype=jnp.float32) * s
        ew3 = jax.random.normal(ks[6], (N_EXPERTS, HIDDEN, D_MODEL), dtype=jnp.float32) * s
        rw = jax.random.normal(ks[7], (D_MODEL, N_EXPERTS), dtype=jnp.float32) * s
        rb = jax.random.normal(ks[8], (N_EXPERTS,), dtype=jnp.float32) * s
        return {'x': x, 'sw1': sw1, 'sw2': sw2, 'sw3': sw3, 'ew1': ew1, 'ew2': ew2, 'ew3': ew3, 'rw': rw, 'rb': rb}
    _L0_ffn_in = _L0_ffn_setup()
    _d = {'L0_attn_a_x': _L0_attn_a_in['x'], 'L0_attn_a_w_attn': _L0_attn_a_in['w_attn'], 'L0_attn_a_b_attn': _L0_attn_a_in['b_attn'], 'L0_attn_a_w_k2': _L0_attn_a_in['w_k2'], 'L0_attn_a_b_k2': _L0_attn_a_in['b_k2'], 'L0_attn_a_w_proj': _L0_attn_a_in['w_proj'], 'L0_attn_a_b_proj': _L0_attn_a_in['b_proj'], 'L0_attn_b_W_in': _L0_attn_b_in['W_in'], 'L0_attn_b_conv_w': _L0_attn_b_in['conv_w'], 'L0_attn_b_conv_b': _L0_attn_b_in['conv_b'], 'L0_attn_b_W_x': _L0_attn_b_in['W_x'], 'L0_attn_b_W_dt': _L0_attn_b_in['W_dt'], 'L0_attn_b_b_dt': _L0_attn_b_in['b_dt'], 'L0_attn_b_A_log': _L0_attn_b_in['A_log'], 'L0_attn_b_D': _L0_attn_b_in['D'], 'L0_attn_b_W_out': _L0_attn_b_in['W_out'], 'L0_ffn_sw1': _L0_ffn_in['sw1'], 'L0_ffn_sw2': _L0_ffn_in['sw2'], 'L0_ffn_sw3': _L0_ffn_in['sw3'], 'L0_ffn_ew1': _L0_ffn_in['ew1'], 'L0_ffn_ew2': _L0_ffn_in['ew2'], 'L0_ffn_ew3': _L0_ffn_in['ew3'], 'L0_ffn_rw': _L0_ffn_in['rw'], 'L0_ffn_rb': _L0_ffn_in['rb']}
    _x0 = _d['L0_attn_a_x']
    _d['L0_attn_a_x'] = jax.random.normal(jax.random.fold_in(jax.random.key(seed), 1), (4, 1024, 128), dtype=_x0.dtype)
    del _x0
    return _d

def reference(L0_attn_a_x, L0_attn_a_w_attn, L0_attn_a_b_attn, L0_attn_a_w_k2, L0_attn_a_b_k2, L0_attn_a_w_proj, L0_attn_a_b_proj, L0_attn_b_W_in, L0_attn_b_conv_w, L0_attn_b_conv_b, L0_attn_b_W_x, L0_attn_b_W_dt, L0_attn_b_b_dt, L0_attn_b_A_log, L0_attn_b_D, L0_attn_b_W_out, L0_ffn_sw1, L0_ffn_sw2, L0_ffn_sw3, L0_ffn_ew1, L0_ffn_ew2, L0_ffn_ew3, L0_ffn_rw, L0_ffn_rb):

    def _L0_attn_a_ref(x, w_attn, b_attn, w_k2, b_k2, w_proj, b_proj):
        import math
        import jax, jax.numpy as jnp
        import numpy as np
        N_EMBD = 128
        N_HEAD = 16
        B, T = (2, 256)

        def _heads(t):
            b, s, d = t.shape
            return t.reshape(b, s, N_HEAD, d // N_HEAD).transpose(0, 2, 1, 3)
        b, t, d = x.shape
        hd = d // N_HEAD
        scale = 1.0 / math.sqrt(hd)
        qk = x @ w_attn.T + b_attn
        q, k = jnp.split(qk, 2, axis=-1)
        q, k, v = (_heads(q), _heads(k), _heads(x))
        scores = jnp.einsum('bhqd,bhkd->bhqk', q, k) * scale
        causal = jnp.tril(jnp.ones((t, t), dtype=bool))
        scores = jnp.where(causal, scores, -jnp.inf)
        y_ar = jnp.einsum('bhqk,bhkd->bhqd', jax.nn.softmax(scores, axis=-1), v)
        e = v[:, :, 1:, :] - y_ar[:, :, :-1, :]
        q2 = q[:, :, 1:, :]
        k2 = _heads(x[:, :-1] @ w_k2.T + b_k2)
        qa = -jax.nn.leaky_relu(-q2 * scale, negative_slope=0.02)
        ka = jax.nn.sigmoid(k2 * scale * 0.02)
        ma = jnp.einsum('bhqd,bhkd->bhqk', qa, ka)
        ma = jnp.where(jnp.tril(jnp.ones((t - 1, t - 1), dtype=bool)), ma, 0.0)
        y_ma = jnp.einsum('bhqk,bhkd->bhqd', ma, e)
        y_ma = jnp.concatenate([jnp.zeros_like(y_ma[:, :, :1, :]), y_ma], axis=2)

        def merge(z):
            return z.transpose(0, 2, 1, 3).reshape(b, t, d)
        out = merge(y_ar) @ w_proj.T + b_proj + (merge(y_ma) @ w_proj.T + b_proj)
        return out

    def _L0_attn_b_ref(x, W_in, conv_w, conv_b, W_x, W_dt, b_dt, A_log, D, W_out):
        import jax, jax.numpy as jnp
        import numpy as np
        from jax import lax
        D_MODEL, D_STATE, D_CONV, D_INNER, DT_RANK = (128, 16, 4, 256, 64)
        B_SZ, SEQ = (2, 128)

        def silu(v):
            return v * jax.nn.sigmoid(v)

        def _mamba_fwd(x, W_in, conv_w, conv_b, W_x, W_dt, b_dt, A_log, D, W_out):
            b, l, _ = x.shape
            xz = x @ W_in
            x_e, z = jnp.split(xz, 2, axis=-1)
            xc = lax.conv_general_dilated(x_e.transpose(0, 2, 1), conv_w, window_strides=(1,), padding=[(D_CONV - 1, 0)], dimension_numbers=('NCH', 'OIH', 'NCH'), feature_group_count=D_INNER)
            xc = (xc + conv_b[None, :, None]).transpose(0, 2, 1)
            xc = silu(xc)
            x_dbl = xc @ W_x
            delta_r = x_dbl[..., :DT_RANK]
            Bmat = x_dbl[..., DT_RANK:DT_RANK + D_STATE]
            Cmat = x_dbl[..., DT_RANK + D_STATE:]
            delta = jax.nn.softplus(delta_r @ W_dt + b_dt)
            A = -jnp.exp(A_log)
            deltaA = jnp.exp(delta[..., None] * A[None, None])
            deltaB_x = delta[..., None] * Bmat[:, :, None, :] * xc[..., None]

            def combine(left, right):
                a_l, b_l = left
                a_r, b_r = right
                return (a_r * a_l, a_r * b_l + b_r)
            _, H = lax.associative_scan(combine, (deltaA, deltaB_x), axis=1)
            y = jnp.einsum('bldn,bln->bld', H, Cmat) + xc * D[None, None, :]
            y = y * silu(z)
            return y @ W_out
        return _mamba_fwd(x, W_in, conv_w, conv_b, W_x, W_dt, b_dt, A_log, D, W_out)

    def _L0_ffn_ref(x, sw1, sw2, sw3, ew1, ew2, ew3, rw, rb):
        import jax, jax.numpy as jnp
        import numpy as np
        D_MODEL = 128
        HIDDEN = 256
        N_EXPERTS = 8
        TOP_K = 2
        shared = jnp.einsum('bth,hd->btd', jax.nn.silu(jnp.einsum('btd,dh->bth', x, sw1)) * jnp.einsum('btd,dh->bth', x, sw2), sw3)
        probs = jax.nn.softmax(jnp.einsum('btd,de->bte', x, rw) + rb, axis=-1)
        w, idx = jax.lax.top_k(probs, TOP_K)
        w = w / jnp.sum(w, axis=-1, keepdims=True)
        gates = jnp.sum(w[..., None] * jax.nn.one_hot(idx, N_EXPERTS, dtype=x.dtype), axis=-2)
        h = jax.nn.silu(jnp.einsum('btd,edh->beth', x, ew1)) * jnp.einsum('btd,edh->beth', x, ew2)
        eout = jnp.einsum('beth,ehd->betd', h, ew3)
        routed = jnp.einsum('betd,bte->btd', eout, gates)
        return shared + routed
    x = L0_attn_a_x
    x = x + _L0_attn_a_ref(_layernorm(x, axis=-1), L0_attn_a_w_attn, L0_attn_a_b_attn, L0_attn_a_w_k2, L0_attn_a_b_k2, L0_attn_a_w_proj, L0_attn_a_b_proj)
    x = x + _L0_ffn_ref(_layernorm(x, axis=-1), L0_ffn_sw1, L0_ffn_sw2, L0_ffn_sw3, L0_ffn_ew1, L0_ffn_ew2, L0_ffn_ew3, L0_ffn_rw, L0_ffn_rb)
    x = x + _L0_attn_b_ref(_layernorm(x, axis=-1), L0_attn_b_W_in, L0_attn_b_conv_w, L0_attn_b_conv_b, L0_attn_b_W_x, L0_attn_b_W_dt, L0_attn_b_b_dt, L0_attn_b_A_log, L0_attn_b_D, L0_attn_b_W_out)
    x = x + _L0_ffn_ref(_layernorm(x, axis=-1), L0_ffn_sw1, L0_ffn_sw2, L0_ffn_sw3, L0_ffn_ew1, L0_ffn_ew2, L0_ffn_ew3, L0_ffn_rw, L0_ffn_rb)
    return x

_drawn_inputs = setup_inputs


def setup_inputs(seed=0):
    import zlib

    import numpy as np

    out = dict(_drawn_inputs(seed))
    spreads = {'L0_attn_a_b_attn': (0.0, 0.1),
     'L0_attn_a_b_k2': (0.0, 2.0),
     'L0_attn_a_b_proj': (0.0, 0.1),
     'L0_attn_b_D': (1.0, 0.2)}
    factors = {'L0_attn_a_w_k2': 8.0,
     'L0_attn_b_conv_b': 8.0,
     'L0_attn_b_b_dt': 8.0,
     'L0_ffn_sw1': 4.683,
     'L0_ffn_sw2': 4.617,
     'L0_ffn_sw3': 4.602,
     'L0_ffn_ew1': 6.695,
     'L0_ffn_ew2': 6.652,
     'L0_ffn_ew3': 6.667,
     'L0_ffn_rw': 7.877,
     'L0_ffn_rb': 8.0}
    for name, (base, spread) in spreads.items():
        noise = np.random.default_rng([zlib.crc32(name.encode()), seed]).standard_normal(out[name].shape)
        drawn = base * np.exp(spread * noise) if base else spread * noise
        out[name] = jnp.asarray(drawn.astype(out[name].dtype))
    for name, factor in factors.items():
        out[name] = (out[name] * factor).astype(out[name].dtype)
    return out
```

```python
from contextlib import ExitStack

import concourse.bass as bass
from concourse import mybir

ALU = mybir.AluOpType
ACT = mybir.ActivationFunctionType
AX = mybir.AxisListType
F32 = mybir.dt.float32
BF16 = mybir.dt.bfloat16
I32 = mybir.dt.int32

P = 128
B, T, D = 4, 1024, 128
N = B * T
HEADS, HD = 16, 8
GH = 4
GPB = HEADS // GH
GROUPS = B * GPB
BLK = T // P
PARTS = 3
COMBOS = PARTS * PARTS
KROWS = COMBOS * HD
MROW = 96
SCALE = HD ** -0.5
EPS = 1e-5
MINUS = -1e30
UNIT = 512
UPT = UNIT // P
ds = bass.ds


class Mem:

    def __init__(self, nc, ctx, stage):
        self.nc, self.ctx, self.stage, self.sems = nc, ctx, stage, []

    def sb(self, name, shape, dt=F32):
        return self.ctx.enter_context(self.nc.sbuf_tensor(f"{self.stage}_{name}", shape, dt))

    def ps(self, name, shape, dt=F32):
        return self.ctx.enter_context(self.nc.psum_tensor(f"{self.stage}_{name}", shape, dt))

    def sem(self, name):
        self.sems.append(self.ctx.enter_context(self.nc.semaphore(f"{self.stage}_{name}")))
        return self.sems[-1]

    def clear(self):
        with self.nc.Block() as block:
            @block.gpsimd
            def _(pool):
                for sem in self.sems:
                    pool.sem_clear(sem)

    def pair(self, name):
        return [self.sem(f"{name}{k}") for k in range(2)]


class Turns:

    def __init__(self, eng, name, strides):
        self.eng = eng
        self.kept = {s: eng.alloc_register(f"{name}_turn_x{s}") for s in strides}
        self.scratch = [eng.alloc_register(f"{name}_value{n}") for n in range(4)]
        self.used = 0
        for r in self.kept.values():
            eng.reg_mov(r, 0)

    def step(self):
        for s, r in self.kept.items():
            self.eng.reg_add(r, r, s)

    def at(self, stride, c):
        if c == 0:
            return self.kept[stride]
        r = self.scratch[self.used % 4]
        self.used += 1
        self.eng.reg_add(r, self.kept[stride], c)
        return r


class Linear:

    def __init__(self, turns, i, a=1, b=0):
        self.turns, self.i, self.a, self.b = turns, i, a, b

    def __mul__(self, n):
        return Linear(self.turns, self.i, self.a * n, self.b * n)

    def __add__(self, n):
        return Linear(self.turns, self.i, self.a, self.b + n)

    def __sub__(self, n):
        return self + -n


def now(v):
    return v.turns.at(v.a, v.b) if isinstance(v, Linear) else v


def constants(nc, m, dram):
    c = {}
    c["ident"] = m.sb("ident", [P, P])
    c["identb"] = m.sb("identb", [P, P], BF16)
    c["mask_rows"] = m.sb("mask_rows", [P, P], BF16)
    c["mask_cols"] = m.sb("mask_cols", [P, P], BF16)
    c["strict"] = m.sb("strict", [P, GH, P])
    c["same_head"] = m.sb("same_head", [P, P])
    zrow = m.sb("zrow", [1, D])
    filled, made, zero_stored = m.sem("filled"), m.sem("made"), m.sem("zero_stored")
    with nc.Block() as block:
        @block.gpsimd
        def _(pool):
            for t, v in ((c["ident"], 0.0), (c["identb"], 0.0), (c["mask_rows"], 0.0), (c["mask_cols"], 0.0),
                         (c["strict"], 1.0), (c["same_head"], 0.0), (zrow, 0.0)):
                nc.gpsimd.memset(t[:], v).then_inc(filled, 1)
            pool.wait_ge(filled, 7)
            nc.gpsimd.affine_select(out=c["ident"][:], in_=c["ident"][:], compare_op=ALU.not_equal, fill=1.0,
                                    base=0, pattern=[[-1, P]], channel_multiplier=1).then_inc(made, 1)
            nc.gpsimd.affine_select(out=c["identb"][:], in_=c["identb"][:], compare_op=ALU.not_equal, fill=1.0,
                                    base=0, pattern=[[-1, P]], channel_multiplier=1).then_inc(made, 1)
            nc.gpsimd.affine_select(out=c["mask_rows"][:], in_=c["mask_rows"][:], compare_op=ALU.is_ge, fill=MINUS,
                                    base=0, pattern=[[-1, P]], channel_multiplier=1).then_inc(made, 1)
            nc.gpsimd.affine_select(out=c["mask_cols"][:], in_=c["mask_cols"][:], compare_op=ALU.is_ge, fill=MINUS,
                                    base=0, pattern=[[1, P]], channel_multiplier=-1).then_inc(made, 1)
            nc.gpsimd.affine_select(out=c["strict"][:], in_=c["strict"][:], compare_op=ALU.is_gt, fill=0.0,
                                    base=0, pattern=[[0, GH], [1, P]], channel_multiplier=-1).then_inc(made, 1)
            heads = c["same_head"][:].rearrange("p (g h d) -> p g h d", g=GPB, d=HD)
            for d in range(HD):
                nc.gpsimd.affine_select(out=heads, in_=heads, compare_op=ALU.not_equal, fill=1.0, base=-GH * d,
                                        pattern=[[-GH * HD, GPB], [-1, GH], [0, HD]], channel_multiplier=1).then_inc(made, 1)
                pool.wait_ge(made, 6 + d)

        @block.sync
        def _(sp):
            sp.wait_ge(filled, 7)
            sp.dma_start(dram["xn"][N:N + 1, :], zrow[:]).then_inc(zero_stored, 16)
            sp.wait_ge(zero_stored, 16)
    return c


def project(nc, dram, c, a):
    with ExitStack() as ctx:
        m = Mem(nc, ctx, "proj")
        wrow = m.sb("wrow", [P, 3, P])
        wT = m.sb("wT", [P, 3, P])
        brow = m.sb("brow", [1, 3, P])
        bperm = m.sb("bperm", [1, 3, P])
        bias = m.sb("bias", [P, 3])
        sbias = m.sb("sbias", [P, 3])
        x = [m.sb(f"x{k}", [P, UPT, D]) for k in range(2)]
        stats = m.sb("stats", [P, UPT, 6])
        mv = m.sb("mv", [P, UPT, 2])
        veps = m.sb("veps", [P, UPT])
        power = m.sb("power", [P, UPT])
        rstd = m.sb("rstd", [P, UPT])
        xn = [m.sb(f"xn{k}", [P, UPT, D]) for k in range(2)]
        vp = [m.sb(f"vp{k}", [P, UPT, HEADS, HD + 1]) for k in range(2)]
        xnT = [m.sb(f"xnT{k}", [P, UNIT]) for k in range(2)]
        f = [m.sb(f"f{k}", [P, 4, UNIT]) for k in range(2)]
        r = [m.sb(f"r{k}", [P, 4, UNIT]) for k in range(2)]
        parts = [m.sb(f"parts{k}", [P, 4, PARTS, UNIT], BF16) for k in range(2)]
        psw = m.ps("psw", [P, UNIT])
        psx = [m.ps(f"psx{k}", [P, UNIT]) for k in range(2)]
        psq = [m.ps(f"psq{j}", [P, UNIT]) for j in range(3)]
        w_loaded, w_turned, w_ready = m.sem("w_loaded"), m.sem("w_turned"), m.sem("w_ready")
        bias_ready, ones_ready = m.sem("bias_ready"), m.sem("ones_ready")
        veps_ready, passed = m.pair("veps"), m.sem("passed")
        x_loaded, stat, mean, rstd_ready, xn_ready = (m.pair(n) for n in ("x_loaded", "stat", "mean", "rstd", "xn_ready"))
        vp_ready, xT_made, xT_ready, mm_done = (m.pair(n) for n in ("vp_ready", "xT_made", "xT_ready", "mm_done"))
        q_ready, k_ready, ka_ready, qa_ready = (m.pair(n) for n in ("q_ready", "k_ready", "ka_ready", "qa_ready"))
        part1, rest1, part2, part3 = (m.pair(n) for n in ("part1", "rest1", "part2", "part3"))
        xn_stored, vp_stored, f_stored, parts_stored = (m.pair(n) for n in ("xn_st", "vp_st", "f_st", "parts_st"))

        def unit_of(t, i, k):
            at = ds(i * T + k * UNIT, UNIT) if not isinstance(i, int) else slice(i * T + k * UNIT, i * T + (k + 1) * UNIT)
            return t[at, :].rearrange("(j p) d -> p j d", p=P)

        def ahead(i, k):
            return (i, 1) if k == 0 else (i + 1, 0)

        with nc.Block() as block:
            @block.sync
            def _(sp):
                sp.dma_start(wrow[:, 0:2, :], a["w_attn"].rearrange("(j p) d -> p j d", p=P)).then_inc(w_loaded, 16)
                sp.dma_start(wrow[:, 2, :], a["w_k2"]).then_inc(w_loaded, 16)
                sp.dma_start(brow[:, 0:2, :], a["b_attn"].rearrange("(o j p) -> o j p", o=1, p=P)).then_inc(w_loaded, 16)
                sp.dma_start(brow[:, 2, :], a["b_k2"].rearrange("(o p) -> o p", o=1)).then_inc(w_loaded, 16)
                for k in range(2):
                    sp.dma_start(x[k][:], a["x"][k * UNIT:(k + 1) * UNIT, :].rearrange("(j p) d -> p j d", p=P)).then_inc(x_loaded[k], 16)

                def stores(i, k, more):
                    sp.wait_ge(xn_ready[k], i * UPT + UPT)
                    sp.dma_start(unit_of(dram["xn"], i, k), xn[k][:]).then_inc(xn_stored[k], 16)
                    if more:
                        sp.dma_start(x[k][:], unit_of(a["x"], i + 1, k)).then_inc(x_loaded[k], 16)
                    sp.wait_ge(vp_ready[k], i + 1)
                    sp.dma_start(unit_of(dram["vp"], i, k), vp[k][:].rearrange("p j h d -> p j (h d)")).then_inc(vp_stored[k], 16)
                    for s in range(PARTS):
                        sp.wait_ge((part1, part2, part3)[s][k], i + 1)
                    sp.dma_start(dram["parts"][:, i, :, k * UNIT:(k + 1) * UNIT].rearrange("s p t -> p s t"),
                                 parts[k][:].rearrange("p q s t -> p (q s) t")).then_inc(parts_stored[k], 16)

                with sp.Fori(0, B - 1) as i:
                    for k in range(2):
                        stores(i, k, True)
                for k in range(2):
                    stores(B - 1, k, False)
                for k in range(2):
                    sp.wait_ge(xn_stored[k], B * 16)
                    sp.wait_ge(vp_stored[k], B * 16)
                    sp.wait_ge(parts_stored[k], B * 16)

            @block.vector
            def _(dve):
                dve.wait_ge(w_loaded, 64)
                for j in range(3):
                    nc.vector.tensor_copy(bperm[:, j, :].rearrange("p (g d h) -> p g d h", g=GPB, h=GH),
                                          brow[:, j, :].rearrange("p (g h d) -> p g d h", g=GPB, h=GH)).then_inc(w_ready, 1)
                dve.wait_ge(w_turned, 1)
                nc.vector.tensor_copy(bias[:], psw[:, 3 * P:3 * P + 3]).then_inc(w_ready, 1)
                for j in range(3):
                    nc.vector.tensor_copy(wT[:, j, :].rearrange("p (g d h) -> p g d h", g=GPB, h=GH),
                                          psw[:, j * P:(j + 1) * P].rearrange("p (g h d) -> p g d h", g=GPB, h=GH)).then_inc(w_ready, 1)
                dve.wait_ge(w_ready, 7)
                nc.vector.tensor_scalar(sbias[:, 1:2], bias[:, 1:2], 1.0, None, ALU.mult).then_inc(bias_ready, 1)
                nc.vector.tensor_scalar(sbias[:, 0:1], bias[:, 0:1], SCALE, None, ALU.mult).then_inc(bias_ready, 1)
                nc.vector.tensor_scalar(sbias[:, 2:3], bias[:, 2:3], SCALE * 0.02, None, ALU.mult).then_inc(bias_ready, 1)

                def normalise(i, k):
                    dve.wait_ge(x_loaded[k], i * 16 + 16)
                    for j in range(UPT):
                        nc.vector.bn_stats(stats[:, j, :], x[k][:, j, :]).then_inc(stat[k], 1)
                    dve.wait_ge(stat[k], i * UPT + UPT)
                    dve.sem_inc(passed, 1)
                    for j in range(UPT):
                        nc.vector.bn_aggr(mv[:, j, :], stats[:, j, :]).then_inc(mean[k], 1)
                    dve.wait_ge(rstd_ready[k], i + 1)
                    dve.wait_ge(xT_made[k], i)
                    dve.wait_ge(vp_ready[k], i)
                    dve.wait_ge(xn_stored[k], i * 16)
                    for j in range(UPT):
                        nc.vector.tensor_scalar(xn[k][:, j, :], x[k][:, j, :], mv[:, j, 0:1], rstd[:, j:j + 1],
                                                ALU.subtract, ALU.mult).then_inc(xn_ready[k], 1)

                def split_first(i, k):
                    dve.wait_ge(q_ready[k], i + 1)
                    nc.vector.scalar_tensor_tensor(f[k][:, 2, :], f[k][:, 0, :], 0.02, f[k][:, 0, :],
                                                   ALU.mult, ALU.min).then_inc(qa_ready[k], 1)
                    dve.wait_ge(qa_ready[k], i + 1)
                    dve.wait_ge(k_ready[k], i + 1)
                    dve.wait_ge(ka_ready[k], i + 1)
                    dve.wait_ge(parts_stored[k], i * 16)
                    nc.vector.tensor_copy(parts[k][:, :, 0, :], f[k][:]).then_inc(part1[k], 1)
                    dve.wait_ge(part1[k], i + 1)
                    dve.wait_ge(part3[k], i)
                    nc.vector.tensor_tensor(r[k][:], f[k][:], parts[k][:, :, 0, :], ALU.subtract).then_inc(rest1[k], 1)

                normalise(0, 0)
                with dve.Fori(0, B - 1) as i:
                    for k in range(2):
                        normalise(*ahead(i, k))
                        split_first(i, k)
                normalise(B - 1, 1)
                for k in range(2):
                    split_first(B - 1, k)

            @block.tensor
            def _(pe):
                pe.wait_ge(w_loaded, 64)
                for j in range(3):
                    turned = nc.tensor.transpose(psw[:, j * P:(j + 1) * P], wrow[:, j, :], c["ident"][:])
                pe.wait_ge(w_ready, 3)
                for j in range(3):
                    turned = nc.tensor.matmul(psw[:, 3 * P + j:3 * P + j + 1],
                                              bperm[:, j, :],
                                              c["ident"][0:1, 0:1], start=True, stop=True)
                turned.then_inc(w_turned, 1)
                pe.wait_ge(w_ready, 7)
                with pe.Fori(0, B) as i:
                    for k in range(2):
                        pe.wait_ge(xn_ready[k], i * UPT + UPT)
                        pe.wait_ge(xT_ready[k], i)
                        for j in range(UPT):
                            turned = nc.tensor.transpose(psx[k][:, j * P:(j + 1) * P], xn[k][:, j, :], c["ident"][:])
                        turned.then_inc(xT_made[k], 1)
                        pe.wait_ge(xT_ready[k], i + 1)
                        pe.wait_ge(q_ready[1 - k], i + k)
                        pe.wait_ge(k_ready[1 - k], i + k)
                        pe.wait_ge(ka_ready[1 - k], i + k)
                        for j in range(3):
                            nc.tensor.matmul(psq[j][:], wT[:, j, :], xnT[k][:], start=True, stop=True).then_inc(mm_done[k], 1)

            @block.scalar
            def _(act):
                act.wait_ge(bias_ready, 3)
                with act.Fori(0, B) as i:
                    for k in range(2):
                        act.wait_ge(xT_made[k], i + 1)
                        act.wait_ge(mm_done[k], i * 3)
                        nc.scalar.activation(xnT[k][:], psx[k][:], ACT.Copy).then_inc(xT_ready[k], 1)
                        act.wait_ge(rest1[k], i)
                        act.wait_ge(f_stored[k], i * 16)
                        act.wait_ge(mm_done[k], i * 3 + 1)
                        nc.scalar.activation(f[k][:, 0, :], psq[0][:], ACT.Identity, bias=sbias[:, 0:1], scale=SCALE).then_inc(q_ready[k], 1)
                        act.wait_ge(mm_done[k], i * 3 + 2)
                        nc.scalar.activation(f[k][:, 1, :], psq[1][:], ACT.Identity, bias=sbias[:, 1:2], scale=1.0).then_inc(k_ready[k], 1)
                        act.wait_ge(mm_done[k], i * 3 + 3)
                        nc.scalar.activation(f[k][:, 3, :], psq[2][:], ACT.Sigmoid, bias=sbias[:, 2:3], scale=SCALE * 0.02).then_inc(ka_ready[k], 1)
                        act.wait_ge(rest1[k], i + 1)
                        nc.scalar.activation(parts[k][:, :, 1, :], r[k][:], ACT.Copy).then_inc(part2[k], 1)
                        act.wait_ge(qa_ready[k], i + 1)
                        act.wait_ge(ka_ready[k], i + 1)
                        act.dma_start(dram["fT"][:, :, ds(i * T + k * UNIT, UNIT)].rearrange("q p t -> p q t"),
                                      f[k][:, 2:4, :]).then_inc(f_stored[k], 16)
                for k in range(2):
                    act.wait_ge(f_stored[k], B * 16)

            @block.gpsimd
            def _(pool):
                for k in range(2):
                    nc.gpsimd.memset(vp[k][:], 1.0).then_inc(ones_ready, 1)
                nc.gpsimd.memset(power[:], -0.5).then_inc(ones_ready, 1)
                pool.wait_ge(ones_ready, 3)

                def widen(i, k):
                    pool.wait_ge(mean[k], i * UPT + UPT)
                    if not isinstance(i, int) or i + k:
                        pool.wait_ge(xn_ready[1 - k], (i + k) * UPT)
                    pool.sem_inc(passed, 1)
                    nc.gpsimd.tensor_scalar(veps[:], mv[:, :, 1], EPS, 1.0, ALU.add, ALU.mult).then_inc(veps_ready[k], 1)
                    pool.wait_ge(veps_ready[k], i + 1)
                    nc.gpsimd.tensor_tensor(rstd[:], veps[:], power[:], ALU.pow).then_inc(rstd_ready[k], 1)
                    pool.wait_ge(xn_ready[k], i * UPT + UPT)
                    pool.wait_ge(vp_stored[k], i * 16)
                    pool.sem_inc(passed, 1)
                    nc.gpsimd.tensor_copy(vp[k][:, :, :, 0:HD], xn[k][:].rearrange("p j (h d) -> p j h d", d=HD)).then_inc(vp_ready[k], 1)

                def split_last(i, k):
                    pool.wait_ge(part2[k], i + 1)
                    nc.gpsimd.tensor_tensor(parts[k][:, :, 2, :], r[k][:], parts[k][:, :, 1, :], ALU.subtract).then_inc(part3[k], 1)

                widen(0, 0)
                with pool.Fori(0, B - 1) as i:
                    for k in range(2):
                        widen(*ahead(i, k))
                        split_last(i, k)
                widen(B - 1, 1)
                for k in range(2):
                    split_last(B - 1, k)
        m.clear()


QW = 512
UNITS = [(0, j) for j in range(4)] + [(1, j) for j in range(8)]
TILES = [(h, i) for h in range(GH) for i in range(BLK)]
TPG = len(TILES) + 1
UPG = len(UNITS)
ROW_PACE = 38
TURN_AT = 10
STRIDES = sorted({1, 2, 16, 32, UPG, TPG, UPG * GH, COMBOS * 16, PARTS * 16})


def attention(nc, dram, c):
    with ExitStack() as ctx:
        m = Mem(nc, ctx, "attn")
        qs = [m.sb(f"qs{k}", [P, GH, T], BF16) for k in range(2)]
        ks = [m.sb(f"ks{k}", [P, GH, T], BF16) for k in range(2)]
        vc = [m.sb(f"vc{k}", [P, BLK, GH * (HD + 1)]) for k in range(2)]
        vw = [m.sb(f"vw{k}", [P, BLK, GH, 32]) for k in range(2)]
        nm = m.sb("nm", [P, GH * BLK])
        nrest = m.sb("nrest", [P, GH * BLK])
        nparts = m.sb("nparts", [P, PARTS, GH * BLK], BF16)
        nrows = m.sb("nrows", [PARTS * GH * BLK, P], BF16)
        prob = [m.sb(f"prob{s}", [P, GH, QW]) for s in range(2)]
        o = [m.sb(f"o{ch}", [P, QW]) for ch in range(2)]
        rec = [m.sb(f"rec{ch}", [P, UPT * GH]) for ch in range(2)]
        y = [m.sb(f"y{ch}", [P, UPT, GH, HD]) for ch in range(2)]
        ps_rows = [m.ps(f"ps_rows{s}", [P, T]) for s in range(2)]
        ps_cols = [m.ps(f"ps_cols{s}", [P, QW]) for s in range(2)]
        ps_o = [m.ps(f"ps_o{ch}", [P, QW]) for ch in range(2)]
        filled, passed = m.sem("filled"), m.sem("passed")
        q_loaded, k_loaded, v_loaded, v_wide = (m.pair(n) for n in ("q_ld", "k_ld", "v_ld", "v_wide"))
        rows_done, rows_free = m.pair("rows_done"), m.pair("rows_free")
        split_a, split_b, split_c, split_d = (m.pair(n) for n in ("split_a", "split_b", "split_c", "split_d"))
        max_stored = m.pair("max_st")
        cols_done, prob_done, pv_done = m.pair("cols_done"), m.pair("prob_done"), m.pair("pv_done")
        o_ready, turned, rec_ready, y_ready, y_stored = (m.pair(n) for n in ("o_ready", "turned", "rec", "y_ready", "y_st"))

        vp = dram["vp"].rearrange("(b j p) (g n) -> b g p j n", b=B, p=P, n=GH * (HD + 1))
        split = [dram["parts"][q * PARTS:(q + 1) * PARTS].rearrange("s b (g d h) t -> (b g) s d (h t)", g=GPB, h=GH) for q in range(2)]
        yar = dram["yar"].rearrange("g (c j p) n -> g c p j n", c=2, p=P)

        def load(sp, i, k):
            sp.wait_ge(cols_done[k], i * UPG * GH)
            for s in range(PARTS):
                at = s * PARTS * HD
                for n in range(PARTS):
                    sp.dma_start(qs[k][at + n * HD:at + (n + 1) * HD], split[0][i * 2 + k, s]).then_inc(q_loaded[k], 16)
                sp.dma_start(ks[k][at:at + PARTS * HD], split[1][i * 2 + k]).then_inc(k_loaded[k], 16)
            sp.wait_ge(v_wide[k], i)
            sp.dma_start(vc[k][:], vp[i // 2, (i % 2) * 2 + k]).then_inc(v_loaded[k], 16)

        def store_max(sp, i, k):
            sp.wait_ge(rows_free[k], (i + 1) * TPG)
            sp.dma_start(qs[k][MROW:MROW + PARTS].rearrange("s h (j t) -> s (h j) t", t=P), nrows[:]).then_inc(max_stored[k], 16)

        def store_y(sp, i, k, ch):
            sp.wait_ge(y_ready[ch], i * 2 + k + 1)
            sp.dma_start(yar[i * 2 + k, ch], y[ch][:].rearrange("p j h d -> p j (h d)")).then_inc(y_stored[ch], 16)

        def row_tile(i, k, n):
            pe = nc.tensor
            if n == 0:
                pe.wait_ge(q_loaded[k], now((i + 1) * COMBOS * 16))
                pe.wait_ge(k_loaded[k], now((i + 1) * PARTS * 16))
                pe.wait_ge(rows_free[1 - k], now((i + k) * TPG))
            if n >= 2:
                pe.wait_ge(rows_free[k], now(i * TPG + n - 1))
            h, blk = TILES[n]
            out = ps_rows[n % 2]
            for at in range(0, (blk + 1) * P, QW):
                to = min(at + QW, (blk + 1) * P)
                last = to == (blk + 1) * P
                done = nc.tensor.matmul(out[:, at:to], qs[k][0:KROWS, h, blk * P:(blk + 1) * P], ks[k][0:KROWS, h, at:to],
                                        start=True, stop=not last)
            done = nc.tensor.matmul(out[:, blk * P:(blk + 1) * P], c["identb"][:], c["mask_rows"][:], start=False, stop=True)
            done.then_inc(rows_done[k], 1)

        def turn_max(i, k):
            nc.tensor.wait_ge(split_d[k], now(i + 1))
            nc.tensor.wait_ge(rows_free[k], now(i * TPG + TPG - 1))
            nc.tensor.transpose(turned_max, nparts[:].rearrange("p s n -> p (s n)"), c["identb"][:]).then_inc(rows_done[k], 1)

        def rows_of(ch, j):
            at = max(j * P, ch * QW)
            return at, (ch + 1) * QW - at

        def col_tile(i, k, u, h):
            ch, j = UNITS[u]
            at, w = rows_of(ch, j)
            q = u * GH + h
            if q == 0:
                nc.tensor.wait_ge(max_stored[k], now((i + 1) * 16))
                nc.tensor.wait_ge(prob_done[1 - k], now((i + k) * UPG * GH))
            if q >= 2:
                nc.tensor.wait_ge(prob_done[k], now(i * UPG * GH + q - 1))
            diagonal = at == j * P
            out = ps_cols[q % 2]
            done = nc.tensor.matmul(out[:, 0:w], ks[k][0:MROW + PARTS, h, j * P:(j + 1) * P],
                                    qs[k][0:MROW + PARTS, h, at:at + w], start=True, stop=not diagonal)
            if diagonal:
                done = nc.tensor.matmul(out[:, 0:P], c["identb"][:], c["mask_cols"][:], start=False, stop=True)
            done.then_inc(cols_done[k], 1)

        def weighted(i, k, u):
            ch, j = UNITS[u]
            at, w = rows_of(ch, j)
            if u == 0:
                nc.tensor.wait_ge(v_wide[k], now(i + 1))
            if j == 0:
                nc.tensor.wait_ge(y_ready[ch], now(i * 2 + k))
            nc.tensor.wait_ge(prob_done[k], now(i * UPG * GH + (u + 1) * GH))
            last = (ch, j + 1) not in UNITS
            for h in range(GH):
                done = nc.tensor.matmul(ps_o[ch][32 * h:32 * h + 32, at - ch * QW:at - ch * QW + w], vw[k][:, j, h, :],
                                        prob[u % 2][:, h, 0:w], start=j == 0, stop=last)
            done.then_inc(pv_done[k], 1)

        def turn(i, k, ch):
            nc.tensor.wait_ge(o_ready[ch], now(i * 2 + k + 1))
            for b in range(UPT):
                done = nc.tensor.transpose(ps_o[ch][:, b * P:(b + 1) * P], o[ch][:, b * P:(b + 1) * P], c["ident"][:])
            done.then_inc(turned[ch], 1)

        def max_tile(i, k, n):
            if n == 0:
                nc.vector.wait_ge(split_d[1 - k], now(i + k))
            nc.vector.wait_ge(rows_done[k], now(i * TPG + n + 1))
            h, blk = TILES[n]
            nc.vector.tensor_reduce(nm[:, n:n + 1], ps_rows[n % 2][:, 0:(blk + 1) * P], AX.X, ALU.max,
                                    negate=True).then_inc(rows_free[k], 1)

        def split_max(dve, i, k):
            dve.wait_ge(rows_free[k], now(i * TPG + TPG - 1))
            nc.vector.tensor_copy(nparts[:, 0, :], nm[:]).then_inc(split_a[k], 1)
            dve.wait_ge(split_a[k], now(i + 1))
            nc.vector.tensor_tensor(nrest[:], nm[:], nparts[:, 0, :], ALU.subtract).then_inc(split_b[k], 1)
            dve.wait_ge(split_b[k], now(i + 1))
            nc.vector.tensor_copy(nparts[:, 1, :], nrest[:]).then_inc(split_c[k], 1)
            dve.wait_ge(split_c[k], now(i + 1))
            nc.vector.tensor_tensor(nparts[:, 2, :], nrest[:], nparts[:, 1, :], ALU.subtract).then_inc(split_d[k], 1)

        def keep_max(dve, i, k):
            dve.wait_ge(rows_done[k], now((i + 1) * TPG))
            dve.wait_ge(max_stored[1 - k], now((i + k) * 16))
            nc.vector.tensor_copy(nrows[:], turned_max).then_inc(rows_free[k], 1)

        def divide(dve, i, k, ch):
            by_row = ps_o[ch][:].rearrange("p (n d) -> p n d", d=32)
            dve.wait_ge(turned[ch], now(i * 2 + k + 1))
            nc.vector.reciprocal(rec[ch][:], by_row[:, :, HD]).then_inc(rec_ready[ch], 1)
            dve.wait_ge(rec_ready[ch], now(i * 2 + k + 1))
            dve.wait_ge(y_stored[ch], now((i * 2 + k) * 16))
            nc.vector.tensor_tensor(y[ch][:].rearrange("p j h d -> p (j h) d"), by_row[:, :, 0:HD],
                                    rec[ch][:].unsqueeze(2).broadcast_to([P, UPT * GH, HD]), ALU.mult).then_inc(y_ready[ch], 1)

        def pe_group(i, k, more):
            ni, nk = (i, 1) if k == 0 else (i + 1, 0)
            n = 0
            for u in range(UPG):
                for h in range(GH):
                    col_tile(i, k, u, h)
                    q = u * GH + h
                    while more and n < len(TILES) and n * ROW_PACE <= q * len(TILES):
                        row_tile(ni, nk, n)
                        n += 1
                if u > 0:
                    weighted(i, k, u - 1)
                if u == 6:
                    turn(i, k, 0)
                if more and u == TURN_AT:
                    turn_max(ni, nk)
            weighted(i, k, UPG - 1)
            turn(i, k, 1)

        def dve_group(dve, i, k, more):
            ni, nk = (i, 1) if k == 0 else (i + 1, 0)
            n = 0
            for u in range(UPG):
                for h in range(GH):
                    q = u * GH + h
                    while more and n < len(TILES) and n * ROW_PACE <= q * len(TILES):
                        max_tile(ni, nk, n)
                        n += 1
                        if n == len(TILES):
                            split_max(dve, ni, nk)
                if u == 6:
                    divide(dve, i, k, 0)
                if more and u == TURN_AT:
                    keep_max(dve, ni, nk)
            divide(dve, i, k, 1)

        def act_group(act, i, k):
            for u in range(UPG):
                ch, j = UNITS[u]
                w = rows_of(ch, j)[1]
                if u < 2:
                    act.wait_ge(pv_done[1 - k], now((i + k) * UPG))
                else:
                    act.wait_ge(pv_done[k], now(i * UPG + u - 1))
                for h in range(GH):
                    act.wait_ge(cols_done[k], now(i * UPG * GH + u * GH + h + 1))
                    nc.scalar.activation(prob[u % 2][:, h, 0:w], ps_cols[(u * GH + h) % 2][:, 0:w], ACT.Exp).then_inc(prob_done[k], 1)
                if u == 5:
                    keep_o(act, i, k, 0)
            keep_o(act, i, k, 1)

        def keep_o(act, i, k, ch):
            act.wait_ge(pv_done[k], now(i * UPG + (4 if ch == 0 else UPG)))
            act.wait_ge(turned[ch], now(i * 2 + k))
            nc.scalar.activation(o[ch][:], ps_o[ch][:], ACT.Copy).then_inc(o_ready[ch], 1)

        def sp_group(sp, i, k, more, load_more):
            ni, nk = (i, 1) if k == 0 else (i + 1, 0)
            store_y(sp, i, k, 0)
            if more:
                store_max(sp, ni, nk)
            if load_more:
                load(sp, i + 1, k)
            store_y(sp, i, k, 1)

        turned_max = ps_rows[0][:].bitcast(BF16)[0:PARTS * GH * BLK, 0:P]
        last = GROUPS // 2 - 1
        with nc.Block() as block:
            @block.sync
            def _(sp):
                sp.wait_ge(filled, 8)
                load(sp, 0, 0)
                load(sp, 0, 1)
                store_max(sp, 0, 0)
                with sp.Fori(0, last) as i:
                    for k in range(2):
                        sp_group(sp, i, k, True, True)
                for k in range(2):
                    sp_group(sp, last, k, k == 0, False)
                for ch in range(2):
                    sp.wait_ge(y_stored[ch], GROUPS * 16)

            @block.tensor
            def _(pe):
                pe.wait_ge(filled, 8)
                for n in range(len(TILES)):
                    row_tile(0, 0, n)
                turn_max(0, 0)
                turns = Turns(pe, "attn_pe", STRIDES)
                with pe.Fori(0, last) as turn:
                    i = Linear(turns, turn)
                    for k in range(2):
                        pe_group(i, k, True)
                    turns.step()
                for k in range(2):
                    pe_group(last, k, k == 0)

            @block.vector
            def _(dve):
                for k in range(2):
                    nc.vector.memset(qs[k][P // 2:P], 0.0).then_inc(filled, 1)
                    nc.vector.memset(ks[k][P // 2:P], 0.0).then_inc(filled, 1)
                    nc.vector.memset(vw[k][:], 0.0).then_inc(filled, 1)
                dve.wait_ge(filled, 6)
                for k in range(2):
                    nc.vector.memset(ks[k][MROW:P], 1.0).then_inc(filled, 1)
                for n in range(len(TILES)):
                    max_tile(0, 0, n)
                split_max(dve, 0, 0)
                keep_max(dve, 0, 0)
                turns = Turns(dve, "attn_dve", STRIDES)
                with dve.Fori(0, last) as turn:
                    i = Linear(turns, turn)
                    for k in range(2):
                        dve_group(dve, i, k, True)
                    turns.step()
                for k in range(2):
                    dve_group(dve, last, k, k == 0)

            @block.scalar
            def _(act):
                turns = Turns(act, "attn_act", STRIDES)
                with act.Fori(0, last + 1) as turn:
                    i = Linear(turns, turn)
                    for k in range(2):
                        act_group(act, i, k)
                    turns.step()

            @block.gpsimd
            def _(pool):
                pool.wait_ge(filled, 8)
                with pool.Fori(0, last + 1) as i:
                    for k in range(2):
                        pool.wait_ge(v_loaded[k], i * 16 + 16)
                        pool.wait_ge(pv_done[k], i * UPG)
                        pool.sem_inc(passed, 1)
                        nc.gpsimd.tensor_copy(vw[k][:, :, :, 0:HD + 1].rearrange("p j h n -> p (j h) n"),
                                              vc[k][:].rearrange("p j (h n) -> p (j h) n", h=GH)).then_inc(v_wide[k], 1)
        m.clear()


HALF = BLK // 2
MEM_STRIDES = sorted({1, 2, 7, 8, 16, 32, 64, 2 * COMBOS * 16, 2 * PARTS * 16})


def memory(nc, dram, c, a):
    with ExitStack() as ctx:
        m = Mem(nc, ctx, "mem")
        wrow, wT, wpad = m.sb("wrow", [P, P]), m.sb("wT", [P, P]), m.sb("wpad", [P, GPB, P])
        brow, bias2 = m.sb("brow", [P, P]), m.sb("bias2", [P, P])
        qs = [m.sb(f"qs{k}", [KROWS, GH, T], BF16) for k in range(2)]
        ks = [m.sb(f"ks{k}", [KROWS, GH, T], BF16) for k in range(2)]
        yt, vs, e = m.sb("yt", [P, BLK, D]), m.sb("vs", [P, BLK, D]), m.sb("e", [P, BLK, D])
        kaT, qaT, ka = m.sb("kaT", [P, T]), m.sb("qaT", [P, T]), m.sb("ka", [P, BLK, P])
        yT = m.sb("yT", [P, T])
        x, xb, x1 = m.sb("x", [P, BLK, D]), m.sb("xb", [P, BLK, D]), m.sb("x1", [P, BLK, D])
        state = m.sb("state", [P, BLK, HEADS, 32])
        am = [m.sb(f"am{s}", [P, GH, P]) for s in range(2)]
        ymT = m.sb("ymT", [P, GPB, T])
        ps_t, ps_state, ps_p = m.ps("ps_t", [P, T]), m.ps("ps_state", [P, P]), m.ps("ps_p", [P, HALF, P])
        ps_a = [m.ps(f"ps_a{s}", [P, GH, P]) for s in range(2)]
        ps_y = [m.ps(f"ps_y{s}", [P, HALF, P]) for s in range(2)]
        w_loaded, w_turned, w_ready, w_spread, filled = (m.sem(n) for n in ("w_ld", "w_turned", "w_ready", "w_spread", "filled"))
        bias_ready = m.sem("bias_ready")
        y_loaded, v_loaded, ka_loaded, qa_loaded, x_loaded = (m.sem(n) for n in ("y_ld", "v_ld", "ka_ld", "qa_ld", "x_ld"))
        qs_loaded, ks_loaded = m.pair("qs_ld"), m.pair("ks_ld")
        e_ready, ka_turned, ka_ready, y_turned, yT_ready = (m.sem(n) for n in ("e_ready", "ka_turned", "ka_ready", "y_turned", "yT_ready"))
        state_done, state_ready = m.sem("state_done"), m.sem("state_ready")
        a_done, a_ready, y_done, ym_ready = (m.sem(n) for n in ("a_done", "a_ready", "y_done", "ym_ready"))
        p_done, xb_ready, x1_ready, x1_stored, passed = (m.sem(n) for n in ("p_done", "xb_ready", "x1_ready", "x1_st", "passed"))
        split = [dram["parts"][q * PARTS:(q + 1) * PARTS].rearrange("s b (g d h) t -> (b g) s d (h t)", g=GPB, h=GH) for q in (2, 3)]
        yar = dram["yar"].rearrange("(b g) (j p) n -> b g p j n", b=B, p=P)

        def load_stack(sp, i, hg):
            k = hg % 2
            sp.wait_ge(a_done, i * 32 + (hg - 1) * 8 if hg >= 2 else i * 32)
            for s in range(PARTS):
                at = s * PARTS * HD
                for n in range(PARTS):
                    sp.dma_start(qs[k][at + n * HD:at + (n + 1) * HD], split[0][i * GPB + hg, s]).then_inc(qs_loaded[k], 16)
                sp.dma_start(ks[k][at:at + PARTS * HD], split[1][i * GPB + hg]).then_inc(ks_loaded[k], 16)

        def products(i, hg, b):
            t, k = hg * BLK + b, hg % 2
            if b == 0:
                nc.tensor.wait_ge(qs_loaded[k], now(i * (2 * COMBOS * 16) + (hg // 2 + 1) * COMBOS * 16))
                nc.tensor.wait_ge(ks_loaded[k], now(i * (2 * PARTS * 16) + (hg // 2 + 1) * PARTS * 16))
            nc.tensor.wait_ge(a_ready, now(i * 32 + t - 1) if t else now(i * 32))
            for h in range(GH):
                done = nc.tensor.matmul(ps_a[t % 2][:, h, :], ks[k][:, h, b * P:(b + 1) * P], qs[k][:, h, b * P:(b + 1) * P],
                                        start=True, stop=True)
            done.then_inc(a_done, 1)

        def outputs(i, hg, b):
            t, half = hg * BLK + b, b // HALF
            out = ps_y[half][:, b % HALF, :]
            if b % HALF == 0:
                if hg:
                    nc.tensor.wait_ge(ym_ready, now(i * 8 + hg * 2 - 1 + half))
                else:
                    nc.tensor.wait_ge(ym_ready, now(i * 8))
            if hg == 0 and b:
                nc.tensor.wait_ge(state_ready, now(i * 7 + b))
            nc.tensor.matmul(out, state[:, b, hg * GH:(hg + 1) * GH, :].rearrange("p h n -> p (h n)"), qaT[:, b * P:(b + 1) * P],
                             start=True, stop=False)
            nc.tensor.wait_ge(a_ready, now(i * 32 + t + 1))
            for h in range(GH):
                at = (hg * GH + h) * HD
                done = nc.tensor.matmul(out[32 * h:32 * h + HD], e[:, b, at:at + HD], am[t % 2][:, h, :], start=False, stop=True)
            done.then_inc(y_done, 1)

        def add_state(i, b):
            if b == 0:
                nc.tensor.wait_ge(e_ready, now(i * 1 + 1))
                nc.tensor.wait_ge(ka_ready, now(i * 1 + 1))
            nc.tensor.wait_ge(state_ready, now(i * 7 + b))
            nc.tensor.matmul(ps_state[:], ka[:, b, :], e[:, b, :], start=b == 0, stop=True,
                             skip_group_check=b > 0).then_inc(state_done, 1)

        with nc.Block() as block:
            @block.sync
            def _(sp):
                sp.dma_start(wrow[:], a["w_proj"]).then_inc(w_loaded, 16)
                sp.dma_start(brow[:], a["b_proj"].rearrange("(o n) -> o n", o=1).broadcast_to([P, P])).then_inc(w_loaded, 16)
                sp.wait_ge(w_ready, 1)
                sp.wait_ge(filled, 2)
                for h in range(HEADS):
                    at = 32 * (h % GH)
                    sp.dma_start(wpad[at:at + HD, h // GH, :], wT[h * HD:(h + 1) * HD, :]).then_inc(w_spread, 16)
                with sp.Fori(0, B) as i:
                    sp.wait_ge(ka_turned, i)
                    sp.dma_start(kaT[:], dram["fT"][1, :, ds(i * T, T)]).then_inc(ka_loaded, 16)
                    sp.wait_ge(e_ready, i)
                    sp.sem_inc(passed, 1)
                    sp.dma_start(vs[:], dram["xn"][ds(i * T + 1, T), :].rearrange("(j p) d -> p j d", p=P)).then_inc(v_loaded, 16)
                    sp.wait_ge(y_turned, i)
                    for g in range(GPB):
                        sp.dma_start(yt[:, :, g * GH * HD:(g + 1) * GH * HD], yar[i, g]).then_inc(y_loaded, 16)
                    sp.wait_ge(y_done, i * 32)
                    sp.sem_inc(passed, 1)
                    sp.dma_start(qaT[:], dram["fT"][0, :, ds(i * T, T)]).then_inc(qa_loaded, 16)
                    load_stack(sp, i, 0)
                    load_stack(sp, i, 1)
                    sp.wait_ge(xb_ready, i)
                    sp.dma_start(x[:], a["x"][ds(i * T, T), :].rearrange("(j p) d -> p j d", p=P)).then_inc(x_loaded, 16)
                    load_stack(sp, i, 2)
                    load_stack(sp, i, 3)

            @block.tensor
            def _(pe):
                pe.wait_ge(w_loaded, 32)
                nc.tensor.transpose(ps_t[:, 0:P], wrow[:], c["ident"][:]).then_inc(w_turned, 1)
                pe.wait_ge(w_ready, 1)
                pe.wait_ge(w_spread, HEADS * 16)
                pe.wait_ge(filled, 2)
                turns = Turns(pe, "mem_pe", MEM_STRIDES)
                with pe.Fori(0, B) as turn:
                    i = Linear(turns, turn)
                    pe.wait_ge(ka_loaded, now(i * 16 + 16))
                    pe.wait_ge(yT_ready, now(i * 1))
                    for b in range(BLK):
                        done = nc.tensor.transpose(ps_t[:, b * P:(b + 1) * P], kaT[:, b * P:(b + 1) * P], c["ident"][:])
                    done.then_inc(ka_turned, 1)
                    pe.wait_ge(qa_loaded, now(i * 16 + 16))
                    for t in range(GPB * BLK):
                        products(i, t // BLK, t % BLK)
                        if t < BLK - 1:
                            add_state(i, t)
                        if t == 0:
                            pe.wait_ge(y_loaded, now(i * 64 + 64))
                            for b in range(BLK):
                                done = nc.tensor.transpose(ps_t[:, b * P:(b + 1) * P], yt[:, b, :], c["ident"][:])
                            done.then_inc(y_turned, 1)
                        if t:
                            outputs(i, (t - 1) // BLK, (t - 1) % BLK)
                    outputs(i, GPB - 1, BLK - 1)
                    pe.wait_ge(yT_ready, now(i * 1 + 1))
                    for half in range(2):
                        pe.wait_ge(ym_ready, now(i * 8 + 7 + half))
                        pe.wait_ge(x1_ready, now(i * 2 + half))
                        for b in range(half * HALF, (half + 1) * HALF):
                            out = ps_p[:, b % HALF, :]
                            nc.tensor.matmul(out, yT[:, b * P:(b + 1) * P], wT[:], start=True, stop=False)
                            for hg in range(GPB):
                                done = nc.tensor.matmul(out, ymT[:, hg, b * P:(b + 1) * P], wpad[:, hg, :], start=False, stop=hg == GPB - 1)
                        done.then_inc(p_done, 1)
                    turns.step()

            @block.vector
            def _(dve):
                nc.vector.memset(wpad[:], 0.0).then_inc(filled, 1)
                nc.vector.memset(state[:], 0.0).then_inc(filled, 1)
                dve.wait_ge(w_turned, 1)
                nc.vector.tensor_copy(wT[:], ps_t[:, 0:P]).then_inc(w_ready, 1)
                dve.wait_ge(w_loaded, 32)
                nc.vector.tensor_scalar(bias2[:], brow[:], 2.0, None, ALU.mult).then_inc(bias_ready, 1)
                dve.wait_ge(filled, 2)
                turns = Turns(dve, "mem_dve", MEM_STRIDES)
                with dve.Fori(0, B) as turn:
                    i = Linear(turns, turn)
                    dve.wait_ge(v_loaded, now(i * 16 + 16))
                    dve.wait_ge(y_loaded, now(i * 64 + 64))
                    dve.wait_ge(y_done, now(i * 32))
                    nc.vector.tensor_tensor(e[:], vs[:], yt[:], ALU.subtract).then_inc(e_ready, 1)
                    for t in range(GPB * BLK):
                        dve.wait_ge(a_done, now(i * 32 + t + 1))
                        if t >= 2:
                            dve.wait_ge(y_done, now(i * 32 + t - 1))
                        nc.vector.tensor_tensor(am[t % 2][:], ps_a[t % 2][:], c["strict"][:], ALU.mult).then_inc(a_ready, 1)
                        if t < BLK - 1:
                            dve.wait_ge(state_done, now(i * 7 + t + 1))
                            nc.vector.tensor_tensor(state[:, t + 1, :, 0:HD], ps_state[:].rearrange("p (h d) -> p h d", d=HD),
                                                    c["same_head"][:].rearrange("p (h d) -> p h d", d=HD), ALU.mult).then_inc(state_ready, 1)
                    for half in range(2):
                        dve.wait_ge(p_done, now(i * 2 + half + 1))
                        dve.wait_ge(xb_ready, now(i * 1 + 1))
                        dve.wait_ge(x1_stored, now(i * 32 + half * 16))
                        nc.vector.tensor_tensor(x1[:, half * HALF:(half + 1) * HALF, :], ps_p[:], xb[:, half * HALF:(half + 1) * HALF, :],
                                                ALU.add).then_inc(x1_ready, 1)
                    turns.step()

            @block.scalar
            def _(act):
                turns = Turns(act, "mem_act", MEM_STRIDES)
                with act.Fori(0, B) as turn:
                    i = Linear(turns, turn)
                    act.wait_ge(ka_turned, now(i * 1 + 1))
                    act.wait_ge(state_done, now(i * 7))
                    nc.scalar.activation(ka[:].rearrange("p j n -> p (j n)"), ps_t[:], ACT.Copy).then_inc(ka_ready, 1)
                    act.wait_ge(y_turned, now(i * 1 + 1))
                    act.wait_ge(p_done, now(i * 2))
                    nc.scalar.activation(yT[:], ps_t[:], ACT.Copy).then_inc(yT_ready, 1)
                    for hg in range(GPB):
                        for half in range(2):
                            act.wait_ge(y_done, now(i * 32 + hg * BLK + (half + 1) * HALF))
                            nc.scalar.activation(ymT[:, hg, half * HALF * P:(half + 1) * HALF * P],
                                                 ps_y[half][:].rearrange("p j n -> p (j n)"), ACT.Copy).then_inc(ym_ready, 1)
                    for half in range(2):
                        act.wait_ge(x1_ready, now(i * 2 + half + 1))
                        act.dma_start(dram["x1"][ds(turn * T + half * HALF * P, HALF * P), :].rearrange("(j p) d -> p j d", p=P),
                                      x1[:, half * HALF:(half + 1) * HALF, :]).then_inc(x1_stored, 16)
                    turns.step()
                act.wait_ge(x1_stored, B * 32)

            @block.gpsimd
            def _(pool):
                pool.wait_ge(bias_ready, 1)
                with pool.Fori(0, B) as i:
                    pool.wait_ge(x_loaded, i * 16 + 16)
                    pool.wait_ge(x1_ready, i * 2)
                    nc.gpsimd.tensor_tensor(xb[:], x[:], bias2[:].unsqueeze(1).broadcast_to([P, BLK, P]), ALU.add).then_inc(xb_ready, 1)
        m.clear()


EXPERTS, HIDDEN = 8, 256
HC = HIDDEN // P
ALL = EXPERTS + 1
STEPS = UPT * ALL
FFN_STRIDES = sorted({1, 2, 4, 16, STEPS, 2 * UPT})


def ffn(nc, dram, c, a, stage, src, dst):
    with ExitStack() as ctx:
        m = Mem(nc, ctx, stage)
        w12 = m.sb("w12", [P, ALL, 2, HIDDEN])
        w3 = m.sb("w3", [P, ALL, HC, D])
        rw, rb = m.sb("rw", [P, EXPERTS]), m.sb("rb", [P, EXPERTS])
        x = [m.sb(f"x{k}", [P, UPT, D]) for k in range(2)]
        stats, mv = m.sb("stats", [P, UPT, 6]), m.sb("mv", [P, UPT, 2])
        veps, power, rstd = m.sb("veps", [P, UPT]), m.sb("power", [P, UPT]), m.sb("rstd", [P, UPT])
        xn = m.sb("xn", [P, UPT, D])
        xnT = [m.sb(f"xnT{k}", [P, UNIT]) for k in range(2)]
        logits, top = m.sb("logits", [P, UPT, EXPERTS]), m.sb("top", [P, UPT, EXPERTS])
        index, order = m.sb("index", [P, UPT, EXPERTS], mybir.dt.uint32), m.sb("order", [P, UPT, EXPERTS])
        number = m.sb("number", [P, UPT, EXPERTS])
        gap, gate = m.sb("gap", [P, 2, UPT]), m.sb("gate", [P, 2, UPT])
        first, second = m.sb("first", [P, UPT, EXPERTS]), m.sb("second", [P, UPT, EXPERTS])
        gates = [m.sb(f"gates{k}", [P, UPT, EXPERTS]) for k in range(2)]
        act1 = [m.sb(f"act{s}", [P, HIDDEN]) for s in range(2)]
        hid = [m.sb(f"hid{s}", [P, HIDDEN]) for s in range(2)]
        hidT = [m.sb(f"hidT{s}", [P, HIDDEN]) for s in range(2)]
        out = [m.sb(f"out{k}", [P, UPT, D]) for k in range(2)]
        ps_x, ps_r = m.ps("ps_x", [P, UNIT]), m.ps("ps_r", [P, UPT, EXPERTS])
        ps_h = [m.ps(f"ps_h{s}", [P, 2, HIDDEN]) for s in range(2)]
        ps_t = [m.ps(f"ps_t{s}", [P, HIDDEN]) for s in range(2)]
        ps_o = [m.ps(f"ps_o{s}", [P, UPT, D]) for s in range(2)]
        w_loaded, ready, passed = m.sem("w_ld"), m.sem("ready"), m.sem("passed")
        x_loaded, stat, mean, veps_ready, rstd_ready, xn_ready = (m.pair(n) for n in ("x_ld", "stat", "mean", "veps", "rstd", "xn"))
        xT_made, xT_ready, r_done, logits_ready, top_ready, index_ready = (m.pair(n) for n in ("xT_made", "xT", "r_done", "logits", "top", "index"))
        order_ready, gap_ready, gate_ready, pick_ready, gates_ready = (m.pair(n) for n in ("order", "gap", "gate", "pick", "gates"))
        h_done, act_ready, hid_ready, t_done, hidT_ready, o_done = (m.pair(n) for n in ("h_done", "act", "hid", "t_done", "hidT", "o_done"))
        out_ready, out_stored = m.pair("out"), m.pair("out_st")

        def unit_of(t, i, k):
            return t[ds(i * T + k * UNIT, UNIT), :].rearrange("(j p) d -> p j d", p=P)

        def hidden(i, k, n):
            t, e = n // ALL, n % ALL
            if n < 2:
                nc.tensor.wait_ge(hid_ready[1 - k], now((i + k) * STEPS))
            else:
                nc.tensor.wait_ge(hid_ready[k], now(i * STEPS + n - 1))
            nc.tensor.matmul(ps_h[n % 2][:].rearrange("p w n -> p (w n)"), xnT[k][:, t * P:(t + 1) * P],
                             w12[:, e].rearrange("p w n -> p (w n)"), start=True, stop=True).then_inc(h_done[k], 1)

        def turn_hidden(i, k, n):
            nc.tensor.wait_ge(hid_ready[k], now(i * STEPS + n + 1))
            if n < 2:
                nc.tensor.wait_ge(hidT_ready[1 - k], now((i + k) * STEPS))
            else:
                nc.tensor.wait_ge(hidT_ready[k], now(i * STEPS + n - 1))
            for h in range(HC):
                done = nc.tensor.transpose(ps_t[n % 2][:, h * P:(h + 1) * P], hid[n % 2][:, h * P:(h + 1) * P], c["ident"][:])
            done.then_inc(t_done[k], 1)

        def back(i, k, n):
            t, e = n // ALL, n % ALL
            nc.tensor.wait_ge(hidT_ready[k], now(i * STEPS + n + 1))
            if n == 0:
                nc.tensor.wait_ge(out_ready[k], now(i * 1))
            for h in range(HC):
                done = nc.tensor.matmul(ps_o[k][:, t, :], hidT[n % 2][:, h * P:(h + 1) * P], w3[:, e, h, :],
                                        start=e == 0 and h == 0, stop=e == ALL - 1 and h == HC - 1)
            done.then_inc(o_done[k], 1)

        def prepare(i, k):
            nc.tensor.wait_ge(xn_ready[k], now(i * UPT + UPT))
            nc.tensor.wait_ge(xT_ready[1 - k], now(i + k))
            for j in range(UPT):
                done = nc.tensor.transpose(ps_x[:, j * P:(j + 1) * P], xn[:, j, :], c["ident"][:])
            done.then_inc(xT_made[k], 1)

        def route(i, k):
            nc.tensor.wait_ge(xT_ready[k], now(i + 1))
            nc.tensor.wait_ge(logits_ready[1 - k], now(i + k))
            for j in range(UPT):
                done = nc.tensor.matmul(ps_r[:, j, :], xnT[k][:, j * P:(j + 1) * P], rw[:], start=True, stop=True)
            done.then_inc(r_done[k], 1)

        def norm_dve(dve, i, k):
            dve.wait_ge(x_loaded[k], now(i * 16 + 16))
            for j in range(UPT):
                nc.vector.bn_stats(stats[:, j, :], x[k][:, j, :]).then_inc(stat[k], 1)
            dve.wait_ge(stat[k], now(i * UPT + UPT))
            dve.sem_inc(passed, 1)
            for j in range(UPT):
                nc.vector.bn_aggr(mv[:, j, :], stats[:, j, :]).then_inc(mean[k], 1)
            dve.wait_ge(rstd_ready[k], now(i + 1))
            dve.wait_ge(xT_made[1 - k], now(i + k))
            for j in range(UPT):
                nc.vector.tensor_scalar(xn[:, j, :], x[k][:, j, :], mv[:, j, 0:1], rstd[:, j:j + 1],
                                        ALU.subtract, ALU.mult).then_inc(xn_ready[k], 1)

        def gates_dve(dve, i, k):
            dve.wait_ge(r_done[k], now(i + 1))
            nc.vector.tensor_tensor(logits[:], ps_r[:], rb[:].unsqueeze(1).broadcast_to([P, UPT, EXPERTS]), ALU.add).then_inc(logits_ready[k], 1)
            dve.wait_ge(logits_ready[k], now(i + 1))
            dve.sem_inc(passed, 1)
            for j in range(UPT):
                nc.vector.max(top[:, j, :], logits[:, j, :]).then_inc(top_ready[k], 1)
            dve.wait_ge(top_ready[k], now(i * UPT + UPT))
            dve.sem_inc(passed, 1)
            for j in range(UPT):
                nc.vector.max_index(index[:, j, :], top[:, j, :], logits[:, j, :]).then_inc(index_ready[k], 1)
            dve.wait_ge(gate_ready[1 - k], now(i + k))
            nc.vector.tensor_tensor(gap[:, 0, :], top[:, :, 0], top[:, :, 1], ALU.subtract).then_inc(gap_ready[k], 1)
            nc.vector.tensor_tensor(gap[:, 1, :], top[:, :, 1], top[:, :, 0], ALU.subtract).then_inc(gap_ready[k], 1)
            dve.wait_ge(index_ready[k], now(i * UPT + UPT))
            nc.vector.tensor_copy(order[:], index[:]).then_inc(order_ready[k], 1)
            dve.wait_ge(order_ready[k], now(i + 1))
            dve.wait_ge(gate_ready[k], now(i + 1))
            for n, t in enumerate((first, second)):
                nc.vector.tensor_tensor(t[:], number[:], order[:, :, n:n + 1].broadcast_to([P, UPT, EXPERTS]), ALU.is_equal).then_inc(pick_ready[k], 1)
            dve.wait_ge(pick_ready[k], now(i * 4 + 2))
            for n, t in enumerate((first, second)):
                nc.vector.tensor_tensor(t[:], t[:], gate[:, n, :].unsqueeze(2).broadcast_to([P, UPT, EXPERTS]), ALU.mult).then_inc(pick_ready[k], 1)
            dve.wait_ge(pick_ready[k], now(i * 4 + 4))
            dve.wait_ge(hid_ready[k], now(i * STEPS))
            nc.vector.tensor_tensor(gates[k][:], first[:], second[:], ALU.add).then_inc(gates_ready[k], 1)

        def experts_dve(dve, i, k):
            dve.wait_ge(gates_ready[k], now(i + 1))
            for n in range(STEPS + 1):
                if n < STEPS:
                    t, e = n // ALL, n % ALL
                    dve.wait_ge(act_ready[k], now(i * STEPS + n + 1))
                    if n < 2:
                        dve.wait_ge(t_done[1 - k], now((i + k) * STEPS))
                    else:
                        dve.wait_ge(t_done[k], now(i * STEPS + n - 1))
                    g = gates[k][:, t, e:e + 1] if e < EXPERTS else 1.0
                    nc.vector.scalar_tensor_tensor(hid[n % 2][:], act1[n % 2][:], g, ps_h[n % 2][:, 1, :],
                                                   ALU.mult, ALU.mult).then_inc(hid_ready[k], 1)
                if n > 0:
                    dve.wait_ge(t_done[k], now(i * STEPS + n))
                    if n - 1 < 2:
                        dve.wait_ge(o_done[1 - k], now((i + k) * STEPS))
                    else:
                        dve.wait_ge(o_done[k], now(i * STEPS + n - 2))
                    nc.vector.tensor_copy(hidT[(n - 1) % 2][:], ps_t[(n - 1) % 2][:]).then_inc(hidT_ready[k], 1)
            dve.wait_ge(o_done[k], now(i * STEPS + STEPS))
            dve.wait_ge(out_stored[k], now(i * 16))
            nc.vector.tensor_tensor(out[k][:], ps_o[k][:], x[k][:], ALU.add).then_inc(out_ready[k], 1)

        with nc.Block() as block:
            @block.sync
            def _(sp):
                sp.dma_start(rw[:], a["rw"]).then_inc(w_loaded, 16)
                sp.dma_start(rb[:], a["rb"].rearrange("(o n) -> o n", o=1).broadcast_to([P, EXPERTS])).then_inc(w_loaded, 16)
                for w, n in enumerate(("w1", "w2")):
                    sp.dma_start(w12[:, 0:EXPERTS, w, :], a["e" + n].rearrange("e p n -> p e n")).then_inc(w_loaded, 16)
                    sp.dma_start(w12[:, EXPERTS, w, :], a["s" + n]).then_inc(w_loaded, 16)
                sp.dma_start(w3[:, 0:EXPERTS], a["ew3"].rearrange("e (h p) n -> p e h n", p=P)).then_inc(w_loaded, 16)
                sp.dma_start(w3[:, EXPERTS], a["sw3"].rearrange("(h p) n -> p h n", p=P)).then_inc(w_loaded, 16)
                for k in range(2):
                    sp.dma_start(x[k][:], src[k * UNIT:(k + 1) * UNIT, :].rearrange("(j p) d -> p j d", p=P)).then_inc(x_loaded[k], 16)
                with sp.Fori(0, B - 1) as i:
                    for k in range(2):
                        sp.wait_ge(out_ready[k], i + 1)
                        sp.dma_start(unit_of(dst, i, k), out[k][:]).then_inc(out_stored[k], 16)
                        sp.dma_start(x[k][:], unit_of(src, i + 1, k)).then_inc(x_loaded[k], 16)
                for k in range(2):
                    sp.wait_ge(out_ready[k], B)
                    sp.dma_start(dst[(B - 1) * T + k * UNIT:(B - 1) * T + (k + 1) * UNIT, :].rearrange("(j p) d -> p j d", p=P),
                                 out[k][:]).then_inc(out_stored[k], 16)
                for k in range(2):
                    sp.wait_ge(out_stored[k], B * 16)

            @block.tensor
            def _(pe):
                pe.wait_ge(w_loaded, 8 * 16)
                prepare(0, 0)
                route(0, 0)

                def unit(i, k, more):
                    ni, nk = (i, 1) if k == 0 else (i + 1, 0)
                    for n in range(STEPS + 2):
                        if n < STEPS:
                            hidden(i, k, n)
                        if 0 < n <= STEPS:
                            turn_hidden(i, k, n - 1)
                        if n > 1:
                            back(i, k, n - 2)
                        if more and n == 12:
                            prepare(ni, nk)
                        if more and n == 16:
                            route(ni, nk)

                turns = Turns(pe, stage + "_pe", FFN_STRIDES)
                with pe.Fori(0, B - 1) as turn:
                    i = Linear(turns, turn)
                    for k in range(2):
                        unit(i, k, True)
                    turns.step()
                for k in range(2):
                    unit(B - 1, k, k == 0)

            @block.vector
            def _(dve):
                dve.wait_ge(w_loaded, 8 * 16)
                dve.wait_ge(ready, 2)
                norm_dve(dve, 0, 0)
                gates_dve(dve, 0, 0)

                def unit(i, k, more):
                    ni, nk = (i, 1) if k == 0 else (i + 1, 0)
                    experts_dve(dve, i, k)
                    if more:
                        gates_dve(dve, ni, nk)

                turns = Turns(dve, stage + "_dve", FFN_STRIDES)
                with dve.Fori(0, B - 1) as turn:
                    i = Linear(turns, turn)
                    for k in range(2):
                        norm_dve(dve, *((i, 1) if k == 0 else (i + 1, 0)))
                        unit(i, k, True)
                    turns.step()
                norm_dve(dve, B - 1, 1)
                unit(B - 1, 0, True)
                unit(B - 1, 1, False)

            @block.scalar
            def _(act):
                act.wait_ge(w_loaded, 8 * 16)

                def prep(i, k):
                    act.wait_ge(xT_made[k], now(i + 1))
                    act.wait_ge(h_done[k], now(i * STEPS))
                    nc.scalar.activation(xnT[k][:], ps_x[:], ACT.Copy).then_inc(xT_ready[k], 1)

                def gate_act(i, k):
                    act.wait_ge(gap_ready[k], now(i * 2 + 2))
                    act.wait_ge(pick_ready[1 - k], now((i + k) * 4))
                    nc.scalar.activation(gate[:], gap[:], ACT.Sigmoid).then_inc(gate_ready[k], 1)

                def unit(i, k, more):
                    ni, nk = (i, 1) if k == 0 else (i + 1, 0)
                    for n in range(STEPS):
                        act.wait_ge(h_done[k], now(i * STEPS + n + 1))
                        if n < 2:
                            act.wait_ge(hid_ready[1 - k], now((i + k) * STEPS))
                        else:
                            act.wait_ge(hid_ready[k], now(i * STEPS + n - 1))
                        nc.scalar.activation(act1[n % 2][:], ps_h[n % 2][:, 0, :], ACT.Silu).then_inc(act_ready[k], 1)
                        if more and n == 13:
                            prep(ni, nk)
                    if more:
                        gate_act(ni, nk)

                prep(0, 0)
                gate_act(0, 0)
                turns = Turns(act, stage + "_act", FFN_STRIDES)
                with act.Fori(0, B - 1) as turn:
                    i = Linear(turns, turn)
                    for k in range(2):
                        unit(i, k, True)
                    turns.step()
                for k in range(2):
                    unit(B - 1, k, k == 0)

            @block.gpsimd
            def _(pool):
                nc.gpsimd.memset(power[:], -0.5).then_inc(ready, 1)
                nc.gpsimd.iota(number[:], pattern=[[0, UPT], [1, EXPERTS]], base=0, channel_multiplier=0,
                               allow_small_or_imprecise_dtypes=True).then_inc(ready, 1)
                pool.wait_ge(ready, 2)
                with pool.Fori(0, B) as i:
                    for k in range(2):
                        pool.wait_ge(mean[k], i * UPT + UPT)
                        pool.wait_ge(xn_ready[1 - k], (i + k) * UPT)
                        pool.sem_inc(passed, 1)
                        nc.gpsimd.tensor_scalar(veps[:], mv[:, :, 1], EPS, 1.0, ALU.add, ALU.mult).then_inc(veps_ready[k], 1)
                        pool.wait_ge(veps_ready[k], i + 1)
                        nc.gpsimd.tensor_tensor(rstd[:], veps[:], power[:], ALU.pow).then_inc(rstd_ready[k], 1)
        m.clear()


INNER, STATES, TAPS, DT_RANK = 256, 16, 4, 64
CH = INNER // P
BC = 2 * STATES
NS = STATES * CH
ITEMS = 9
AT = {0: [0], 1: [], 3: [1], 4: [2], 5: [3], 6: [4], 7: [5, 6], 8: [7], 9: [8, 9], 10: [10, 11], 11: [12], 12: [13], 13: [14], 14: [15]}
FINISH_AT, OUT_AT = 2, 3
LAG = 2
SCAN_STRIDES = sorted({1, 2, 4, 16, STATES, NS, ITEMS, UPT})


def scan(nc, dram, c, a, src, dst):
    with ExitStack() as ctx:
        m = Mem(nc, ctx, "ssm")
        win, wconv = m.sb("win", [P, 2 * INNER]), m.sb("wconv", [P, TAPS, INNER])
        taps = m.sb("taps", [P, INNER, TAPS])
        conv_b, dt_b, skip = m.sb("conv_b", [P, CH]), m.sb("dt_b", [P, CH]), m.sb("skip", [P, CH])
        alog, aneg = m.sb("alog", [P, CH, STATES]), m.sb("aneg", [P, CH, STATES])
        wdr, wbc = m.sb("wdr", [P, CH, DT_RANK]), m.sb("wbc", [P, CH, PARTS, BC])
        wdt, wout = m.sb("wdt", [DT_RANK, INNER]), m.sb("wout", [P, CH, D])
        pick = m.sb("pick", [P, BC, P], BF16)
        x = [m.sb(f"x{k}", [P, UPT, D]) for k in range(2)]
        stats, mv = m.sb("stats", [P, UPT, 6]), m.sb("mv", [P, UPT, 2])
        veps, power, rstd = m.sb("veps", [P, UPT]), m.sb("power", [P, UPT]), m.sb("rstd", [P, UPT])
        xn, xr = m.sb("xn", [P, UPT, D]), m.sb("xr", [P, UPT, D])
        xnT = [m.sb(f"xnT{k}", [P, TAPS - 1 + UNIT]) for k in range(2)]
        pre = m.sb("pre", [P, 2 * CH, UNIT])
        gated = [m.sb(f"gated{k}", [P, 2 * CH, UNIT]) for k in range(2)]
        dr = m.sb("dr", [DT_RANK, UNIT])
        stack = [m.sb(f"stack{k}", [PARTS * BC, UNIT], BF16) for k in range(2)]
        rest, part2 = m.sb("rest", [PARTS * BC, UNIT]), m.sb("part2", [PARTS * BC, UNIT], BF16)
        dtx, soft = m.sb("dtx", [P, CH, UNIT]), m.sb("soft", [P, CH, UNIT])
        delta = [m.sb(f"delta{k}", [P, CH, UNIT]) for k in range(2)]
        u = [m.sb(f"u{k}", [P, CH, UNIT]) for k in range(2)]
        decay = [[m.sb(f"decay{ch}{s}", [P, UNIT]) for s in range(2)] for ch in range(CH)]
        h0 = [m.sb(f"h0{ch}", [P, STATES, UNIT]) for ch in range(CH)]
        h1 = [m.sb(f"h1{ch}", [P, 2, UNIT]) for ch in range(CH)]
        cb = [m.sb(f"cb{s}", [P, UNIT]) for s in range(2)]
        hc = [[m.sb(f"hc{ch}{s}", [P, UNIT]) for s in range(2)] for ch in range(CH)]
        yd, yg, out = m.sb("yd", [P, CH, UNIT]), m.sb("yg", [P, CH, UNIT]), m.sb("out", [P, UPT, D])
        ps_b = [m.ps(f"ps_b{s}", [P, UNIT]) for s in range(2)]
        ps_c, ps_m = m.ps("ps_c", [P, UNIT]), m.ps("ps_m", [P, UNIT])
        ps_d = [m.ps(f"ps_d{ch}", [P, UNIT]) for ch in range(CH)]
        ps_y = [m.ps(f"ps_y{ch}", [P, UNIT]) for ch in range(CH)]
        w_loaded, w_ready, filled, passed, a_ready = (m.sem(n) for n in ("w_ld", "w_ready", "filled", "passed", "a_ready"))
        x_loaded, stat, mean, veps_ready, rstd_ready, xn_ready = (m.pair(n) for n in ("x_ld", "stat", "mean", "veps", "rstd", "xn"))
        item_done, item_free, gated_ready = (m.pair(n) for n in ("item_done", "item_free", "gated"))
        halo, xr_loaded = m.sem("halo"), m.pair("xr_ld")
        part1_ready, part2_ready, part3_ready = (m.pair(n) for n in ("part1", "part2", "part3"))
        abs_ready, exp_ready, ln_ready, delta_ready, u_ready = (m.pair(n) for n in ("abs", "exp", "ln", "delta", "u"))
        b_done, c_done, c_kept, decay_ready = (m.pair(n) for n in ("b_done", "c_done", "c_kept", "decay"))
        dbx_done, scan_done, hc_done, y_done = (m.pair(n) for n in ("dbx", "scan", "hc", "y_done"))
        yd_ready, yg_ready, o_done, out_ready, out_stored = (m.pair(n) for n in ("yd", "yg", "o_done", "out", "out_st"))

        def after(i, k):
            return (i, 1) if k == 0 else (i + 1, 0)

        def item(i, k, j, build):
            if j == 0:
                nc.tensor.wait_ge(out_ready[k], now(i * 1))
                nc.tensor.wait_ge(item_free[1 - k], now((i + k) * ITEMS))
            else:
                nc.tensor.wait_ge(item_free[k], now(i * ITEMS + j))
            build().then_inc(item_done[k], 1)

        def turn_x(k):
            for j in range(UPT):
                done = nc.tensor.transpose(ps_m[:, j * P:(j + 1) * P], xn[:, j, :], c["ident"][:])
            return done

        def conv(k, ch):
            for tap in range(TAPS):
                done = nc.tensor.matmul(ps_m[:], wconv[:, tap, ch * P:(ch + 1) * P], xnT[k][:, tap:tap + UNIT],
                                        start=tap == 0, stop=tap == TAPS - 1)
            return done

        def gate_in(k, ch):
            return nc.tensor.matmul(ps_m[:], win[:, INNER + ch * P:INNER + (ch + 1) * P], xnT[k][:, TAPS - 1:], start=True, stop=True)

        def low_rank(k, w, rows):
            for ch in range(CH):
                done = nc.tensor.matmul(ps_m[0:rows, :], w[:, ch], gated[k][:, ch, :], start=ch == 0, stop=ch == CH - 1)
            return done

        def prepare_pe(i, k, n):
            if n == 2:
                nc.tensor.wait_ge(xn_ready[k], now(i * UPT + UPT))
                item(i, k, 0, lambda: turn_x(k))
            elif n in (3, 4):
                if n == 3 and k == 1:
                    nc.tensor.wait_ge(halo, now(i + 1))
                item(i, k, n - 2, lambda: conv(k, n - 3))
            elif n in (5, 6):
                item(i, k, n - 2, lambda: gate_in(k, n - 5))
            elif n == 8:
                nc.tensor.wait_ge(gated_ready[k], now(i + 1))
                item(i, k, 5, lambda: low_rank(k, wdr, DT_RANK))
            elif n == 9:
                item(i, k, 6, lambda: low_rank(k, wbc[:].rearrange("p c s r -> p c (s r)"), PARTS * BC))
            elif n in (10, 11):
                item(i, k, n - 3, lambda: nc.tensor.matmul(ps_m[:], wdt[:, (n - 10) * P:(n - 9) * P], dr[:], start=True, stop=True))

        def prepare_act(act, i, k, n):
            if n == 2:
                act.wait_ge(item_done[k], now(i * ITEMS + 1))
                act.wait_ge(halo, now(i * 1))
                nc.scalar.activation(xnT[k][:, TAPS - 1:], ps_m[:], ACT.Copy).then_inc(item_free[k], 1)
                if k == 1:
                    act.wait_ge(item_free[0], now(i * ITEMS + ITEMS))
                    nc.scalar.activation(xnT[1][:, 0:TAPS - 1], xnT[0][:, UNIT:], ACT.Copy).then_inc(halo, 1)
            elif 3 <= n <= 6:
                if n == 3:
                    act.wait_ge(gated_ready[1 - k], now(i + k))
                act.wait_ge(item_done[k], now(i * ITEMS + n - 1))
                if n < 5:
                    nc.scalar.activation(pre[:, n - 3, :], ps_m[:], ACT.Identity, bias=conv_b[:, n - 3:n - 2]).then_inc(item_free[k], 1)
                else:
                    nc.scalar.activation(pre[:, n - 3, :], ps_m[:], ACT.Copy).then_inc(item_free[k], 1)
            elif n == 7:
                act.wait_ge(item_free[k], now(i * ITEMS + 5))
                act.wait_ge(yg_ready[k], now(i * 2))
                nc.scalar.activation(gated[k][:], pre[:], ACT.Silu).then_inc(gated_ready[k], 1)
            elif n == 8:
                act.wait_ge(item_done[k], now(i * ITEMS + 6))
                act.wait_ge(item_done[1 - k], now((i + k) * ITEMS))
                nc.scalar.activation(dr[:], ps_m[0:DT_RANK, :], ACT.Copy).then_inc(item_free[k], 1)
            elif n == 9:
                act.wait_ge(item_done[k], now(i * ITEMS + 7))
                act.wait_ge(c_done[k], now(i * STATES))
                nc.scalar.activation(stack[k][:], ps_m[0:PARTS * BC, :], ACT.Copy).then_inc(part1_ready[k], 1)
            elif n == 10:
                act.wait_ge(item_free[k], now(i * ITEMS + 7))
                act.wait_ge(part3_ready[1 - k], now(i + k))
                nc.scalar.activation(stack[k][BC:2 * BC, :], rest[BC:2 * BC, :], ACT.Copy).then_inc(part2_ready[k], 1)
                nc.scalar.activation(part2[2 * BC:3 * BC, :], rest[2 * BC:3 * BC, :], ACT.Copy).then_inc(part2_ready[k], 1)
            elif n == 12:
                act.wait_ge(item_free[k], now(i * ITEMS + ITEMS))
                act.wait_ge(delta_ready[1 - k], now(i + k))
                nc.scalar.activation(soft[:], dtx[:], ACT.Abs).then_inc(abs_ready[k], 1)
                act.wait_ge(abs_ready[k], now(i + 1))
                nc.scalar.activation(soft[:], soft[:], ACT.Exp, scale=-1.0).then_inc(exp_ready[k], 1)
            elif n == 13:
                act.wait_ge(exp_ready[k], now(i + 1))
                nc.scalar.activation(soft[:], soft[:], ACT.Ln, bias=1.0).then_inc(ln_ready[k], 1)

        def prepare_dve(dve, i, k, n):
            if n == 0:
                dve.wait_ge(x_loaded[k], now(i * 16 + 16))
                for j in range(UPT):
                    nc.vector.bn_stats(stats[:, j, :], x[k][:, j, :]).then_inc(stat[k], 1)
                dve.wait_ge(stat[k], now(i * UPT + UPT))
                dve.sem_inc(passed, 1)
                for j in range(UPT):
                    nc.vector.bn_aggr(mv[:, j, :], stats[:, j, :]).then_inc(mean[k], 1)
            elif n == 1:
                dve.wait_ge(rstd_ready[k], now(i + 1))
                dve.wait_ge(item_done[1 - k], now((i + k) * ITEMS))
                for j in range(UPT):
                    nc.vector.tensor_scalar(xn[:, j, :], x[k][:, j, :], mv[:, j, 0:1], rstd[:, j:j + 1],
                                            ALU.subtract, ALU.mult).then_inc(xn_ready[k], 1)
            elif n == 9:
                dve.wait_ge(part1_ready[k], now(i + 1))
                dve.wait_ge(part3_ready[1 - k], now(i + k))
                nc.vector.tensor_tensor(rest[:], ps_m[0:PARTS * BC, :], stack[k][:], ALU.subtract).then_inc(item_free[k], 1)
            elif n in (10, 11):
                ch = n - 10
                dve.wait_ge(item_done[k], now(i * ITEMS + n - 2))
                dve.wait_ge(delta_ready[1 - k], now(i + k))
                nc.vector.tensor_scalar(dtx[:, ch, :], ps_m[:], dt_b[:, ch:ch + 1], None, ALU.add).then_inc(item_free[k], 1)
            elif n == 12:
                dve.wait_ge(part2_ready[k], now(i * 2 + 2))
                nc.vector.tensor_tensor(stack[k][2 * BC:3 * BC, :], rest[2 * BC:3 * BC, :], part2[2 * BC:3 * BC, :],
                                        ALU.subtract).then_inc(part3_ready[k], 1)
            elif n == 14:
                dve.wait_ge(ln_ready[k], now(i + 1))
                dve.wait_ge(decay_ready[k], now(i * NS))
                dve.wait_ge(u_ready[k], now(i * 1))
                nc.vector.scalar_tensor_tensor(delta[k][:], dtx[:], 0.0, soft[:], ALU.max, ALU.add).then_inc(delta_ready[k], 1)
            elif n == 15:
                dve.wait_ge(delta_ready[k], now(i + 1))
                dve.wait_ge(gated_ready[k], now(i + 1))
                dve.wait_ge(dbx_done[k], now(i * NS))
                nc.vector.tensor_tensor(u[k][:], delta[k][:], gated[k][:, 0:CH, :], ALU.mult).then_inc(u_ready[k], 1)

        def prepare_pool(pool, i, k, n):
            if n == 1:
                pool.wait_ge(mean[k], now(i * UPT + UPT))
                pool.wait_ge(xn_ready[1 - k], now((i + k) * UPT))
                pool.sem_inc(passed, 1)
                nc.gpsimd.tensor_scalar(veps[:], mv[:, :, 1], EPS, 1.0, ALU.add, ALU.mult).then_inc(veps_ready[k], 1)
                pool.wait_ge(veps_ready[k], now(i + 1))
                nc.gpsimd.tensor_tensor(rstd[:], veps[:], power[:], ALU.pow).then_inc(rstd_ready[k], 1)

        def core_pe(i, k, n):
            if True:
                if n == 0:
                    nc.tensor.wait_ge(part3_ready[k], now(i + 1))
                    nc.tensor.wait_ge(part2_ready[k], now(i * 2 + 2))
                if n < 2:
                    nc.tensor.wait_ge(dbx_done[1 - k], now((i + k) * NS))
                else:
                    nc.tensor.wait_ge(dbx_done[k], now(i * NS + (n - 1) * CH))
                nc.tensor.matmul(ps_b[n % 2][:], pick[0:PARTS * BC, n, :], stack[k][:], start=True, stop=True).then_inc(b_done[k], 1)
                if n == 0:
                    nc.tensor.wait_ge(c_kept[1 - k], now((i + k) * STATES))
                else:
                    nc.tensor.wait_ge(c_kept[k], now(i * STATES + n))
                nc.tensor.matmul(ps_c[:], pick[0:PARTS * BC, STATES + n, :], stack[k][:], start=True, stop=True).then_inc(c_done[k], 1)
            if n >= LAG:
                sum_pe(i, k, n - LAG)

        def sum_pe(i, k, r):
            for ch in range(CH):
                if r == 0:
                    nc.tensor.wait_ge(yd_ready[1 - k], now((i + k) * 2))
                nc.tensor.wait_ge(hc_done[k], now(i * NS + r * CH + ch + 1))
                nc.tensor.matmul(ps_y[ch][:], c["ident"][:], hc[ch][r % 2][:], start=r == 0, stop=r == STATES - 1).then_inc(y_done[k], 1)

        def core_act(act, i, k, n):
            if n == 0:
                act.wait_ge(delta_ready[k], now(i + 1))
            for ch in range(CH):
                if n < 2:
                    act.wait_ge(scan_done[1 - k], now((i + k) * NS))
                else:
                    act.wait_ge(scan_done[k], now(i * NS + (n - 2) * CH + ch + 1))
                nc.scalar.activation(decay[ch][n % 2][:], delta[k][:, ch, :], ACT.Exp, scale=aneg[:, ch, n:n + 1]).then_inc(decay_ready[k], 1)
            act.wait_ge(c_done[k], now(i * STATES + n + 1))
            if n < 2:
                act.wait_ge(hc_done[1 - k], now((i + k) * NS))
            else:
                act.wait_ge(hc_done[k], now(i * NS + (n - 1) * CH))
            nc.scalar.activation(cb[n % 2][:], ps_c[:], ACT.Copy).then_inc(c_kept[k], 1)

        def core_dve(dve, i, k, n):
            if n == 0:
                dve.wait_ge(u_ready[k], now(i + 1))
                if k == 0:
                    dve.wait_ge(hc_done[0], now(i * NS))
                dve.wait_ge(scan_done[1 - k], now((i + k) * NS))
            dve.wait_ge(b_done[k], now(i * STATES + n + 1))
            for ch in range(CH):
                if n:
                    dve.wait_ge(scan_done[k], now(i * NS + (n - 1) * CH + ch + 1))
                nc.vector.tensor_tensor(ps_d[ch][:], u[k][:, ch, :], ps_b[n % 2][:], ALU.mult).then_inc(dbx_done[k], 1)
            for ch in range(CH):
                q = n * CH + ch + 1
                dve.wait_ge(dbx_done[k], now(i * NS + q))
                dve.wait_ge(decay_ready[k], now(i * NS + q))
                if k == 0:
                    state, start = h0[ch][:, n, :], 0.0
                else:
                    if n < 2:
                        dve.wait_ge(hc_done[1], now(i * NS))
                    else:
                        dve.wait_ge(hc_done[1], now(i * NS + (n - 2) * CH + ch + 1))
                    state, start = h1[ch][:, n % 2, :], h0[ch][:, n, UNIT - 1:UNIT]
                nc.vector.tensor_tensor_scan(state, decay[ch][n % 2][:], ps_d[ch][:], start, ALU.mult, ALU.add).then_inc(scan_done[k], 1)

        def core_pool(pool, i, k, n):
            pool.wait_ge(c_kept[k], now(i * STATES + n + 1))
            for ch in range(CH):
                pool.wait_ge(scan_done[k], now(i * NS + n * CH + ch + 1))
                if n < 2:
                    pool.wait_ge(y_done[1 - k], now((i + k) * NS))
                else:
                    pool.wait_ge(y_done[k], now(i * NS + (n - 2) * CH + ch + 1))
                state = h0[ch][:, n, :] if k == 0 else h1[ch][:, n % 2, :]
                nc.gpsimd.tensor_tensor(hc[ch][n % 2][:], state, cb[n % 2][:], ALU.mult).then_inc(hc_done[k], 1)

        def finish_dve(dve, i, k):
            for ch in range(CH):
                dve.wait_ge(y_done[k], now(i * NS + NS - CH + ch + 1))
                dve.wait_ge(yg_ready[1 - k], now((i + k) * 2))
                nc.vector.scalar_tensor_tensor(yd[:, ch, :], gated[k][:, ch, :], skip[:, ch:ch + 1], ps_y[ch][:],
                                               ALU.mult, ALU.add).then_inc(yd_ready[k], 1)
            for ch in range(CH):
                dve.wait_ge(yd_ready[k], now(i * 2 + ch + 1))
                dve.wait_ge(o_done[1 - k], now(i + k))
                nc.vector.tensor_tensor(yg[:, ch, :], yd[:, ch, :], gated[k][:, CH + ch, :], ALU.mult).then_inc(yg_ready[k], 1)

        def project_out(i, k, more):
            nc.tensor.wait_ge(yg_ready[k], now(i * 2 + 2))
            if more:
                nc.tensor.wait_ge(item_free[1 - k], now((i + k + 1) * ITEMS))
            nc.tensor.wait_ge(out_ready[1 - k], now(i + k))
            for j in range(UPT):
                for ch in range(CH):
                    done = nc.tensor.matmul(ps_m[:, j * P:(j + 1) * P], yg[:, ch, j * P:(j + 1) * P], wout[:, ch, :],
                                            start=ch == 0, stop=ch == CH - 1)
            done.then_inc(o_done[k], 1)

        def add_x(dve, i, k):
            dve.wait_ge(o_done[k], now(i + 1))
            dve.wait_ge(xr_loaded[k], now(i * 16 + 16))
            dve.wait_ge(out_stored[1 - k], now((i + k) * 16))
            nc.vector.tensor_tensor(out[:].rearrange("p j d -> p (j d)"), ps_m[:], xr[:].rearrange("p j d -> p (j d)"), ALU.add).then_inc(out_ready[k], 1)

        def unit_of(t, i, k):
            return t[ds(i * T + k * UNIT, UNIT), :].rearrange("(j p) d -> p j d", p=P)

        def pe_unit(i, k, first, more):
            (pi, pk), (ni, nk) = (i - 1, 1) if k == 0 else (i, 0), after(i, k)
            for n in range(STATES):
                core_pe(i, k, n)
                if not first and n < LAG:
                    sum_pe(pi, pk, STATES - LAG + n)
                if not first and n == OUT_AT:
                    project_out(pi, pk, True)
                if more:
                    for part in AT.get(n, []):
                        prepare_pe(ni, nk, part)

        def dve_unit(dve, i, k, first, more):
            (pi, pk), (ni, nk) = (i - 1, 1) if k == 0 else (i, 0), after(i, k)
            for n in range(STATES):
                if not first and n == FINISH_AT:
                    finish_dve(dve, pi, pk)
                core_dve(dve, i, k, n)
                if not first and n == OUT_AT:
                    add_x(dve, pi, pk)
                if more:
                    for part in AT.get(n, []):
                        prepare_dve(dve, ni, nk, part)

        def act_unit(act, i, k, more):
            for n in range(STATES):
                core_act(act, i, k, n)
                if more:
                    for part in AT.get(n, []):
                        prepare_act(act, *after(i, k), part)

        def pool_unit(pool, i, k, more):
            for n in range(STATES):
                core_pool(pool, i, k, n)
                if more and n == 0:
                    prepare_pool(pool, *after(i, k), 1)

        last = B - 1
        with nc.Block() as block:
            @block.sync
            def _(sp):
                sp.dma_start(x[0][:], src[0:UNIT, :].rearrange("(j p) d -> p j d", p=P)).then_inc(x_loaded[0], 16)
                sp.dma_start(x[1][:], src[UNIT:2 * UNIT, :].rearrange("(j p) d -> p j d", p=P)).then_inc(x_loaded[1], 16)
                loads = [(win[:], a["W_in"]), (taps[:], a["conv_w"].rearrange("n o t -> o n t").broadcast_to([P, INNER, TAPS])),
                         (alog[:], a["A_log"].rearrange("(c p) n -> p c n", p=P)),
                         (wdr[:], a["W_x"][:, 0:DT_RANK].rearrange("(c p) n -> p c n", p=P)), (wdt[:], a["W_dt"]),
                         (wout[:], a["W_out"].rearrange("(c p) n -> p c n", p=P))]
                loads += [(wbc[:, :, s, :], a["W_x"][:, DT_RANK:].rearrange("(c p) n -> p c n", p=P)) for s in range(PARTS)]
                for to, what in loads:
                    sp.dma_start(to, what).then_inc(w_loaded, 16)
                for to, what in ((conv_b, "conv_b"), (dt_b, "b_dt"), (skip, "D")):
                    sp.dma_start(to[:], a[what].rearrange("(c p) -> p c", p=P), allow_slow_non_contiguous=True).then_inc(w_loaded, 16)
                with sp.Fori(0, last) as i:
                    for k in range(2):
                        if k == 0:
                            sp.wait_ge(out_ready[1], i)
                        else:
                            sp.wait_ge(out_ready[0], i + 1)
                        sp.dma_start(xr[:], unit_of(src, i, k)).then_inc(xr_loaded[k], 16)
                        sp.wait_ge(xn_ready[k], i * UPT + UPT)
                        sp.dma_start(x[k][:], unit_of(src, i + 1, k)).then_inc(x_loaded[k], 16)
                        sp.wait_ge(out_ready[k], i + 1)
                        sp.dma_start(unit_of(dst, i, k), out[:]).then_inc(out_stored[k], 16)
                for k in range(2):
                    rows = slice(last * T + k * UNIT, last * T + (k + 1) * UNIT)
                    sp.wait_ge(out_ready[1 - k], last + k)
                    sp.dma_start(xr[:], src[rows, :].rearrange("(j p) d -> p j d", p=P)).then_inc(xr_loaded[k], 16)
                    sp.wait_ge(out_ready[k], last + 1)
                    sp.dma_start(dst[rows, :].rearrange("(j p) d -> p j d", p=P), out[:]).then_inc(out_stored[k], 16)
                for k in range(2):
                    sp.wait_ge(out_stored[k], B * 16)

            @block.tensor
            def _(pe):
                pe.wait_ge(w_ready, TAPS)
                pe.wait_ge(w_loaded, 12 * 16)
                pe.wait_ge(filled, 7)
                for part in range(16):
                    prepare_pe(0, 0, part)
                pe_unit(0, 0, True, True)
                turns = Turns(pe, "ssm_pe", SCAN_STRIDES)
                with pe.Fori(0, last) as turn:
                    i = Linear(turns, turn)
                    pe_unit(i, 1, False, True)
                    pe_unit(i + 1, 0, False, True)
                    turns.step()
                pe_unit(last, 1, False, False)
                for r in range(STATES - LAG, STATES):
                    sum_pe(last, 1, r)
                project_out(last, 1, False)

            @block.vector
            def _(dve):
                nc.vector.memset(xnT[0][:, 0:TAPS - 1], 0.0).then_inc(filled, 1)
                dve.wait_ge(w_loaded, 12 * 16)
                for tap in range(TAPS):
                    nc.vector.tensor_tensor(wconv[:, tap, :], win[:, 0:INNER], taps[:, :, tap], ALU.mult).then_inc(w_ready, 1)
                dve.wait_ge(a_ready, 1)
                nc.vector.tensor_scalar(aneg[:], aneg[:], -1.0, None, ALU.mult).then_inc(a_ready, 1)
                for part in range(16):
                    prepare_dve(dve, 0, 0, part)
                dve_unit(dve, 0, 0, True, True)
                turns = Turns(dve, "ssm_dve", SCAN_STRIDES)
                with dve.Fori(0, last) as turn:
                    i = Linear(turns, turn)
                    dve_unit(dve, i, 1, False, True)
                    dve_unit(dve, i + 1, 0, False, True)
                    turns.step()
                dve_unit(dve, last, 1, False, False)
                finish_dve(dve, last, 1)
                add_x(dve, last, 1)

            @block.scalar
            def _(act):
                act.wait_ge(w_loaded, 12 * 16)
                nc.scalar.activation(aneg[:], alog[:], ACT.Exp).then_inc(a_ready, 1)
                act.wait_ge(a_ready, 2)
                for part in range(16):
                    prepare_act(act, 0, 0, part)
                act_unit(act, 0, 0, True)
                turns = Turns(act, "ssm_act", SCAN_STRIDES)
                with act.Fori(0, last) as turn:
                    i = Linear(turns, turn)
                    act_unit(act, i, 1, True)
                    act_unit(act, i + 1, 0, True)
                    turns.step()
                act_unit(act, last, 1, False)

            @block.gpsimd
            def _(pool):
                nc.gpsimd.memset(power[:], -0.5).then_inc(filled, 1)
                nc.gpsimd.memset(pick[:], 0.0).then_inc(filled, 1)
                pool.wait_ge(filled, 3)
                prepare_pool(pool, 0, 0, 1)
                for s in range(PARTS):
                    nc.gpsimd.affine_select(out=pick[:], in_=pick[:], compare_op=ALU.not_equal, fill=1.0, base=-BC * s,
                                            pattern=[[-1, BC], [0, P]], channel_multiplier=1).then_inc(filled, 1)
                    pool.wait_ge(filled, 4 + s)
                pool.sem_inc(filled, 1)
                pool_unit(pool, 0, 0, True)
                turns = Turns(pool, "ssm_pool", SCAN_STRIDES)
                with pool.Fori(0, last) as turn:
                    i = Linear(turns, turn)
                    pool_unit(pool, i, 1, True)
                    pool_unit(pool, i + 1, 0, True)
                    turns.step()
                pool_unit(pool, last, 1, False)
        m.clear()


def build(nc, x, w_attn, b_attn, w_k2, b_k2, w_proj, b_proj, W_in, conv_w, conv_b, W_x, W_dt, b_dt, A_log, D_skip, W_out,
          sw1, sw2, sw3, ew1, ew2, ew3, rw, rb, y):
    rows = x.rearrange("b t d -> (b t) d")

    def scratch(name, shape, dt=F32):
        return nc.dram_tensor(name, shape, dt).ap()

    dram = {"xn": scratch("xn_dram", (N + 1, D)), "vp": scratch("vp_dram", (N, HEADS * (HD + 1))),
            "fT": scratch("fT_dram", (2, P, N)), "parts": scratch("parts_dram", (4 * PARTS, B, P, T), BF16),
            "yar": scratch("yar_dram", (16, T, 32)), "x1": scratch("x1_dram", (N, D))}
    x2, x3 = scratch("x2_dram", (N, D)), scratch("x3_dram", (N, D))
    experts = {"sw1": sw1, "sw2": sw2, "sw3": sw3, "ew1": ew1, "ew2": ew2, "ew3": ew3, "rw": rw, "rb": rb}
    with ExitStack() as ctx:
        c = constants(nc, Mem(nc, ctx, "const"), dram)
        project(nc, dram, c, {"x": rows, "w_attn": w_attn, "b_attn": b_attn, "w_k2": w_k2, "b_k2": b_k2})
        attention(nc, dram, c)
        memory(nc, dram, c, {"x": rows, "w_proj": w_proj, "b_proj": b_proj})
        ffn(nc, dram, c, experts, "ffn1", dram["x1"], x2)
        scan(nc, dram, c, {"W_in": W_in, "conv_w": conv_w, "conv_b": conv_b, "W_x": W_x, "W_dt": W_dt, "b_dt": b_dt,
                           "A_log": A_log, "D": D_skip, "W_out": W_out}, x2, x3)
        ffn(nc, dram, c, experts, "ffn2", x3, y.rearrange("b t d -> (b t) d"))


_INS = ["L0_attn_a_x", "L0_attn_a_w_attn", "L0_attn_a_b_attn", "L0_attn_a_w_k2", "L0_attn_a_b_k2", "L0_attn_a_w_proj",
        "L0_attn_a_b_proj", "L0_attn_b_W_in", "L0_attn_b_conv_w", "L0_attn_b_conv_b", "L0_attn_b_W_x", "L0_attn_b_W_dt",
        "L0_attn_b_b_dt", "L0_attn_b_A_log", "L0_attn_b_D", "L0_attn_b_W_out", "L0_ffn_sw1", "L0_ffn_sw2", "L0_ffn_sw3",
        "L0_ffn_ew1", "L0_ffn_ew2", "L0_ffn_ew3", "L0_ffn_rw", "L0_ffn_rb"]
_OUTS = [((4, 1024, 128), "float32")]


def kernel(**inputs):
    import numpy as _np
    import concourse.bacc as _bacc
    from concourse import mybir as _mybir
    from concourse.bass_utils import run_bass_kernel_spmd as _run

    nc = _bacc.Bacc("TRN2", target_bir_lowering=False, num_devices=1)
    arrays, args = {}, []
    for name in _INS:
        a = _np.ascontiguousarray(inputs[name])
        arrays[f"in_{name}_dram"] = a
        args.append(nc.dram_tensor(f"in_{name}_dram", a.shape, _mybir.dt.from_np(a.dtype), kind="ExternalInput").ap())
    for i, (shape, dtype) in enumerate(_OUTS):
        dt = _mybir.dt.from_np(_np.dtype(dtype))
        args.append(nc.dram_tensor(f"out_{i}_dram", shape, dt, kind="ExternalOutput").ap())
    build(nc, *args)
    r = _run(nc, [arrays], core_ids=[0])
    return r.results[0]["out_0_dram"]
```

```python
from contextlib import ExitStack

import concourse.bass as bass
from concourse import mybir

ALU = mybir.AluOpType
ACT = mybir.ActivationFunctionType
AX = mybir.AxisListType
F32 = mybir.dt.float32
BF16 = mybir.dt.bfloat16
I32 = mybir.dt.int32

P = 128
B, T, D = 4, 1024, 128
N = B * T
HEADS, HD = 16, 8
GH = 4
GPB = HEADS // GH
GROUPS = B * GPB
BLK = T // P
PARTS = 3
COMBOS = PARTS * PARTS
KROWS = COMBOS * HD
MROW = 96
SCALE = HD ** -0.5
EPS = 1e-5
MINUS = -1e30
UNIT = 512
UPT = UNIT // P
ds = bass.ds


class Mem:

    def __init__(self, nc, ctx, stage):
        self.nc, self.ctx, self.stage, self.sems = nc, ctx, stage, []

    def sb(self, name, shape, dt=F32):
        return self.ctx.enter_context(self.nc.sbuf_tensor(f"{self.stage}_{name}", shape, dt))

    def ps(self, name, shape, dt=F32):
        return self.ctx.enter_context(self.nc.psum_tensor(f"{self.stage}_{name}", shape, dt))

    def sem(self, name):
        self.sems.append(self.ctx.enter_context(self.nc.semaphore(f"{self.stage}_{name}")))
        return self.sems[-1]

    def clear(self):
        with self.nc.Block() as block:
            @block.gpsimd
            def _(pool):
                for sem in self.sems:
                    pool.sem_clear(sem)

    def pair(self, name):
        return [self.sem(f"{name}{k}") for k in range(2)]


class Turns:

    def __init__(self, eng, name, strides, room=4, first=0):
        self.eng = eng
        self.kept = {s: eng.alloc_register(f"{name}_turn_x{s}") for s in strides}
        self.scratch = [eng.alloc_register(f"{name}_value{n}") for n in range(room)]
        self.held = {}
        for s, r in self.kept.items():
            eng.reg_mov(r, s * first)

    def step(self):
        self.held = {}
        for s, r in self.kept.items():
            self.eng.reg_add(r, r, s)

    def at(self, stride, c):
        if c == 0:
            return self.kept[stride]
        if (stride, c) in self.held:
            return self.held[stride, c]
        if len(self.held) == len(self.scratch):
            r = self.held.pop(next(iter(self.held)))
        else:
            r = self.scratch[len(self.held)]
        self.held[stride, c] = r
        self.eng.reg_add(r, self.kept[stride], c)
        return r


class Linear:

    def __init__(self, turns, i, a=1, b=0):
        self.turns, self.i, self.a, self.b = turns, i, a, b

    def __mul__(self, n):
        return Linear(self.turns, self.i, self.a * n, self.b * n)

    def __add__(self, n):
        return Linear(self.turns, self.i, self.a, self.b + n)

    def __sub__(self, n):
        return self + -n


def now(v):
    return v.turns.at(v.a, v.b) if isinstance(v, Linear) else v


def constants(nc, m, dram):
    c = {}
    c["ident"] = m.sb("ident", [P, P])
    c["identb"] = m.sb("identb", [P, P], BF16)
    c["mask_rows"] = m.sb("mask_rows", [P, P], BF16)
    c["mask_cols"] = m.sb("mask_cols", [P, P], BF16)
    c["strict"] = m.sb("strict", [P, GH, P])
    c["same_head"] = m.sb("same_head", [P, P])
    zrow = m.sb("zrow", [1, D])
    filled, made, zero_stored = m.sem("filled"), m.sem("made"), m.sem("zero_stored")
    with nc.Block() as block:
        @block.gpsimd
        def _(pool):
            for t, v in ((c["ident"], 0.0), (c["identb"], 0.0), (c["mask_rows"], 0.0), (c["mask_cols"], 0.0),
                         (c["strict"], 1.0), (c["same_head"], 0.0), (zrow, 0.0)):
                nc.gpsimd.memset(t[:], v).then_inc(filled, 1)
            pool.wait_ge(filled, 7)
            nc.gpsimd.affine_select(out=c["ident"][:], in_=c["ident"][:], compare_op=ALU.not_equal, fill=1.0,
                                    base=0, pattern=[[-1, P]], channel_multiplier=1).then_inc(made, 1)
            nc.gpsimd.affine_select(out=c["identb"][:], in_=c["identb"][:], compare_op=ALU.not_equal, fill=1.0,
                                    base=0, pattern=[[-1, P]], channel_multiplier=1).then_inc(made, 1)
            nc.gpsimd.affine_select(out=c["mask_rows"][:], in_=c["mask_rows"][:], compare_op=ALU.is_ge, fill=MINUS,
                                    base=0, pattern=[[-1, P]], channel_multiplier=1).then_inc(made, 1)
            nc.gpsimd.affine_select(out=c["mask_cols"][:], in_=c["mask_cols"][:], compare_op=ALU.is_ge, fill=MINUS,
                                    base=0, pattern=[[1, P]], channel_multiplier=-1).then_inc(made, 1)
            nc.gpsimd.affine_select(out=c["strict"][:], in_=c["strict"][:], compare_op=ALU.is_gt, fill=0.0,
                                    base=0, pattern=[[0, GH], [1, P]], channel_multiplier=-1).then_inc(made, 1)
            heads = c["same_head"][:].rearrange("p (g h d) -> p g h d", g=GPB, d=HD)
            for d in range(HD):
                nc.gpsimd.affine_select(out=heads, in_=heads, compare_op=ALU.not_equal, fill=1.0, base=-GH * d,
                                        pattern=[[-GH * HD, GPB], [-1, GH], [0, HD]], channel_multiplier=1).then_inc(made, 1)
                pool.wait_ge(made, 6 + d)

        @block.sync
        def _(sp):
            sp.wait_ge(filled, 7)
            sp.dma_start(dram["xn"][N:N + 1, :], zrow[:]).then_inc(zero_stored, 16)
            sp.wait_ge(zero_stored, 16)
    return c


def project(nc, dram, c, a):
    with ExitStack() as ctx:
        m = Mem(nc, ctx, "proj")
        wrow = m.sb("wrow", [P, 3, P])
        wT = m.sb("wT", [P, 3, P])
        brow = m.sb("brow", [1, 3, P])
        bperm = m.sb("bperm", [1, 3, P])
        bias = m.sb("bias", [P, 3])
        sbias = m.sb("sbias", [P, 3])
        x = [m.sb(f"x{k}", [P, UPT, D]) for k in range(2)]
        stats = m.sb("stats", [P, UPT, 6])
        mv = [m.sb(f"mv{k}", [P, UPT, 2]) for k in range(2)]
        veps = m.sb("veps", [P, UPT])
        power = m.sb("power", [P, UPT])
        rstd = [m.sb(f"rstd{k}", [P, UPT]) for k in range(2)]
        xn = [m.sb(f"xn{k}", [P, UPT, D]) for k in range(2)]
        vp = [m.sb(f"vp{k}", [P, UPT, HEADS, HD + 1]) for k in range(2)]
        xnT = [m.sb(f"xnT{k}", [P, UNIT]) for k in range(2)]
        f = [m.sb(f"f{k}", [P, 4, UNIT]) for k in range(2)]
        r = [m.sb(f"r{k}", [P, 4, UNIT]) for k in range(2)]
        parts = [m.sb(f"parts{k}", [P, 4, PARTS, UNIT], BF16) for k in range(2)]
        psw = m.ps("psw", [P, UNIT])
        psx = [m.ps(f"psx{k}", [P, UNIT]) for k in range(2)]
        psq = [m.ps(f"psq{j}", [P, UNIT]) for j in range(3)]
        w_loaded, w_turned, w_ready = m.sem("w_loaded"), m.sem("w_turned"), m.sem("w_ready")
        bias_ready, ones_ready = m.sem("bias_ready"), m.sem("ones_ready")
        veps_ready, passed = m.pair("veps"), m.sem("passed")
        x_loaded, stat, mean, rstd_ready, xn_ready = (m.pair(n) for n in ("x_loaded", "stat", "mean", "rstd", "xn_ready"))
        vp_ready, xT_made, xT_ready, mm_done = (m.pair(n) for n in ("vp_ready", "xT_made", "xT_ready", "mm_done"))
        q_ready, k_ready, ka_ready, qa_ready = (m.pair(n) for n in ("q_ready", "k_ready", "ka_ready", "qa_ready"))
        part1, rest1, part2, part3 = (m.pair(n) for n in ("part1", "rest1", "part2", "part3"))
        xn_stored, vp_stored, f_stored, parts_stored = (m.pair(n) for n in ("xn_st", "vp_st", "f_st", "parts_st"))

        def unit_of(t, i, k):
            at = ds(i * T + k * UNIT, UNIT) if not isinstance(i, int) else slice(i * T + k * UNIT, i * T + (k + 1) * UNIT)
            return t[at, :].rearrange("(j p) d -> p j d", p=P)

        def ahead(i, k):
            return (i, 1) if k == 0 else (i + 1, 0)

        with nc.Block() as block:
            @block.sync
            def _(sp):
                sp.dma_start(wrow[:, 0:2, :], a["w_attn"].rearrange("(j p) d -> p j d", p=P)).then_inc(w_loaded, 16)
                sp.dma_start(wrow[:, 2, :], a["w_k2"]).then_inc(w_loaded, 16)
                sp.dma_start(brow[:, 0:2, :], a["b_attn"].rearrange("(o j p) -> o j p", o=1, p=P)).then_inc(w_loaded, 16)
                sp.dma_start(brow[:, 2, :], a["b_k2"].rearrange("(o p) -> o p", o=1)).then_inc(w_loaded, 16)
                for k in range(2):
                    sp.dma_start(x[k][:], a["x"][k * UNIT:(k + 1) * UNIT, :].rearrange("(j p) d -> p j d", p=P)).then_inc(x_loaded[k], 16)

                def stores(i, k, more):
                    sp.wait_ge(xn_ready[k], i * UPT + UPT)
                    sp.dma_start(unit_of(dram["xn"], i, k), xn[k][:]).then_inc(xn_stored[k], 16)
                    if more:
                        sp.dma_start(x[k][:], unit_of(a["x"], i + 1, k)).then_inc(x_loaded[k], 16)
                    sp.wait_ge(vp_ready[k], i + 1)
                    sp.dma_start(unit_of(dram["vp"], i, k), vp[k][:].rearrange("p j h d -> p j (h d)")).then_inc(vp_stored[k], 16)

                def store_parts(i, k):
                    for s in range(PARTS):
                        sp.wait_ge((part1, part2, part3)[s][k], i + 1)
                    sp.dma_start(dram["parts"][:, i, :, k * UNIT:(k + 1) * UNIT].rearrange("s p t -> p s t"),
                                 parts[k][:].rearrange("p q s t -> p (q s) t")).then_inc(parts_stored[k], 16)

                stores(0, 0, True)
                with sp.Fori(0, B - 2) as i:
                    for k in range(2):
                        stores(*ahead(i, k), True)
                        store_parts(i, k)
                for k in range(4):
                    if k < 3:
                        stores(*ahead(B - 2 + k // 2, k % 2), k == 0)
                    store_parts(B - 2 + k // 2, k % 2)
                for k in range(2):
                    sp.wait_ge(xn_stored[k], B * 16)
                    sp.wait_ge(vp_stored[k], B * 16)
                    sp.wait_ge(parts_stored[k], B * 16)

            @block.vector
            def _(dve):
                dve.wait_ge(w_loaded, 64)
                for j in range(3):
                    nc.vector.tensor_copy(bperm[:, j, :].rearrange("p (g d h) -> p g d h", g=GPB, h=GH),
                                          brow[:, j, :].rearrange("p (g h d) -> p g d h", g=GPB, h=GH)).then_inc(w_ready, 1)
                dve.wait_ge(w_turned, 1)
                nc.vector.tensor_copy(bias[:], psw[:, 3 * P:3 * P + 3]).then_inc(w_ready, 1)
                for j in range(3):
                    nc.vector.tensor_copy(wT[:, j, :].rearrange("p (g d h) -> p g d h", g=GPB, h=GH),
                                          psw[:, j * P:(j + 1) * P].rearrange("p (g h d) -> p g d h", g=GPB, h=GH)).then_inc(w_ready, 1)
                dve.wait_ge(w_ready, 7)
                nc.vector.tensor_scalar(sbias[:, 1:2], bias[:, 1:2], 1.0, None, ALU.mult).then_inc(bias_ready, 1)
                nc.vector.tensor_scalar(sbias[:, 0:1], bias[:, 0:1], SCALE, None, ALU.mult).then_inc(bias_ready, 1)
                nc.vector.tensor_scalar(sbias[:, 2:3], bias[:, 2:3], SCALE * 0.02, None, ALU.mult).then_inc(bias_ready, 1)

                def means(i, k):
                    dve.wait_ge(x_loaded[k], i * 16 + 16)
                    if k:
                        dve.wait_ge(mean[0], i * UPT + UPT)
                    else:
                        dve.wait_ge(mean[1], i * UPT)
                    for j in range(UPT):
                        nc.vector.bn_stats(stats[:, j, :], x[k][:, j, :]).then_inc(stat[k], 1)
                    dve.wait_ge(stat[k], i * UPT + UPT)
                    dve.sem_inc(passed, 1)
                    for j in range(UPT):
                        nc.vector.bn_aggr(mv[k][:, j, :], stats[:, j, :]).then_inc(mean[k], 1)

                def normalise(i, k):
                    dve.wait_ge(rstd_ready[k], i + 1)
                    dve.wait_ge(xT_made[k], i)
                    dve.wait_ge(vp_ready[k], i)
                    dve.wait_ge(xn_stored[k], i * 16)
                    for j in range(UPT):
                        nc.vector.tensor_scalar(xn[k][:, j, :], x[k][:, j, :], mv[k][:, j, 0:1], rstd[k][:, j:j + 1],
                                                ALU.subtract, ALU.mult).then_inc(xn_ready[k], 1)

                def split_first(i, k):
                    dve.wait_ge(q_ready[k], i + 1)
                    nc.vector.scalar_tensor_tensor(f[k][:, 2, :], f[k][:, 0, :], 0.02, f[k][:, 0, :],
                                                   ALU.mult, ALU.min).then_inc(qa_ready[k], 1)
                    dve.wait_ge(qa_ready[k], i + 1)
                    dve.wait_ge(k_ready[k], i + 1)
                    dve.wait_ge(ka_ready[k], i + 1)
                    dve.wait_ge(parts_stored[k], i * 16)
                    nc.vector.tensor_copy(parts[k][:, :, 0, :], f[k][:]).then_inc(part1[k], 1)
                    dve.wait_ge(part1[k], i + 1)
                    dve.wait_ge(part3[k], i)
                    nc.vector.tensor_tensor(r[k][:], f[k][:], parts[k][:, :, 0, :], ALU.subtract).then_inc(rest1[k], 1)

                for k in range(2):
                    means(0, k)
                normalise(0, 0)
                with dve.Fori(0, B - 1) as i:
                    for k in range(2):
                        normalise(*ahead(i, k))
                        means(i + 1, k)
                        split_first(i, k)
                normalise(B - 1, 1)
                for k in range(2):
                    split_first(B - 1, k)

            @block.tensor
            def _(pe):
                pe.wait_ge(w_loaded, 64)
                for j in range(3):
                    turned = nc.tensor.transpose(psw[:, j * P:(j + 1) * P], wrow[:, j, :], c["ident"][:])
                pe.wait_ge(w_ready, 3)
                for j in range(3):
                    turned = nc.tensor.matmul(psw[:, 3 * P + j:3 * P + j + 1],
                                              bperm[:, j, :],
                                              c["ident"][0:1, 0:1], start=True, stop=True)
                turned.then_inc(w_turned, 1)
                pe.wait_ge(w_ready, 7)
                with pe.Fori(0, B) as i:
                    for k in range(2):
                        pe.wait_ge(xn_ready[k], i * UPT + UPT)
                        pe.wait_ge(xT_ready[k], i)
                        for j in range(UPT):
                            turned = nc.tensor.transpose(psx[k][:, j * P:(j + 1) * P], xn[k][:, j, :], c["ident"][:])
                        turned.then_inc(xT_made[k], 1)
                        pe.wait_ge(xT_ready[k], i + 1)
                        pe.wait_ge(q_ready[1 - k], i + k)
                        pe.wait_ge(k_ready[1 - k], i + k)
                        pe.wait_ge(ka_ready[1 - k], i + k)
                        for j in range(3):
                            nc.tensor.matmul(psq[j][:], wT[:, j, :], xnT[k][:], start=True, stop=True).then_inc(mm_done[k], 1)

            @block.scalar
            def _(act):
                act.wait_ge(bias_ready, 3)
                act.wait_ge(ones_ready, 3)

                def turned(i, k):
                    act.wait_ge(xT_made[k], i + 1)
                    act.wait_ge(mm_done[k], i * 3)
                    nc.scalar.activation(xnT[k][:], psx[k][:], ACT.Copy).then_inc(xT_ready[k], 1)
                    act.wait_ge(vp_stored[k], i * 16)
                    nc.scalar.activation(vp[k][:, :, :, 0:HD].rearrange("p j h d -> p (j h) d"),
                                         xn[k][:].rearrange("p j (h d) -> p (j h) d", d=HD), ACT.Copy).then_inc(vp_ready[k], 1)

                def features(i, k):
                    act.wait_ge(rest1[k], i)
                    act.wait_ge(f_stored[k], i * 16)
                    act.wait_ge(mm_done[k], i * 3 + 1)
                    nc.scalar.activation(f[k][:, 0, :], psq[0][:], ACT.Identity, bias=sbias[:, 0:1], scale=SCALE).then_inc(q_ready[k], 1)
                    act.wait_ge(mm_done[k], i * 3 + 2)
                    nc.scalar.activation(f[k][:, 1, :], psq[1][:], ACT.Identity, bias=sbias[:, 1:2], scale=1.0).then_inc(k_ready[k], 1)
                    act.wait_ge(mm_done[k], i * 3 + 3)
                    nc.scalar.activation(f[k][:, 3, :], psq[2][:], ACT.Sigmoid, bias=sbias[:, 2:3], scale=SCALE * 0.02).then_inc(ka_ready[k], 1)

                def second_part(i, k):
                    act.wait_ge(rest1[k], i + 1)
                    nc.scalar.activation(parts[k][:, :, 1, :], r[k][:], ACT.Copy).then_inc(part2[k], 1)
                    act.wait_ge(qa_ready[k], i + 1)
                    act.wait_ge(ka_ready[k], i + 1)
                    act.dma_start(dram["fT"][:, :, (ds(i * T + k * UNIT, UNIT) if not isinstance(i, int) else slice(i * T + k * UNIT, i * T + (k + 1) * UNIT))].rearrange("q p t -> p q t"),
                                  f[k][:, 2:4, :]).then_inc(f_stored[k], 16)

                turned(0, 0)
                features(0, 0)
                with act.Fori(0, B - 1) as i:
                    for k in range(2):
                        turned(*ahead(i, k))
                        features(*ahead(i, k))
                        second_part(i, k)
                turned(B - 1, 1)
                features(B - 1, 1)
                for k in range(2):
                    second_part(B - 1, k)
                for k in range(2):
                    act.wait_ge(f_stored[k], B * 16)

            @block.gpsimd
            def _(pool):
                for k in range(2):
                    nc.gpsimd.memset(vp[k][:], 1.0).then_inc(ones_ready, 1)
                nc.gpsimd.memset(power[:], -0.5).then_inc(ones_ready, 1)
                pool.wait_ge(ones_ready, 3)

                def rstd_of(i, k):
                    pool.wait_ge(mean[k], i * UPT + UPT)
                    if not isinstance(i, int) or i + k:
                        pool.wait_ge(rstd_ready[1 - k], i + k)
                    pool.wait_ge(xn_ready[k], i * UPT)
                    pool.sem_inc(passed, 1)
                    nc.gpsimd.tensor_scalar(veps[:], mv[k][:, :, 1], EPS, 1.0, ALU.add, ALU.mult).then_inc(veps_ready[k], 1)
                    pool.wait_ge(veps_ready[k], i + 1)
                    nc.gpsimd.tensor_tensor(rstd[k][:], veps[:], power[:], ALU.pow).then_inc(rstd_ready[k], 1)

                def split_last(i, k):
                    pool.wait_ge(part2[k], i + 1)
                    nc.gpsimd.tensor_tensor(parts[k][:, :, 2, :], r[k][:], parts[k][:, :, 1, :], ALU.subtract).then_inc(part3[k], 1)

                for k in range(2):
                    rstd_of(0, k)
                with pool.Fori(0, B - 1) as i:
                    for k in range(2):
                        rstd_of(i + 1, k)
                        split_last(i, k)
                for k in range(2):
                    split_last(B - 1, k)
        m.clear()


QW = 512
UNITS = [(0, j) for j in range(4)] + [(1, j) for j in range(8)]
TILES = [(h, i) for h in range(GH) for i in range(BLK)]
TPG = len(TILES) + 1
UPG = len(UNITS)
ROW_START = 5
ROW_PACE = 34
TURN_AT = 10
STRIDES = sorted({1, 2, 16, 32, UPG, TPG, UPG * GH, PARTS * 16, PARTS * 16})


def attention(nc, dram, c):
    with ExitStack() as ctx:
        m = Mem(nc, ctx, "attn")
        qs = [m.sb(f"qs{k}", [P, GH, T], BF16) for k in range(2)]
        ks = [m.sb(f"ks{k}", [P, GH, T], BF16) for k in range(2)]
        vc = [m.sb(f"vc{k}", [P, BLK, GH * (HD + 1)]) for k in range(2)]
        vw = [m.sb(f"vw{k}", [P, BLK, GH, 32]) for k in range(2)]
        nm = m.sb("nm", [P, GH * BLK])
        nrest = m.sb("nrest", [P, GH * BLK])
        nparts = m.sb("nparts", [P, PARTS, GH * BLK], BF16)
        nrows = m.sb("nrows", [PARTS * GH * BLK, P], BF16)
        prob = [m.sb(f"prob{s}", [P, GH, QW]) for s in range(2)]
        o = [m.sb(f"o{ch}", [P, QW]) for ch in range(2)]
        rec = [m.sb(f"rec{ch}", [P, UPT * GH]) for ch in range(2)]
        y = [m.sb(f"y{ch}", [P, UPT, GH, HD]) for ch in range(2)]
        ps_rows = [m.ps(f"ps_rows{s}", [P, T]) for s in range(2)]
        ps_cols = [m.ps(f"ps_cols{s}", [P, QW]) for s in range(2)]
        ps_o = [m.ps(f"ps_o{ch}", [P, QW]) for ch in range(2)]
        filled, passed = m.sem("filled"), m.sem("passed")
        q_loaded, k_loaded, v_loaded, v_wide = (m.pair(n) for n in ("q_ld", "k_ld", "v_ld", "v_wide"))
        rows_done, rows_free = m.pair("rows_done"), m.pair("rows_free")
        split_a, split_b, split_c, split_d = (m.pair(n) for n in ("split_a", "split_b", "split_c", "split_d"))
        max_stored = m.pair("max_st")
        cols_done, prob_done, pv_done = m.pair("cols_done"), m.pair("prob_done"), m.pair("pv_done")
        o_ready, turned, rec_ready, y_ready, y_stored = (m.pair(n) for n in ("o_ready", "turned", "rec", "y_ready", "y_st"))

        vp = dram["vp"].rearrange("(b j p) (g n) -> b g p j n", b=B, p=P, n=GH * (HD + 1))
        split = [dram["parts"][q * PARTS:(q + 1) * PARTS].rearrange("s b (g d h) t -> (b g) s d (h t)", g=GPB, h=GH) for q in range(2)]
        yar = dram["yar"].rearrange("g (c j p) n -> g c p j n", c=2, p=P)

        def load(sp, i, k):
            sp.wait_ge(cols_done[k], i * UPG * GH)
            for s in range(PARTS):
                at = s * PARTS * HD
                sp.dma_start(qs[k][at:at + PARTS * HD],
                             split[0][i * 2 + k, s].unsqueeze(0).broadcast_to([PARTS, HD, GH * T])).then_inc(q_loaded[k], 16)
                sp.dma_start(ks[k][at:at + PARTS * HD], split[1][i * 2 + k]).then_inc(k_loaded[k], 16)
            sp.wait_ge(v_wide[k], i)
            sp.dma_start(vc[k][:], vp[i // 2, (i % 2) * 2 + k]).then_inc(v_loaded[k], 16)

        def store_max(sp, i, k):
            sp.wait_ge(rows_free[k], (i + 1) * TPG)
            sp.dma_start(qs[k][MROW:MROW + PARTS].rearrange("s h (j t) -> s (h j) t", t=P), nrows[:]).then_inc(max_stored[k], 16)

        def store_y(sp, i, k, ch):
            sp.wait_ge(y_ready[ch], i * 2 + k + 1)
            sp.dma_start(yar[i * 2 + k, ch], y[ch][:].rearrange("p j h d -> p j (h d)")).then_inc(y_stored[ch], 16)

        def row_tile(i, k, n):
            pe = nc.tensor
            if n == 0:
                pe.wait_ge(q_loaded[k], now((i + 1) * PARTS * 16))
                pe.wait_ge(k_loaded[k], now((i + 1) * PARTS * 16))
                pe.wait_ge(rows_free[1 - k], now((i + k) * TPG))
            if n >= 2:
                pe.wait_ge(rows_free[k], now(i * TPG + n - 1))
            h, blk = TILES[n]
            out = ps_rows[n % 2]
            for at in range(0, (blk + 1) * P, QW):
                to = min(at + QW, (blk + 1) * P)
                last = to == (blk + 1) * P
                done = nc.tensor.matmul(out[:, at:to], qs[k][0:KROWS, h, blk * P:(blk + 1) * P], ks[k][0:KROWS, h, at:to],
                                        start=True, stop=not last)
            done = nc.tensor.matmul(out[:, blk * P:(blk + 1) * P], c["identb"][:], c["mask_rows"][:], start=False, stop=True)
            done.then_inc(rows_done[k], 1)

        def turn_max(i, k):
            nc.tensor.wait_ge(split_d[k], now(i + 1))
            nc.tensor.wait_ge(rows_free[k], now(i * TPG + TPG - 1))
            nc.tensor.transpose(turned_max, nparts[:].rearrange("p s n -> p (s n)"), c["identb"][:]).then_inc(rows_done[k], 1)

        def rows_of(ch, j):
            at = max(j * P, ch * QW)
            return at, (ch + 1) * QW - at

        def col_tile(i, k, u, h):
            ch, j = UNITS[u]
            at, w = rows_of(ch, j)
            q = u * GH + h
            if q == 0:
                nc.tensor.wait_ge(max_stored[k], now((i + 1) * 16))
                nc.tensor.wait_ge(prob_done[1 - k], now((i + k) * UPG * GH))
            if q >= 2:
                nc.tensor.wait_ge(prob_done[k], now(i * UPG * GH + q - 1))
            diagonal = at == j * P
            out = ps_cols[q % 2]
            done = nc.tensor.matmul(out[:, 0:w], ks[k][0:MROW + PARTS, h, j * P:(j + 1) * P],
                                    qs[k][0:MROW + PARTS, h, at:at + w], start=True, stop=not diagonal)
            if diagonal:
                done = nc.tensor.matmul(out[:, 0:P], c["identb"][:], c["mask_cols"][:], start=False, stop=True)
            done.then_inc(cols_done[k], 1)

        def weighted(i, k, u):
            ch, j = UNITS[u]
            at, w = rows_of(ch, j)
            if u == 0:
                nc.tensor.wait_ge(v_wide[k], now(i + 1))
            if j == 0:
                nc.tensor.wait_ge(y_ready[ch], now(i * 2 + k))
            nc.tensor.wait_ge(prob_done[k], now(i * UPG * GH + (u + 1) * GH))
            last = (ch, j + 1) not in UNITS
            for h in range(GH):
                done = nc.tensor.matmul(ps_o[ch][32 * h:32 * h + 32, at - ch * QW:at - ch * QW + w], vw[k][:, j, h, :],
                                        prob[u % 2][:, h, 0:w], start=j == 0, stop=last)
            done.then_inc(pv_done[k], 1)

        def turn(i, k, ch):
            nc.tensor.wait_ge(o_ready[ch], now(i * 2 + k + 1))
            for b in range(UPT):
                done = nc.tensor.transpose(ps_o[ch][:, b * P:(b + 1) * P], o[ch][:, b * P:(b + 1) * P], c["ident"][:])
            done.then_inc(turned[ch], 1)

        def max_tile(i, k, n):
            if n == 0:
                nc.vector.wait_ge(split_d[1 - k], now(i + k))
            nc.vector.wait_ge(rows_done[k], now(i * TPG + n + 1))
            h, blk = TILES[n]
            nc.vector.tensor_reduce(nm[:, n:n + 1], ps_rows[n % 2][:, 0:(blk + 1) * P], AX.X, ALU.max,
                                    negate=True).then_inc(rows_free[k], 1)

        def split_max(dve, i, k):
            dve.wait_ge(rows_free[k], now(i * TPG + TPG - 1))
            nc.vector.tensor_copy(nparts[:, 0, :], nm[:]).then_inc(split_a[k], 1)
            dve.wait_ge(split_a[k], now(i + 1))
            nc.vector.tensor_tensor(nrest[:], nm[:], nparts[:, 0, :], ALU.subtract).then_inc(split_b[k], 1)
            dve.wait_ge(split_b[k], now(i + 1))
            nc.vector.tensor_copy(nparts[:, 1, :], nrest[:]).then_inc(split_c[k], 1)
            dve.wait_ge(split_c[k], now(i + 1))
            nc.vector.tensor_tensor(nparts[:, 2, :], nrest[:], nparts[:, 1, :], ALU.subtract).then_inc(split_d[k], 1)

        def keep_max(dve, i, k):
            dve.wait_ge(rows_done[k], now((i + 1) * TPG))
            dve.wait_ge(max_stored[1 - k], now((i + k) * 16))
            nc.vector.tensor_copy(nrows[:], turned_max).then_inc(rows_free[k], 1)

        def divide(dve, i, k, ch):
            by_row = ps_o[ch][:].rearrange("p (n d) -> p n d", d=32)
            dve.wait_ge(turned[ch], now(i * 2 + k + 1))
            nc.vector.reciprocal(rec[ch][:], by_row[:, :, HD]).then_inc(rec_ready[ch], 1)
            dve.wait_ge(rec_ready[ch], now(i * 2 + k + 1))
            dve.wait_ge(y_stored[ch], now((i * 2 + k) * 16))
            nc.vector.tensor_tensor(y[ch][:].rearrange("p j h d -> p (j h) d"), by_row[:, :, 0:HD],
                                    rec[ch][:].unsqueeze(2).broadcast_to([P, UPT * GH, HD]), ALU.mult).then_inc(y_ready[ch], 1)

        def pe_group(i, k, more):
            ni, nk = (i, 1) if k == 0 else (i + 1, 0)
            n = 0
            for u in range(UPG):
                for h in range(GH):
                    col_tile(i, k, u, h)
                    q = u * GH + h
                    while more and n < len(TILES) and n * ROW_PACE <= (q - ROW_START) * len(TILES):
                        row_tile(ni, nk, n)
                        n += 1
                if u > 0:
                    weighted(i, k, u - 1)
                if u == 6:
                    turn(i, k, 0)
                if more and u == TURN_AT:
                    turn_max(ni, nk)
            weighted(i, k, UPG - 1)
            turn(i, k, 1)

        def dve_group(dve, i, k, more):
            ni, nk = (i, 1) if k == 0 else (i + 1, 0)
            n = 0
            for u in range(UPG):
                for h in range(GH):
                    q = u * GH + h
                    while more and n < len(TILES) and n * ROW_PACE <= (q - ROW_START) * len(TILES):
                        max_tile(ni, nk, n)
                        n += 1
                        if n == len(TILES):
                            split_max(dve, ni, nk)
                if u == 6:
                    divide(dve, i, k, 0)
                if more and u == TURN_AT:
                    keep_max(dve, ni, nk)
            divide(dve, i, k, 1)

        def act_group(act, i, k):
            for u in range(UPG):
                ch, j = UNITS[u]
                w = rows_of(ch, j)[1]
                if u < 2:
                    act.wait_ge(pv_done[1 - k], now((i + k) * UPG))
                else:
                    act.wait_ge(pv_done[k], now(i * UPG + u - 1))
                for h in range(GH):
                    act.wait_ge(cols_done[k], now(i * UPG * GH + u * GH + h + 1))
                    nc.scalar.activation(prob[u % 2][:, h, 0:w], ps_cols[(u * GH + h) % 2][:, 0:w], ACT.Exp).then_inc(prob_done[k], 1)
                if u == 5:
                    keep_o(act, i, k, 0)
            keep_o(act, i, k, 1)

        def keep_o(act, i, k, ch):
            act.wait_ge(pv_done[k], now(i * UPG + (4 if ch == 0 else UPG)))
            act.wait_ge(turned[ch], now(i * 2 + k))
            nc.scalar.activation(o[ch][:], ps_o[ch][:], ACT.Copy).then_inc(o_ready[ch], 1)

        def sp_group(sp, i, k, more, load_more):
            ni, nk = (i, 1) if k == 0 else (i + 1, 0)
            store_y(sp, i, k, 0)
            if more:
                store_max(sp, ni, nk)
            if load_more:
                load(sp, i + 1, k)
            store_y(sp, i, k, 1)

        turned_max = ps_rows[0][:].bitcast(BF16)[0:PARTS * GH * BLK, 0:P]
        last = GROUPS // 2 - 1
        with nc.Block() as block:
            @block.sync
            def _(sp):
                sp.wait_ge(filled, 8)
                load(sp, 0, 0)
                load(sp, 0, 1)
                store_max(sp, 0, 0)
                with sp.Fori(0, last) as i:
                    for k in range(2):
                        sp_group(sp, i, k, True, True)
                for k in range(2):
                    sp_group(sp, last, k, k == 0, False)
                for ch in range(2):
                    sp.wait_ge(y_stored[ch], GROUPS * 16)

            @block.tensor
            def _(pe):
                pe.wait_ge(filled, 8)
                for n in range(len(TILES)):
                    row_tile(0, 0, n)
                turn_max(0, 0)
                turns = Turns(pe, "attn_pe", STRIDES)
                with pe.Fori(0, last) as turn:
                    i = Linear(turns, turn)
                    for k in range(2):
                        pe_group(i, k, True)
                    turns.step()
                for k in range(2):
                    pe_group(last, k, k == 0)

            @block.vector
            def _(dve):
                for k in range(2):
                    nc.vector.memset(qs[k][P // 2:P], 0.0).then_inc(filled, 1)
                    nc.vector.memset(ks[k][P // 2:P], 0.0).then_inc(filled, 1)
                    nc.vector.memset(vw[k][:], 0.0).then_inc(filled, 1)
                dve.wait_ge(filled, 6)
                for k in range(2):
                    nc.vector.memset(ks[k][MROW:P], 1.0).then_inc(filled, 1)
                for n in range(len(TILES)):
                    max_tile(0, 0, n)
                split_max(dve, 0, 0)
                keep_max(dve, 0, 0)
                turns = Turns(dve, "attn_dve", STRIDES)
                with dve.Fori(0, last) as turn:
                    i = Linear(turns, turn)
                    for k in range(2):
                        dve_group(dve, i, k, True)
                    turns.step()
                for k in range(2):
                    dve_group(dve, last, k, k == 0)

            @block.scalar
            def _(act):
                turns = Turns(act, "attn_act", STRIDES)
                with act.Fori(0, last + 1) as turn:
                    i = Linear(turns, turn)
                    for k in range(2):
                        act_group(act, i, k)
                    turns.step()

            @block.gpsimd
            def _(pool):
                pool.wait_ge(filled, 8)
                with pool.Fori(0, last + 1) as i:
                    for k in range(2):
                        pool.wait_ge(v_loaded[k], i * 16 + 16)
                        pool.wait_ge(pv_done[k], i * UPG)
                        pool.sem_inc(passed, 1)
                        nc.gpsimd.tensor_copy(vw[k][:, :, :, 0:HD + 1].rearrange("p j h n -> p (j h) n"),
                                              vc[k][:].rearrange("p j (h n) -> p (j h) n", h=GH)).then_inc(v_wide[k], 1)
        m.clear()


HALF = BLK // 2
MEM_STRIDES = sorted({1, 2, 7, 8, 16, 32, 64, 2 * PARTS * 16, 2 * PARTS * 16})


def memory(nc, dram, c, a):
    with ExitStack() as ctx:
        m = Mem(nc, ctx, "mem")
        wrow, wT, wpad = m.sb("wrow", [P, P]), m.sb("wT", [P, P]), m.sb("wpad", [P, GPB, P])
        brow, bias2 = m.sb("brow", [P, P]), m.sb("bias2", [P, P])
        qs = [m.sb(f"qs{k}", [KROWS, GH, T], BF16) for k in range(2)]
        ks = [m.sb(f"ks{k}", [KROWS, GH, T], BF16) for k in range(2)]
        yt, vs, e = m.sb("yt", [P, BLK, D]), m.sb("vs", [P, BLK, D]), m.sb("e", [P, BLK, D])
        kaT, qaT, ka = m.sb("kaT", [P, T]), m.sb("qaT", [P, T]), m.sb("ka", [P, BLK, P])
        yT = m.sb("yT", [P, T])
        x, xb, x1 = m.sb("x", [P, BLK, D]), m.sb("xb", [P, BLK, D]), m.sb("x1", [P, BLK, D])
        state = m.sb("state", [P, BLK, HEADS, 32])
        am = [m.sb(f"am{s}", [P, GH, P]) for s in range(2)]
        ymT = m.sb("ymT", [P, GPB, T])
        ps_t, ps_state, ps_p = m.ps("ps_t", [P, T]), m.ps("ps_state", [P, P]), m.ps("ps_p", [P, HALF, P])
        ps_a = [m.ps(f"ps_a{s}", [P, GH, P]) for s in range(2)]
        ps_y = [m.ps(f"ps_y{s}", [P, HALF, P]) for s in range(2)]
        w_loaded, w_turned, w_ready, w_spread, filled = (m.sem(n) for n in ("w_ld", "w_turned", "w_ready", "w_spread", "filled"))
        bias_ready = m.sem("bias_ready")
        y_loaded, v_loaded, ka_loaded, qa_loaded, x_loaded = (m.sem(n) for n in ("y_ld", "v_ld", "ka_ld", "qa_ld", "x_ld"))
        qs_loaded, ks_loaded = m.pair("qs_ld"), m.pair("ks_ld")
        e_ready, ka_turned, ka_ready, y_turned, yT_ready = (m.sem(n) for n in ("e_ready", "ka_turned", "ka_ready", "y_turned", "yT_ready"))
        state_done, state_ready = m.sem("state_done"), m.sem("state_ready")
        a_done, a_ready, y_done, ym_ready = (m.sem(n) for n in ("a_done", "a_ready", "y_done", "ym_ready"))
        p_done, xb_ready, x1_ready, x1_stored, passed = (m.sem(n) for n in ("p_done", "xb_ready", "x1_ready", "x1_st", "passed"))
        split = [dram["parts"][q * PARTS:(q + 1) * PARTS].rearrange("s b (g d h) t -> (b g) s d (h t)", g=GPB, h=GH) for q in (2, 3)]
        yar = dram["yar"].rearrange("(b g) (j p) n -> b g p j n", b=B, p=P)

        def load_stack(sp, i, hg):
            k = hg % 2
            sp.wait_ge(a_done, i * 32 + (hg - 1) * 8 if hg >= 2 else i * 32)
            for s in range(PARTS):
                at = s * PARTS * HD
                sp.dma_start(qs[k][at:at + PARTS * HD],
                             split[0][i * GPB + hg, s].unsqueeze(0).broadcast_to([PARTS, HD, GH * T])).then_inc(qs_loaded[k], 16)
                sp.dma_start(ks[k][at:at + PARTS * HD], split[1][i * GPB + hg]).then_inc(ks_loaded[k], 16)

        def products(i, hg, b):
            t, k = hg * BLK + b, hg % 2
            if b == 0:
                nc.tensor.wait_ge(qs_loaded[k], now(i * (2 * PARTS * 16) + (hg // 2 + 1) * PARTS * 16))
                nc.tensor.wait_ge(ks_loaded[k], now(i * (2 * PARTS * 16) + (hg // 2 + 1) * PARTS * 16))
            nc.tensor.wait_ge(a_ready, now(i * 32 + t - 1) if t else now(i * 32))
            for h in range(GH):
                done = nc.tensor.matmul(ps_a[t % 2][:, h, :], ks[k][:, h, b * P:(b + 1) * P], qs[k][:, h, b * P:(b + 1) * P],
                                        start=True, stop=True)
            done.then_inc(a_done, 1)

        def outputs(i, hg, b):
            t, half = hg * BLK + b, b // HALF
            out = ps_y[half][:, b % HALF, :]
            if b % HALF == 0:
                if hg:
                    nc.tensor.wait_ge(ym_ready, now(i * 8 + hg * 2 - 1 + half))
                else:
                    nc.tensor.wait_ge(ym_ready, now(i * 8))
            if hg == 0 and b:
                nc.tensor.wait_ge(state_ready, now(i * 7 + b))
            nc.tensor.matmul(out, state[:, b, hg * GH:(hg + 1) * GH, :].rearrange("p h n -> p (h n)"), qaT[:, b * P:(b + 1) * P],
                             start=True, stop=False)
            nc.tensor.wait_ge(a_ready, now(i * 32 + t + 1))
            for h in range(GH):
                at = (hg * GH + h) * HD
                done = nc.tensor.matmul(out[32 * h:32 * h + HD], e[:, b, at:at + HD], am[t % 2][:, h, :], start=False, stop=True)
            done.then_inc(y_done, 1)

        def add_state(i, b):
            if b == 0:
                nc.tensor.wait_ge(e_ready, now(i * 1 + 1))
                nc.tensor.wait_ge(ka_ready, now(i * 1 + 1))
            nc.tensor.wait_ge(state_ready, now(i * 7 + b))
            nc.tensor.matmul(ps_state[:], ka[:, b, :], e[:, b, :], start=b == 0, stop=True,
                             skip_group_check=b > 0).then_inc(state_done, 1)

        with nc.Block() as block:
            @block.sync
            def _(sp):
                sp.dma_start(wrow[:], a["w_proj"]).then_inc(w_loaded, 16)
                sp.dma_start(brow[:], a["b_proj"].rearrange("(o n) -> o n", o=1).broadcast_to([P, P])).then_inc(w_loaded, 16)
                with sp.Fori(0, B) as i:
                    sp.wait_ge(ka_turned, i)
                    sp.dma_start(kaT[:], dram["fT"][1, :, ds(i * T, T)]).then_inc(ka_loaded, 16)
                    sp.wait_ge(e_ready, i)
                    sp.sem_inc(passed, 1)
                    sp.dma_start(vs[:], dram["xn"][ds(i * T + 1, T), :].rearrange("(j p) d -> p j d", p=P)).then_inc(v_loaded, 16)
                    sp.wait_ge(y_turned, i)
                    for g in range(GPB):
                        sp.dma_start(yt[:, :, g * GH * HD:(g + 1) * GH * HD], yar[i, g]).then_inc(y_loaded, 16)
                    sp.wait_ge(y_done, i * 32)
                    sp.sem_inc(passed, 1)
                    sp.dma_start(qaT[:], dram["fT"][0, :, ds(i * T, T)]).then_inc(qa_loaded, 16)
                    load_stack(sp, i, 0)
                    load_stack(sp, i, 1)
                    sp.wait_ge(xb_ready, i)
                    sp.dma_start(x[:], a["x"][ds(i * T, T), :].rearrange("(j p) d -> p j d", p=P)).then_inc(x_loaded, 16)
                    load_stack(sp, i, 2)
                    load_stack(sp, i, 3)

            @block.tensor
            def _(pe):
                pe.wait_ge(w_loaded, 32)
                nc.tensor.transpose(ps_t[:, 0:P], wrow[:], c["ident"][:]).then_inc(w_turned, 1)
                pe.wait_ge(w_ready, 1)
                pe.wait_ge(filled, 2)
                turns = Turns(pe, "mem_pe", MEM_STRIDES)
                with pe.Fori(0, B) as turn:
                    i = Linear(turns, turn)
                    pe.wait_ge(ka_loaded, now(i * 16 + 16))
                    pe.wait_ge(yT_ready, now(i * 1))
                    for b in range(BLK):
                        done = nc.tensor.transpose(ps_t[:, b * P:(b + 1) * P], kaT[:, b * P:(b + 1) * P], c["ident"][:])
                    done.then_inc(ka_turned, 1)
                    pe.wait_ge(qa_loaded, now(i * 16 + 16))
                    for t in range(GPB * BLK):
                        products(i, t // BLK, t % BLK)
                        if t < BLK - 1:
                            add_state(i, t)
                        if t == 0:
                            pe.wait_ge(y_loaded, now(i * 64 + 64))
                            for b in range(BLK):
                                done = nc.tensor.transpose(ps_t[:, b * P:(b + 1) * P], yt[:, b, :], c["ident"][:])
                            done.then_inc(y_turned, 1)
                        if t:
                            outputs(i, (t - 1) // BLK, (t - 1) % BLK)
                    outputs(i, GPB - 1, BLK - 1)
                    pe.wait_ge(yT_ready, now(i * 1 + 1))
                    pe.wait_ge(w_spread, HEADS * 16)
                    for half in range(2):
                        pe.wait_ge(ym_ready, now(i * 8 + 7 + half))
                        pe.wait_ge(x1_ready, now(i * 2 + half))
                        for b in range(half * HALF, (half + 1) * HALF):
                            out = ps_p[:, b % HALF, :]
                            nc.tensor.matmul(out, yT[:, b * P:(b + 1) * P], wT[:], start=True, stop=False)
                            for hg in range(GPB):
                                done = nc.tensor.matmul(out, ymT[:, hg, b * P:(b + 1) * P], wpad[:, hg, :], start=False, stop=hg == GPB - 1)
                        done.then_inc(p_done, 1)
                    turns.step()

            @block.vector
            def _(dve):
                nc.vector.memset(wpad[:], 0.0).then_inc(filled, 1)
                nc.vector.memset(state[:], 0.0).then_inc(filled, 1)
                dve.wait_ge(w_turned, 1)
                nc.vector.tensor_copy(wT[:], ps_t[:, 0:P]).then_inc(w_ready, 1)
                dve.wait_ge(w_loaded, 32)
                nc.vector.tensor_scalar(bias2[:], brow[:], 2.0, None, ALU.mult).then_inc(bias_ready, 1)
                dve.wait_ge(filled, 2)
                turns = Turns(dve, "mem_dve", MEM_STRIDES)
                with dve.Fori(0, B) as turn:
                    i = Linear(turns, turn)
                    dve.wait_ge(v_loaded, now(i * 16 + 16))
                    dve.wait_ge(y_loaded, now(i * 64 + 64))
                    dve.wait_ge(y_done, now(i * 32))
                    nc.vector.tensor_tensor(e[:], vs[:], yt[:], ALU.subtract).then_inc(e_ready, 1)
                    for t in range(GPB * BLK):
                        dve.wait_ge(a_done, now(i * 32 + t + 1))
                        if t >= 2:
                            dve.wait_ge(y_done, now(i * 32 + t - 1))
                        nc.vector.tensor_tensor(am[t % 2][:], ps_a[t % 2][:], c["strict"][:], ALU.mult).then_inc(a_ready, 1)
                        if t < BLK - 1:
                            dve.wait_ge(state_done, now(i * 7 + t + 1))
                            nc.vector.tensor_tensor(state[:, t + 1, :, 0:HD], ps_state[:].rearrange("p (h d) -> p h d", d=HD),
                                                    c["same_head"][:].rearrange("p (h d) -> p h d", d=HD), ALU.mult).then_inc(state_ready, 1)
                    for half in range(2):
                        dve.wait_ge(p_done, now(i * 2 + half + 1))
                        dve.wait_ge(xb_ready, now(i * 1 + 1))
                        dve.wait_ge(x1_stored, now(i * 32 + half * 16))
                        nc.vector.tensor_tensor(x1[:, half * HALF:(half + 1) * HALF, :], ps_p[:], xb[:, half * HALF:(half + 1) * HALF, :],
                                                ALU.add).then_inc(x1_ready, 1)
                    turns.step()

            @block.scalar
            def _(act):
                def batch(i, turn):
                    act.wait_ge(ka_turned, now(i * 1 + 1))
                    act.wait_ge(state_done, now(i * 7))
                    nc.scalar.activation(ka[:].rearrange("p j n -> p (j n)"), ps_t[:], ACT.Copy).then_inc(ka_ready, 1)
                    act.wait_ge(y_turned, now(i * 1 + 1))
                    act.wait_ge(p_done, now(i * 2))
                    nc.scalar.activation(yT[:], ps_t[:], ACT.Copy).then_inc(yT_ready, 1)
                    if isinstance(i, int):
                        act.wait_ge(w_ready, 1)
                        act.wait_ge(filled, 2)
                        for h in range(HEADS):
                            at = 32 * (h % GH)
                            act.dma_start(wpad[at:at + HD, h // GH, :], wT[h * HD:(h + 1) * HD, :]).then_inc(w_spread, 16)
                    for hg in range(GPB):
                        for half in range(2):
                            act.wait_ge(y_done, now(i * 32 + (hg * BLK + (half + 1) * HALF)))
                            nc.scalar.activation(ymT[:, hg, half * HALF * P:(half + 1) * HALF * P],
                                                 ps_y[half][:].rearrange("p j n -> p (j n)"), ACT.Copy).then_inc(ym_ready, 1)
                    for half in range(2):
                        at = turn * T + half * HALF * P
                        act.wait_ge(x1_ready, now(i * 2 + (half + 1)))
                        act.dma_start(dram["x1"][slice(at, at + HALF * P) if isinstance(at, int) else ds(at, HALF * P), :].rearrange("(j p) d -> p j d", p=P),
                                      x1[:, half * HALF:(half + 1) * HALF, :]).then_inc(x1_stored, 16)

                batch(0, 0)
                turns = Turns(act, "mem_act", MEM_STRIDES, first=1)
                with act.Fori(1, B) as turn:
                    batch(Linear(turns, turn), turn)
                    turns.step()
                act.wait_ge(x1_stored, B * 32)

            @block.gpsimd
            def _(pool):
                pool.wait_ge(bias_ready, 1)
                with pool.Fori(0, B) as i:
                    pool.wait_ge(x_loaded, i * 16 + 16)
                    pool.wait_ge(x1_ready, i * 2)
                    nc.gpsimd.tensor_tensor(xb[:], x[:], bias2[:].unsqueeze(1).broadcast_to([P, BLK, P]), ALU.add).then_inc(xb_ready, 1)
        m.clear()


EXPERTS, HIDDEN, TOP = 8, 256, 2
HC = HIDDEN // P
TILES_IN = N // P
SUB = 2
ROWS = SUB * P
TILES_EX = TOP * N // ROWS + EXPERTS
REGION = N + ROWS
EW = 2 * HIDDEN + HC * D
IDLE = EXPERTS * REGION
ROWS_EX = IDLE + ROWS
AHEAD = 4
ROUTE_STRIDES = [2, 4, 8, 16, 32, 128]
EXPERT_STRIDES = [AHEAD, 16]
JOIN_STRIDES = [4, 16, 32, 128]


def unit_no(i, k):
    return slice(i * 2 + k, i * 2 + k + 1) if isinstance(i, int) else ds(i * 2 + k, 1)


def past(s, n):
    return not isinstance(s, int) or s >= n


def ffn(nc, dram, c, a, stage, src, dst):
    with ExitStack() as ctx:
        m = Mem(nc, ctx, stage)
        w = m.sb("w", [P, EXPERTS, EW])
        count = m.sb("count", [P, EXPERTS])
        choice = m.sb("choice", [P, 2 * B * TOP * UPT])
        t = table_memory(m)
        w_loaded = m.sem("w_ld")
        route(nc, dram, c, a, stage + "r", src, w, w_loaded, count, choice, t)
        run_experts(nc, dram, c, stage + "e", w, w_loaded, count, choice, t)
        m.clear()
    join(nc, dram, stage + "j", dst)


def route(nc, dram, c, a, stage, src, w, w_loaded, count, choice, t):
    with ExitStack() as ctx:
        m = Mem(nc, ctx, stage)
        sw1, sw3 = m.sb("sw1", [P, 2, HIDDEN]), m.sb("sw3", [P, HC, D])
        rw, rb = m.sb("rw", [P, EXPERTS]), m.sb("rb", [P, EXPERTS])
        ones, before = m.sb("ones", [P, P], BF16), m.sb("before", [P, P], BF16)
        x = [m.sb(f"x{k}", [P, UPT, D]) for k in range(2)]
        xr = [m.sb(f"xr{k}", [P, UPT, D]) for k in range(2)]
        stats, mv = m.sb("stats", [P, UPT, 6]), [m.sb(f"mv{k}", [P, UPT, 2]) for k in range(2)]
        veps, power, rstd = m.sb("veps", [P, UPT]), m.sb("power", [P, UPT]), [m.sb(f"rstd{k}", [P, UPT]) for k in range(2)]
        xn = [m.sb(f"xn{k}", [P, UPT, D]) for k in range(2)]
        xnT = [m.sb(f"xnT{k}", [P, UNIT]) for k in range(2)]
        logits, top = m.sb("logits", [P, UPT, EXPERTS]), m.sb("top", [P, UPT, EXPERTS])
        index, order = m.sb("index", [P, UPT, EXPERTS], mybir.dt.uint32), m.sb("order", [P, UPT, EXPERTS])
        number = m.sb("number", [P, UPT, EXPERTS])
        region = m.sb("region", [P, EXPERTS])
        gap, gate = m.sb("gap", [P, TOP, UPT]), [m.sb(f"gate{k}", [P, TOP, UPT]) for k in range(2)]
        tanh = m.sb("tanh", [P, TOP, UPT])
        pick = m.sb("pick", [P, TOP, UPT, EXPERTS])
        chosen = m.sb("chosen", [P, UPT + 1, EXPERTS], BF16)
        row, rows = m.sb("row", [P, UPT, EXPERTS]), m.sb("rows", [P, TOP, UPT, EXPERTS])
        rowf, pos = m.sb("rowf", [P, TOP, UPT]), [m.sb(f"pos{k}", [P, TOP, UPT], I32) for k in range(2)]
        act1 = [m.sb(f"act{h}", [P, UNIT]) for h in range(HC)]
        hid = [m.sb(f"hid{h}", [P, UNIT]) for h in range(HC)]
        base = [m.sb(f"base{k}", [P, UPT, D]) for k in range(2)]
        zeros = m.sb("zeros", [P, SUB, D])
        counti = m.sb("counti", [1, EXPERTS], I32)
        ps_x, ps_r = m.ps("ps_x", [P, UNIT]), m.ps("ps_r", [P, UPT, EXPERTS])
        ps_k = m.ps("ps_k", [P, UPT + 1, EXPERTS])
        ps_h = [[m.ps(f"ps_h{w}{h}", [P, UNIT]) for h in range(HC)] for w in range(2)]
        ps_o = m.ps("ps_o", [P, UPT, D])
        s_loaded, ready, passed, counted = m.sem("s_ld"), m.sem("ready"), m.sem("passed"), m.sem("counted")
        x_loaded, xr_loaded, xT_made, stored = m.pair("x_ld"), m.pair("xr_ld"), m.sem("xT_made"), m.pair("stored")
        stat, mean, veps_ready, rstd_ready, xn_ready = (m.sem(n) for n in ("stat", "mean", "veps", "rstd", "xn"))
        xT_ready, r_done, logits_ready, top_ready, index_ready, order_ready = (m.sem(n) for n in ("xT", "r_done", "logits", "top", "index", "order"))
        gap_ready, tanh_ready, gate_ready, pick_ready, chosen_ready = (m.sem(n) for n in ("gap", "tanh", "gate", "pick", "chosen"))
        ranked, row_ready, rows_ready, rowf_ready, pos_ready, count_ready = (m.sem(n) for n in ("ranked", "row", "rows", "rowf", "pos", "count"))
        h_done, act_ready, hid_ready, o_done, base_ready = (m.sem(n) for n in ("h_done", "act", "hid", "o_done", "base"))
        pads_stored, choice_ready = m.sem("pads"), m.sem("choice")
        made, step_dve, tabled = m.sem("made"), m.sem("step_dve"), m.sem("tabled")
        scattered = dram[stage + "_sent"]

        def unit_of(t, i, k):
            at = ds(i * T + k * UNIT, UNIT) if not isinstance(i, int) else slice(i * T + k * UNIT, i * T + (k + 1) * UNIT)
            return t[at, :].rearrange("(j p) d -> p j d", p=P)

        def ahead(i, k):
            return (i, 1) if k == 0 else (i + 1, 0)

        def mean_dve(dve, i, k):
            u = i * 2 + k
            dve.wait_ge(x_loaded[k], now(i * 16 + 16))
            dve.wait_ge(mean, now(u * UPT))
            for j in range(UPT):
                nc.vector.bn_stats(stats[:, j, :], x[k][:, j, :]).then_inc(stat, 1)
            dve.wait_ge(stat, now(u * UPT + UPT))
            dve.sem_inc(passed, 1)
            for j in range(UPT):
                nc.vector.bn_aggr(mv[k][:, j, :], stats[:, j, :]).then_inc(mean, 1)

        def norm_dve(dve, i, k):
            u = i * 2 + k
            dve.wait_ge(rstd_ready, now(u + 1))
            dve.wait_ge(scattered[k], now(i * 128))
            dve.wait_ge(xT_made, now(u * 1))
            for j in range(UPT):
                nc.vector.tensor_scalar(xn[k][:, j, :], x[k][:, j, :], mv[k][:, j, 0:1], rstd[k][:, j:j + 1],
                                        ALU.subtract, ALU.mult).then_inc(xn_ready, 1)

        def choose_dve(dve, i, k):
            u = i * 2 + k
            dve.wait_ge(r_done, now(u + 1))
            nc.vector.tensor_tensor(logits[:], ps_r[:], rb[:].unsqueeze(1).broadcast_to([P, UPT, EXPERTS]), ALU.add).then_inc(logits_ready, 1)
            dve.wait_ge(logits_ready, now(u + 1))
            dve.sem_inc(passed, 1)
            for j in range(UPT):
                nc.vector.max(top[:, j, :], logits[:, j, :]).then_inc(top_ready, 1)
            dve.wait_ge(top_ready, now(u * UPT + UPT))
            dve.sem_inc(passed, 1)
            for j in range(UPT):
                nc.vector.max_index(index[:, j, :], top[:, j, :], logits[:, j, :]).then_inc(index_ready, 1)
            dve.wait_ge(tanh_ready, now(u * 1))
            for n in range(TOP):
                nc.vector.tensor_tensor(gap[:, n, :], top[:, :, n], top[:, :, 1 - n], ALU.subtract).then_inc(gap_ready, 1)
            dve.wait_ge(index_ready, now(u * UPT + UPT))
            nc.vector.tensor_copy(order[:], index[:]).then_inc(order_ready, 1)
            dve.wait_ge(order_ready, now(u + 1))
            dve.wait_ge(chosen_ready, now(u * 1))
            for n in range(TOP):
                nc.vector.tensor_tensor(pick[:, n], number[:], order[:, :, n:n + 1].broadcast_to([P, UPT, EXPERTS]), ALU.is_equal).then_inc(pick_ready, 1)
            dve.wait_ge(pick_ready, now(u * 2 + 2))
            dve.wait_ge(ranked, now(u * 1))
            nc.vector.tensor_tensor(chosen[:, 0:UPT, :], pick[:, 0], pick[:, 1], ALU.add).then_inc(chosen_ready, 1)

        def place_dve(dve, i, k, turn):
            u = i * 2 + k
            dve.wait_ge(tanh_ready, now(u + 1))
            dve.wait_ge(stored[k], now(i * 32))
            nc.vector.tensor_scalar(gate[k][:], tanh[:], 0.5, 0.5, ALU.mult, ALU.add).then_inc(gate_ready, 1)
            dve.wait_ge(ranked, now(u + 1))
            dve.wait_ge(count_ready, now(u * 1))
            nc.vector.tensor_tensor(row[:], ps_k[:, 0:UPT, :], count[:].unsqueeze(1).broadcast_to([P, UPT, EXPERTS]), ALU.add).then_inc(row_ready, 1)
            dve.wait_ge(row_ready, now(u + 1))
            nc.vector.tensor_tensor(count[:], count[:], ps_k[:, UPT, :], ALU.add).then_inc(count_ready, 1)
            for n in range(TOP):
                nc.vector.tensor_tensor(rows[:, n], pick[:, n], row[:], ALU.mult).then_inc(rows_ready, 1)
            dve.wait_ge(rows_ready, now(u * 2 + 2))
            nc.vector.tensor_reduce(rowf[:], rows[:], AX.X, ALU.add).then_inc(rowf_ready, 1)
            dve.wait_ge(rowf_ready, now(u + 1))
            dve.wait_ge(scattered[k], now(i * 128))
            nc.vector.tensor_copy(pos[k][:], rowf[:]).then_inc(pos_ready, 1)
            at = (turn * 2 + k) * (TOP * UPT)
            nc.vector.tensor_copy(choice[:, slice(at, at + TOP * UPT) if isinstance(at, int) else ds(at, TOP * UPT)],
                                  rowf[:].rearrange("p n j -> p (n j)")).then_inc(choice_ready, 1)

        def share_dve(dve, i, k):
            u = i * 2 + k
            for h in range(HC):
                dve.wait_ge(act_ready, now(u * 2 + h + 1))
                dve.wait_ge(o_done, now(u * 1))
                nc.vector.tensor_tensor(hid[h][:], act1[h][:], ps_h[1][h][:], ALU.mult).then_inc(hid_ready, 1)

        def base_dve(dve, i, k):
            u = i * 2 + k
            dve.wait_ge(o_done, now(u + 1))
            dve.wait_ge(stored[k], now(i * 32))
            dve.wait_ge(xr_loaded[k], now(i * 16 + 16))
            nc.vector.tensor_tensor(base[k][:], ps_o[:], xr[k][:], ALU.add).then_inc(base_ready, 1)

        def turn_pe(i, k):
            u = i * 2 + k
            nc.tensor.wait_ge(xn_ready, now(u * UPT + UPT))
            nc.tensor.wait_ge(xT_ready, now(u * 1))
            for j in range(UPT):
                done = nc.tensor.transpose(ps_x[:, j * P:(j + 1) * P], xn[k][:, j, :], c["ident"][:])
            done.then_inc(xT_made, 1)
            nc.tensor.wait_ge(xT_ready, now(u + 1))
            nc.tensor.wait_ge(logits_ready, now(u * 1))
            for j in range(UPT):
                done = nc.tensor.matmul(ps_r[:, j, :], xnT[k][:, j * P:(j + 1) * P], rw[:], start=True, stop=True)
            done.then_inc(r_done, 1)

        def share_pe(i, k):
            u = i * 2 + k
            nc.tensor.wait_ge(hid_ready, now(u * 2))
            for h in range(HC):
                for w in range(2):
                    nc.tensor.matmul(ps_h[w][h][:], sw1[:, w, h * P:(h + 1) * P], xnT[k][:], start=True, stop=True).then_inc(h_done, 1)

        def rank_pe(i, k):
            u = i * 2 + k
            nc.tensor.wait_ge(chosen_ready, now(u + 1))
            nc.tensor.wait_ge(count_ready, now(u * 1))
            nc.tensor.matmul(ps_k[:], before[:], chosen[:], start=True, stop=True)
            for j in range(UPT):
                done = nc.tensor.matmul(ps_k[:, j + 1:, :], ones[:], chosen[:, j:j + 1, :].broadcast_to([P, UPT - j, EXPERTS]),
                                        start=False, stop=True, skip_group_check=True)
            done.then_inc(ranked, 1)

        def back_pe(i, k):
            u = i * 2 + k
            nc.tensor.wait_ge(hid_ready, now(u * 2 + 2))
            nc.tensor.wait_ge(base_ready, now(u * 1))
            for j in range(UPT):
                for h in range(HC):
                    done = nc.tensor.matmul(ps_o[:, j, :], hid[h][:, j * P:(j + 1) * P], sw3[:, h, :], start=h == 0, stop=h == HC - 1)
            done.then_inc(o_done, 1)

        with nc.Block() as block:
            @block.sync
            def _(sp):
                for k in range(2):
                    sp.dma_start(x[k][:], unit_of(src, 0, k)).then_inc(x_loaded[k], 16)
                sp.dma_start(rw[:], a["rw"]).then_inc(s_loaded, 16)
                sp.dma_start(rb[:], a["rb"].rearrange("(o n) -> o n", o=1).broadcast_to([P, EXPERTS])).then_inc(s_loaded, 16)
                for h, n in enumerate(("sw1", "sw2")):
                    sp.dma_start(sw1[:, h, :], a[n]).then_inc(s_loaded, 16)
                sp.dma_start(sw3[:], a["sw3"].rearrange("(h p) n -> p h n", p=P)).then_inc(s_loaded, 16)
                for h, n in enumerate(("ew1", "ew2")):
                    sp.dma_start(w[:, :, h * HIDDEN:(h + 1) * HIDDEN], a[n].rearrange("e p n -> p e n")).then_inc(w_loaded, 16)
                for h in range(HC):
                    sp.dma_start(w[:, :, 2 * HIDDEN + h * D:2 * HIDDEN + (h + 1) * D],
                                 a["ew3"][:, h * P:(h + 1) * P, :].rearrange("e p n -> p e n")).then_inc(w_loaded, 16)

                def stores(i, k, more):
                    if more:
                        sp.wait_ge(xn_ready, i * 8 + (k + 1) * UPT)
                        sp.dma_start(x[k][:], unit_of(src, i + 1, k)).then_inc(x_loaded[k], 16)
                    sp.wait_ge(gate_ready, i * 2 + k + 1)
                    sp.dma_start(dram["gate"][unit_no(i, k)].rearrange("u p n -> (u p) n"),
                                 gate[k][:].rearrange("p n j -> p (n j)")).then_inc(stored[k], 16)
                    sp.wait_ge(base_ready, i * 2 + k + 1)
                    sp.dma_start(unit_of(dram["base"], i, k), base[k][:]).then_inc(stored[k], 16)
                    if more:
                        sp.dma_start(xr[k][:], unit_of(src, i + 1, k)).then_inc(xr_loaded[k], 16)

                for k in range(2):
                    sp.dma_start(xr[k][:], unit_of(src, 0, k)).then_inc(xr_loaded[k], 16)
                with sp.Fori(0, B - 1) as i:
                    for k in range(2):
                        stores(i, k, True)
                for k in range(2):
                    stores(B - 1, k, False)
                sp.wait_ge(counted, 1)
                sp.dma_start(dram["ex"][IDLE:ROWS_EX, :].rearrange("(j p) d -> p j d", p=P), zeros[:]).then_inc(pads_stored, 16)
                for e in range(EXPERTS):
                    n = sp.value_load(counti[0:1, e:e + 1], min_val=0, max_val=N)
                    sp.dma_start(dram["ex"][ds(n + e * REGION, ROWS), :].rearrange("(j p) d -> p j d", p=P), zeros[:]).then_inc(pads_stored, 16)
                sp.wait_ge(pads_stored, (EXPERTS + 1) * 16)
                for k in range(2):
                    sp.wait_ge(stored[k], B * 32)

            @block.tensor
            def _(pe):
                pe.wait_ge(s_loaded, 5 * 16)
                pe.wait_ge(ready, 8)
                turns = Turns(pe, stage + "_pe", ROUTE_STRIDES)

                def unit(i, k, more):
                    share_pe(i, k)
                    rank_pe(i, k)
                    back_pe(i, k)
                    if more:
                        turn_pe(*ahead(i, k))

                turn_pe(0, 0)
                with pe.Fori(0, B - 1) as turn:
                    i = Linear(turns, turn)
                    for k in range(2):
                        unit(i, k, True)
                    turns.step()
                for k in range(2):
                    unit(B - 1, k, k == 0)

            @block.vector
            def _(dve):
                dve.wait_ge(s_loaded, 5 * 16)
                dve.wait_ge(ready, 5)
                nc.vector.tensor_copy(before[:], c["strict"][:, 0, :]).then_inc(ready, 1)
                for free in (region, count):
                    nc.vector.tensor_scalar(free[:], number[:, 0, :], float(REGION), None, ALU.mult).then_inc(ready, 1)
                dve.wait_ge(ready, 8)
                turns = Turns(dve, stage + "_dve", ROUTE_STRIDES)
                for k in range(2):
                    mean_dve(dve, 0, k)
                norm_dve(dve, 0, 0)

                def unit(i, k, turn, more, most):
                    choose_dve(dve, i, k)
                    if most:
                        mean_dve(dve, i + 1, k)
                    share_dve(dve, i, k)
                    place_dve(dve, i, k, turn)
                    if more:
                        norm_dve(dve, *ahead(i, k))
                    base_dve(dve, i, k)

                with dve.Fori(0, B - 1) as turn:
                    i = Linear(turns, turn)
                    for k in range(2):
                        unit(i, k, turn, True, True)
                    turns.step()
                for k in range(2):
                    unit(B - 1, k, B - 1, k == 0, False)
                dve.wait_ge(count_ready, 2 * B)
                nc.vector.tensor_tensor(count[:], count[:], region[:], ALU.subtract).then_inc(count_ready, 1)
                dve.wait_ge(count_ready, 2 * B + 1)
                nc.vector.tensor_copy(counti[:], count[0:1, :]).then_inc(counted, 1)
                dve.wait_ge(made, 4)
                dve.wait_ge(choice_ready, 2 * B)
                make_table(nc, dve, t, count, choice, step_dve, tabled)

            @block.scalar
            def _(act):
                turns = Turns(act, stage + "_act", ROUTE_STRIDES)

                def turn_act(i, k):
                    act.wait_ge(xT_made, now(i * 2 + (k + 1)))
                    act.wait_ge(h_done, now(i * 8))
                    nc.scalar.activation(xnT[k][:], ps_x[:], ACT.Copy).then_inc(xT_ready, 1)

                def unit(i, k, more):
                    u = i * 2 + k
                    for h in range(HC):
                        act.wait_ge(h_done, now(u * UPT + (2 * h + 2)))
                        act.wait_ge(hid_ready, now(u * 2))
                        nc.scalar.activation(act1[h][:], ps_h[0][h][:], ACT.Silu).then_inc(act_ready, 1)
                    act.wait_ge(gap_ready, now(u * 2 + 2))
                    act.wait_ge(gate_ready, now(u * 1))
                    nc.scalar.activation(tanh[:], gap[:], ACT.Tanh, scale=0.5).then_inc(tanh_ready, 1)
                    if more:
                        turn_act(*ahead(i, k))

                turn_act(0, 0)
                with act.Fori(0, B - 1) as turn:
                    i = Linear(turns, turn)
                    for k in range(2):
                        unit(i, k, True)
                    turns.step()
                for k in range(2):
                    unit(B - 1, k, k == 0)

            @block.gpsimd
            def _(pool):
                nc.gpsimd.memset(power[:], -0.5).then_inc(ready, 1)
                nc.gpsimd.memset(ones[:], 1.0).then_inc(ready, 1)
                nc.gpsimd.memset(zeros[:], 0.0).then_inc(ready, 1)
                nc.gpsimd.memset(chosen[:], 0.0).then_inc(ready, 1)
                nc.gpsimd.iota(number[:], pattern=[[0, UPT], [1, EXPERTS]], base=0, channel_multiplier=0,
                               allow_small_or_imprecise_dtypes=True).then_inc(ready, 1)

                def rstd_of(i, k):
                    u = i * 2 + k
                    pool.wait_ge(mean, now(u * UPT + UPT))
                    pool.wait_ge(rstd_ready, now(u * 1))
                    if past(i, 1):
                        pool.wait_ge(xn_ready, now((u + -1) * UPT))
                    pool.sem_inc(passed, 1)
                    nc.gpsimd.tensor_scalar(veps[:], mv[k][:, :, 1], EPS, 1.0, ALU.add, ALU.mult).then_inc(veps_ready, 1)
                    pool.wait_ge(veps_ready, now(u + 1))
                    nc.gpsimd.tensor_tensor(rstd[k][:], veps[:], power[:], ALU.pow).then_inc(rstd_ready, 1)

                def send(u, k):
                    pool.wait_ge(pos_ready, now(u + 1))
                    pool.wait_ge(xn_ready, now(u * UPT + UPT))
                    pool.sem_inc(passed, 1)
                    for n in range(TOP):
                        for j in range(UPT):
                            nc.gpsimd.indirect_dma_start(dram["ex"], bass.IndirectOffsetOnAxis(ap=pos[k][:, n, j:j + 1], axis=0),
                                                         xn[k][:, j, :], None).then_inc(scattered[k], 16)

                for k in range(2):
                    rstd_of(0, k)
                nc.gpsimd.iota(t["tile"][:], pattern=[[1, TILES_EX], [0, EXPERTS]], base=0, channel_multiplier=0,
                               allow_small_or_imprecise_dtypes=True).then_inc(made, 1)
                nc.gpsimd.iota(t["enum"][:], pattern=[[0, TILES_EX], [1, EXPERTS]], base=0, channel_multiplier=0,
                               allow_small_or_imprecise_dtypes=True).then_inc(made, 1)
                nc.gpsimd.memset(t["onesv"][:], 1.0).then_inc(made, 1)
                nc.gpsimd.iota(t["number"][:], pattern=[[1, EXPERTS]], base=0, channel_multiplier=0,
                               allow_small_or_imprecise_dtypes=True).then_inc(made, 1)
                turns = Turns(pool, stage + "_pool", ROUTE_STRIDES)
                with pool.Fori(0, B - 1) as turn:
                    i = Linear(turns, turn)
                    for k in range(2):
                        rstd_of(i + 1, k)
                        send(i * 2 + k, k)
                    turns.step()
                for k in range(2):
                    send(2 * B - 2 + k, k)
                for k in range(2):
                    pool.wait_ge(scattered[k], B * 128)
        m.clear()


def table_memory(m):
    tab = [1, TILES_EX, EXPERTS]
    tiles, tilesi = m.sb("tiles", [P, EXPERTS]), m.sb("tilesi", [P, EXPERTS], I32)
    ends = m.sb("ends", [P, EXPERTS])
    starts, onesv = m.sb("starts", [P, EXPERTS]), m.sb("onesv", [P, EXPERTS])
    shift, jump = m.sb("shift", [P, EXPERTS]), m.sb("jump", [P, EXPERTS])
    number = m.sb("number", [P, EXPERTS])
    total = m.sb("total", [P, 2 * B * TOP * UPT])
    moved = m.sb("moved", [P, 2 * B * TOP * UPT])
    result_row = m.sb("result_row", [P, 2 * B * TOP * UPT], I32)
    tile, enum = m.sb("tile", tab), m.sb("enum", tab)
    begun, over, mine = m.sb("begun", tab), m.sb("over", tab), m.sb("mine", tab)
    local, rows = m.sb("local", tab), m.sb("rows", tab)
    eid, first = m.sb("eid", [1, TILES_EX]), m.sb("first", [1, TILES_EX])
    at_expert, firsti = m.sb("at_expert", [1, TILES_EX], I32), m.sb("firsti", [1, TILES_EX], I32)
    return {"tiles": tiles, "tilesi": tilesi, "ends": ends, "starts": starts, "onesv": onesv, "shift": shift, "jump": jump, "number": number, "total": total, "moved": moved, "result_row": result_row, "tile": tile, "enum": enum, "begun": begun, "over": over, "mine": mine, "local": local, "rows": rows, "eid": eid, "first": first, "at_expert": at_expert, "firsti": firsti}


def make_table(nc, dve, t, count, choice, step_dve, tabled):
    tiles, tilesi, ends, starts, onesv, shift = t["tiles"], t["tilesi"], t["ends"], t["starts"], t["onesv"], t["shift"]
    jump, number, total, moved, result_row, tile = t["jump"], t["number"], t["total"], t["moved"], t["result_row"], t["tile"]
    enum, begun, over, mine, local, rows = t["enum"], t["begun"], t["over"], t["mine"], t["local"], t["rows"]
    eid, first, at_expert, firsti = t["eid"], t["first"], t["at_expert"], t["firsti"]
    steps = 0

    def did(done):
        nonlocal steps
        steps += 1
        done.then_inc(step_dve, 1)
        dve.wait_ge(step_dve, steps)

    did(nc.vector.tensor_scalar(tiles[:], count[:], float(ROWS - 1), None, ALU.add))
    did(nc.vector.tensor_copy(tilesi[:], tiles[:]))
    did(nc.vector.tensor_scalar(tilesi[:], tilesi[:], ROWS.bit_length() - 1, None, ALU.arith_shift_right))
    did(nc.vector.tensor_copy(tiles[:], tilesi[:]))
    did(nc.vector.tensor_tensor_scan(ends[:], onesv[:], tiles[:], 0.0, ALU.mult, ALU.add))
    did(nc.vector.tensor_tensor(starts[:], ends[:], tiles[:], ALU.subtract))
    wide = [1, TILES_EX, EXPERTS]
    did(nc.vector.tensor_tensor(begun[:], tile[:], starts[0:1, :].unsqueeze(1).broadcast_to(wide), ALU.is_ge))
    did(nc.vector.tensor_tensor(over[:], tile[:], ends[0:1, :].unsqueeze(1).broadcast_to(wide), ALU.is_lt))
    did(nc.vector.tensor_tensor(mine[:], begun[:], over[:], ALU.mult))
    did(nc.vector.tensor_tensor(begun[:], mine[:], enum[:], ALU.mult))
    did(nc.vector.tensor_reduce(eid[:], begun[:], AX.X, ALU.add))
    did(nc.vector.tensor_scalar(eid[:], eid[:], float(EW), None, ALU.mult))
    nc.vector.tensor_copy(at_expert[:], eid[:]).then_inc(tabled, 1)
    did(nc.vector.tensor_tensor(local[:], tile[:], starts[0:1, :].unsqueeze(1).broadcast_to(wide), ALU.subtract))
    did(nc.vector.tensor_scalar(local[:], local[:], float(ROWS), float(-IDLE), ALU.mult, ALU.add))
    did(nc.vector.scalar_tensor_tensor(rows[:], enum[:], float(REGION), local[:], ALU.mult, ALU.add))
    did(nc.vector.tensor_tensor(rows[:], rows[:], mine[:], ALU.mult))
    did(nc.vector.tensor_reduce(first[:], rows[:], AX.X, ALU.add))
    did(nc.vector.tensor_scalar(first[:], first[:], float(IDLE), None, ALU.add))
    nc.vector.tensor_copy(firsti[:], first[:]).then_inc(tabled, 1)
    did(nc.vector.tensor_scalar(shift[:], number[:], float(-REGION), None, ALU.mult))
    did(nc.vector.scalar_tensor_tensor(shift[:], starts[:], float(ROWS), shift[:], ALU.mult, ALU.add))
    did(nc.vector.tensor_tensor(jump[:, 1:], shift[:, 1:], shift[:, 0:EXPERTS - 1], ALU.subtract))
    for e in range(1, EXPERTS):
        did(nc.vector.tensor_scalar(moved[:], choice[:], float(e * REGION), jump[:, e:e + 1], ALU.is_ge, ALU.mult))
        last = choice if e == 1 else total
        did(nc.vector.tensor_tensor(total[:], last[:], moved[:], ALU.add))
    nc.vector.tensor_copy(result_row[:], total[:]).then_inc(tabled, 1)


def run_experts(nc, dram, c, stage, w, w_loaded, count, choice, t):
    with ExitStack() as ctx:
        m = Mem(nc, ctx, stage)
        at_expert, firsti = t["at_expert"], t["firsti"]
        result_row = t["result_row"]
        x = [m.sb(f"x{q}", [P, SUB, D]) for q in range(AHEAD)]
        xT = [m.sb(f"xT{q}", [P, ROWS]) for q in range(2)]
        act1 = [m.sb(f"act{q}", [P, SUB, HIDDEN]) for q in range(2)]
        hid = [m.sb(f"hid{q}", [P, SUB, HIDDEN]) for q in range(2)]
        hidT = [m.sb(f"hidT{q}", [P, SUB, HIDDEN]) for q in range(2)]
        out = [m.sb(f"out{q}", [P, SUB, D]) for q in range(AHEAD)]
        ps_x = m.ps("ps_x", [P, ROWS])
        ps_h = [m.ps(f"ps_h{q}", [P, SUB, 2 * HIDDEN]) for q in range(2)]
        ps_t = [m.ps(f"ps_t{q}", [P, SUB, HIDDEN]) for q in range(2)]
        ps_o = m.ps("ps_o", [P, SUB, D])
        step, rows_stored = m.sem("step"), m.sem("rows_stored")
        loaded = [m.sem(f"loaded{q}") for q in range(AHEAD)]
        stored = [m.sem(f"stored{q}") for q in range(AHEAD)]
        x_made, xT_ready, h_done, act_ready, hid_ready = (m.sem(n) for n in ("x_made", "xT", "h_done", "act", "hid"))
        t_done, hidT_ready, o_done, out_ready = (m.sem(n) for n in ("t_done", "hidT", "o_done", "out"))

        def number_of(i, q):
            return ds(i * AHEAD + q, 1) if not isinstance(i, int) else slice(i * AHEAD + q, i * AHEAD + q + 1)

        def rows_of(i, q):
            at = (i * AHEAD + q) * ROWS
            return slice(at, at + ROWS) if isinstance(i, int) else ds(at, ROWS)

        def shifted(i, q, by):
            at = q + by
            return i + at // AHEAD, at % AHEAD

        def pipeline(body, turns, eng, lag):
            deepest = max(lag)
            for s in range(AHEAD):
                body(0, 0, s, [g <= s for g in lag])
            with eng.Fori(1, TILES_EX // AHEAD) as turn:
                for q in range(AHEAD):
                    body(Linear(turns, turn), turn, q, [True] * len(lag))
                turns.step()
            for s in range(deepest):
                body(TILES_EX // AHEAD, TILES_EX // AHEAD, s, [g > s for g in lag])

        with nc.Block() as block:
            @block.sync
            def _(sp):
                turns = Turns(sp, stage + "_sp", EXPERT_STRIDES, first=1)

                def body(i, at, q, on):
                    if past(i, 1):
                        sp.wait_ge(x_made, now(i * AHEAD + (q + 1 - AHEAD)))
                        sp.sem_inc(step, 1)
                    r = sp.value_load(firsti[0:1, number_of(at, q)], min_val=0, max_val=IDLE)
                    sp.dma_start(x[q][:], dram["ex"][ds(r, ROWS), :].rearrange("(j p) d -> p j d", p=P)).then_inc(loaded[q], 16)

                pipeline(body, turns, sp, [0])
                sp.dma_start(dram["pos"].rearrange("u p n -> p u n"), result_row[:].rearrange("p (u n) -> p u n", u=2 * B)).then_inc(rows_stored, 16)
                sp.wait_ge(rows_stored, 16)

            @block.vector
            def _(dve):
                turns = Turns(dve, stage + "_dve", EXPERT_STRIDES, first=1)

                def body(i, at, q, on):
                    s = i * AHEAD + q
                    if on[1]:
                        z = (q - 3) % 2
                        dve.wait_ge(t_done, now(s - 2))
                        if past(s, 5):
                            dve.wait_ge(o_done, now(s - 4))
                        nc.vector.tensor_copy(hidT[z][:], ps_t[z][:]).then_inc(hidT_ready, 1)
                    if on[0]:
                        z = (q - 1) % 2
                        dve.wait_ge(act_ready, now(s + 0))
                        if past(s, 3):
                            dve.wait_ge(t_done, now(s - 2))
                        nc.vector.tensor_tensor(hid[z][:], act1[z][:], ps_h[z][:, :, HIDDEN:], ALU.mult).then_inc(hid_ready, 1)

                pipeline(body, turns, dve, [1, 3])

            @block.tensor
            def _(pe):
                pe.wait_ge(w_loaded, 4 * 16)
                turns = Turns(pe, stage + "_pe", EXPERT_STRIDES, room=8, first=1)
                flat = w[:].rearrange("p e n -> p (e n)")

                def body(i, at, q, on):
                    s = i * AHEAD + q
                    if on[3]:
                        z, (ti, tq) = q % 2, shifted(at, q, -4)
                        e = pe.value_load(at_expert[0:1, number_of(ti, tq)])
                        pe.wait_ge(hidT_ready, now(s - 3))
                        if past(s, 5):
                            pe.wait_ge(out_ready, now(s - 4))
                        for h in range(HC):
                            w3 = flat[:, ds(e + (2 * HIDDEN + h * D), D)]
                            for j in range(SUB):
                                done = nc.tensor.matmul(ps_o[:, j, :], hidT[z][:, j, h * P:(h + 1) * P], w3,
                                                        start=h == 0 and j == 0, stop=h == HC - 1, skip_group_check=True)
                        done.then_inc(o_done, 1)
                    if on[2]:
                        z = (q - 3) % 2
                        pe.wait_ge(hid_ready, now(s - 2))
                        if past(s, 5):
                            pe.wait_ge(hidT_ready, now(s - 4))
                        for j in range(SUB):
                            for h in range(HC):
                                done = nc.tensor.transpose(ps_t[z][:, j, h * P:(h + 1) * P], hid[z][:, j, h * P:(h + 1) * P], c["ident"][:])
                        done.then_inc(t_done, 1)
                    if on[1]:
                        z, (ti, tq) = (q - 1) % 2, shifted(at, q, -1)
                        e = pe.value_load(at_expert[0:1, number_of(ti, tq)])
                        pe.wait_ge(xT_ready, now(s + 0))
                        if past(s, 3):
                            pe.wait_ge(hid_ready, now(s - 2))
                        for j in range(SUB):
                            done = nc.tensor.matmul(ps_h[z][:, j, :], xT[z][:, j * P:(j + 1) * P], flat[:, ds(e, 2 * HIDDEN)], start=True, stop=True)
                        done.then_inc(h_done, 1)
                    if on[0]:
                        pe.wait_ge(loaded[q], now(i * 16 + 16))
                        if past(s, 1):
                            pe.wait_ge(xT_ready, now(s + 0))
                        for j in range(SUB):
                            done = nc.tensor.transpose(ps_x[:, j * P:(j + 1) * P], x[q][:, j, :], c["ident"][:])
                        done.then_inc(x_made, 1)

                pipeline(body, turns, pe, [0, 1, 3, 4])

            @block.scalar
            def _(act):
                turns = Turns(act, stage + "_act", EXPERT_STRIDES, first=1)

                def body(i, at, q, on):
                    s = i * AHEAD + q
                    if on[2]:
                        z, (ti, tq) = q, shifted(at, q, -4)
                        act.wait_ge(o_done, now(s - 3))
                        if past(s, 2 * AHEAD):
                            act.wait_ge(stored[z], now(i * 16 - 16))
                        nc.scalar.activation(out[z][:], ps_o[:], ACT.Copy).then_inc(out_ready, 1)
                        act.wait_ge(out_ready, now(s - 3))
                        act.dma_start(dram["ey"][rows_of(ti, tq), :].rearrange("(j p) d -> p j d", p=P), out[z][:]).then_inc(stored[z], 16)
                    if on[1]:
                        z = (q - 1) % 2
                        act.wait_ge(h_done, now(s + 0))
                        if past(s, 3):
                            act.wait_ge(hid_ready, now(s - 2))
                        nc.scalar.activation(act1[z][:], ps_h[z][:, :, 0:HIDDEN], ACT.Silu).then_inc(act_ready, 1)
                    if on[0]:
                        act.wait_ge(x_made, now(s + 1))
                        if past(s, 2):
                            act.wait_ge(h_done, now(s - 1))
                        nc.scalar.activation(xT[q % 2][:], ps_x[:], ACT.Copy).then_inc(xT_ready, 1)

                pipeline(body, turns, act, [0, 1, 4])
                for q in range(AHEAD):
                    act.wait_ge(stored[q], TILES_EX // AHEAD * 16)
        m.clear()


def join(nc, dram, stage, dst):
    with ExitStack() as ctx:
        m = Mem(nc, ctx, stage)
        pos = [m.sb(f"pos{k}", [P, TOP, UPT], I32) for k in range(2)]
        gate = [m.sb(f"gate{k}", [P, TOP, UPT]) for k in range(2)]
        base = [m.sb(f"base{k}", [P, UPT, D]) for k in range(2)]
        y = [m.sb(f"y{k}", [P, TOP, UPT, D]) for k in range(2)]
        half = m.sb("half", [P, UPT, D])
        out = [m.sb(f"out{k}", [P, UPT, D]) for k in range(2)]
        pos_loaded, gate_loaded, half_ready, out_ready, stored = (m.pair(n) for n in ("pos_ld", "gate_ld", "half", "out", "stored"))
        passed = m.sem("passed")
        gathered = dram[stage + "_got"]

        def unit_of(t, i, k):
            at = ds(i * T + k * UNIT, UNIT) if not isinstance(i, int) else slice(i * T + k * UNIT, i * T + (k + 1) * UNIT)
            return t[at, :].rearrange("(j p) d -> p j d", p=P)

        with nc.Block() as block:
            @block.sync
            def _(sp):
                def loads(i, k):
                    sp.wait_ge(gathered[k], i * 128)
                    sp.dma_start(pos[k][:].rearrange("p n j -> p (n j)"), dram["pos"][unit_no(i, k)].rearrange("u p n -> (u p) n")).then_inc(pos_loaded[k], 16)
                    sp.wait_ge(out_ready[k], i * UPT)
                    sp.dma_start(gate[k][:].rearrange("p n j -> p (n j)"), dram["gate"][unit_no(i, k)].rearrange("u p n -> (u p) n")).then_inc(gate_loaded[k], 16)
                    sp.dma_start(base[k][:], unit_of(dram["base"], i, k)).then_inc(gate_loaded[k], 16)

                def store(i, k):
                    sp.wait_ge(out_ready[k], i * UPT + UPT)
                    sp.dma_start(unit_of(dst, i, k), out[k][:]).then_inc(stored[k], 16)

                for k in range(2):
                    loads(0, k)
                with sp.Fori(0, B - 1) as i:
                    for k in range(2):
                        store(i, k)
                        loads(i + 1, k)
                for k in range(2):
                    store(B - 1, k)
                for k in range(2):
                    sp.wait_ge(stored[k], B * 16)

            @block.gpsimd
            def _(pool):
                turns = Turns(pool, stage + "_pool", JOIN_STRIDES)
                with pool.Fori(0, B) as turn:
                    i = Linear(turns, turn)
                    for k in range(2):
                        pool.wait_ge(pos_loaded[k], now(i * 16 + 16))
                        pool.wait_ge(out_ready[k], now(i * UPT))
                        pool.sem_inc(passed, 1)
                        for j in range(UPT):
                            for n in range(TOP):
                                nc.gpsimd.indirect_dma_start(y[k][:, n, j, :], None, dram["ey"],
                                                             bass.IndirectOffsetOnAxis(ap=pos[k][:, n, j:j + 1], axis=0)).then_inc(gathered[k], 16)
                    turns.step()
                for k in range(2):
                    pool.wait_ge(gathered[k], B * 128)

            @block.vector
            def _(dve):
                turns = Turns(dve, stage + "_dve", JOIN_STRIDES)
                with dve.Fori(0, B) as turn:
                    i = Linear(turns, turn)
                    for k in range(2):
                        dve.wait_ge(gathered[k], now(i * 128 + 128))
                        dve.wait_ge(gate_loaded[k], now(i * 32 + 32))
                        dve.wait_ge(stored[k], now(i * 16))
                        if k == 0:
                            dve.wait_ge(out_ready[1], now(i * UPT))
                        else:
                            dve.wait_ge(out_ready[0], now(i * UPT + UPT))
                        for j in range(UPT):
                            nc.vector.scalar_tensor_tensor(half[:, j, :], y[k][:, 0, j, :], gate[k][:, 0, j:j + 1], base[k][:, j, :],
                                                           ALU.mult, ALU.add).then_inc(half_ready[k], 1)
                        for j in range(UPT):
                            dve.wait_ge(half_ready[k], now(i * UPT + j + 1))
                            nc.vector.scalar_tensor_tensor(out[k][:, j, :], y[k][:, 1, j, :], gate[k][:, 1, j:j + 1], half[:, j, :],
                                                           ALU.mult, ALU.add).then_inc(out_ready[k], 1)
                    turns.step()
        m.clear()


def routing_scratch(nc, m, dram, stages):
    for name, shape, dt in (("ex", (ROWS_EX, D), F32), ("ey", (TILES_EX * ROWS, D), F32), ("base", (N, D), F32),
                            ("pos", (2 * B, P, TOP * UPT), I32), ("gate", (2 * B, P, TOP * UPT), F32)):
        dram[name] = nc.dram_tensor(f"{name}_dram", shape, dt).ap()
    for stage in stages:
        dram[stage + "r_sent"] = m.pair(stage + "_sent")
        dram[stage + "j_got"] = m.pair(stage + "_got")


INNER, STATES, TAPS, DT_RANK = 256, 16, 4, 64
CH = INNER // P
BC = 2 * STATES
NS = STATES * CH
ITEMS = 9
AT = {0: [0], 1: [], 3: [1], 4: [2], 5: [3], 6: [4], 7: [5, 6], 8: [7], 9: [8, 9], 10: [10, 11], 11: [12], 12: [13], 13: [14], 14: [15]}
FINISH_AT, OUT_AT = 2, 3
LAG = 2
SCAN_STRIDES = sorted({1, 2, 4, 16, STATES, NS, ITEMS, UPT})


def scan(nc, dram, c, a, src, dst):
    with ExitStack() as ctx:
        m = Mem(nc, ctx, "ssm")
        win, wconv = m.sb("win", [P, 2 * INNER]), m.sb("wconv", [P, TAPS, INNER])
        taps = m.sb("taps", [P, INNER, TAPS])
        conv_b, dt_b, skip = m.sb("conv_b", [P, CH]), m.sb("dt_b", [P, CH]), m.sb("skip", [P, CH])
        alog, aneg = m.sb("alog", [P, CH, STATES]), m.sb("aneg", [P, CH, STATES])
        wdr, wbc = m.sb("wdr", [P, CH, DT_RANK]), m.sb("wbc", [P, CH, PARTS, BC])
        wdt, wout = m.sb("wdt", [DT_RANK, INNER]), m.sb("wout", [P, CH, D])
        pick = m.sb("pick", [P, BC, P], BF16)
        x = [m.sb(f"x{k}", [P, UPT, D]) for k in range(2)]
        stats, mv = m.sb("stats", [P, UPT, 6]), m.sb("mv", [P, UPT, 2])
        veps, power, rstd = m.sb("veps", [P, UPT]), m.sb("power", [P, UPT]), m.sb("rstd", [P, UPT])
        xn, xr = m.sb("xn", [P, UPT, D]), m.sb("xr", [P, UPT, D])
        xnT = [m.sb(f"xnT{k}", [P, TAPS - 1 + UNIT]) for k in range(2)]
        pre = m.sb("pre", [P, 2 * CH, UNIT])
        gated = [m.sb(f"gated{k}", [P, 2 * CH, UNIT]) for k in range(2)]
        dr = m.sb("dr", [DT_RANK, UNIT])
        stack = [m.sb(f"stack{k}", [PARTS * BC, UNIT], BF16) for k in range(2)]
        rest, part2 = m.sb("rest", [PARTS * BC, UNIT]), m.sb("part2", [PARTS * BC, UNIT], BF16)
        dtx, soft = m.sb("dtx", [P, CH, UNIT]), m.sb("soft", [P, CH, UNIT])
        delta = [m.sb(f"delta{k}", [P, CH, UNIT]) for k in range(2)]
        u = [m.sb(f"u{k}", [P, CH, UNIT]) for k in range(2)]
        decay = [[m.sb(f"decay{ch}{s}", [P, UNIT]) for s in range(2)] for ch in range(CH)]
        h0 = [m.sb(f"h0{ch}", [P, STATES, UNIT]) for ch in range(CH)]
        h1 = [m.sb(f"h1{ch}", [P, 2, UNIT]) for ch in range(CH)]
        cb = [m.sb(f"cb{s}", [P, UNIT]) for s in range(2)]
        hc = [[m.sb(f"hc{ch}{s}", [P, UNIT]) for s in range(2)] for ch in range(CH)]
        yd, yg, out = m.sb("yd", [P, CH, UNIT]), m.sb("yg", [P, CH, UNIT]), m.sb("out", [P, UPT, D])
        ps_b = [m.ps(f"ps_b{s}", [P, UNIT]) for s in range(2)]
        ps_c, ps_m = m.ps("ps_c", [P, UNIT]), m.ps("ps_m", [P, UNIT])
        ps_d = [m.ps(f"ps_d{ch}", [P, UNIT]) for ch in range(CH)]
        ps_y = [m.ps(f"ps_y{ch}", [P, UNIT]) for ch in range(CH)]
        w_loaded, w_ready, filled, passed, a_ready = (m.sem(n) for n in ("w_ld", "w_ready", "filled", "passed", "a_ready"))
        x_loaded, stat, mean, veps_ready, rstd_ready, xn_ready = (m.pair(n) for n in ("x_ld", "stat", "mean", "veps", "rstd", "xn"))
        item_done, item_free, gated_ready = (m.pair(n) for n in ("item_done", "item_free", "gated"))
        halo, xr_loaded = m.sem("halo"), m.pair("xr_ld")
        part1_ready, part2_ready, part3_ready = (m.pair(n) for n in ("part1", "part2", "part3"))
        abs_ready, exp_ready, ln_ready, delta_ready, u_ready = (m.pair(n) for n in ("abs", "exp", "ln", "delta", "u"))
        b_done, c_done, c_kept, decay_ready = (m.pair(n) for n in ("b_done", "c_done", "c_kept", "decay"))
        dbx_done, scan_done, hc_done, y_done = (m.pair(n) for n in ("dbx", "scan", "hc", "y_done"))
        yd_ready, yg_ready, o_done, out_ready, out_stored = (m.pair(n) for n in ("yd", "yg", "o_done", "out", "out_st"))

        def after(i, k):
            return (i, 1) if k == 0 else (i + 1, 0)

        def item(i, k, j, build):
            if j == 0:
                nc.tensor.wait_ge(out_ready[k], now(i * 1))
                nc.tensor.wait_ge(item_free[1 - k], now((i + k) * ITEMS))
            else:
                nc.tensor.wait_ge(item_free[k], now(i * ITEMS + j))
            build().then_inc(item_done[k], 1)

        def turn_x(k):
            for j in range(UPT):
                done = nc.tensor.transpose(ps_m[:, j * P:(j + 1) * P], xn[:, j, :], c["ident"][:])
            return done

        def conv(k, ch):
            for tap in range(TAPS):
                done = nc.tensor.matmul(ps_m[:], wconv[:, tap, ch * P:(ch + 1) * P], xnT[k][:, tap:tap + UNIT],
                                        start=tap == 0, stop=tap == TAPS - 1)
            return done

        def gate_in(k, ch):
            return nc.tensor.matmul(ps_m[:], win[:, INNER + ch * P:INNER + (ch + 1) * P], xnT[k][:, TAPS - 1:], start=True, stop=True)

        def low_rank(k, w, rows):
            for ch in range(CH):
                done = nc.tensor.matmul(ps_m[0:rows, :], w[:, ch], gated[k][:, ch, :], start=ch == 0, stop=ch == CH - 1)
            return done

        def prepare_pe(i, k, n):
            if n == 2:
                nc.tensor.wait_ge(xn_ready[k], now(i * UPT + UPT))
                item(i, k, 0, lambda: turn_x(k))
            elif n in (3, 4):
                if n == 3 and k == 1:
                    nc.tensor.wait_ge(halo, now(i + 1))
                item(i, k, n - 2, lambda: conv(k, n - 3))
            elif n in (5, 6):
                item(i, k, n - 2, lambda: gate_in(k, n - 5))
            elif n == 8:
                nc.tensor.wait_ge(gated_ready[k], now(i + 1))
                item(i, k, 5, lambda: low_rank(k, wdr, DT_RANK))
            elif n == 9:
                item(i, k, 6, lambda: low_rank(k, wbc[:].rearrange("p c s r -> p c (s r)"), PARTS * BC))
            elif n in (10, 11):
                item(i, k, n - 3, lambda: nc.tensor.matmul(ps_m[:], wdt[:, (n - 10) * P:(n - 9) * P], dr[:], start=True, stop=True))

        def prepare_act(act, i, k, n):
            if n == 2:
                act.wait_ge(item_done[k], now(i * ITEMS + 1))
                act.wait_ge(halo, now(i * 1))
                nc.scalar.activation(xnT[k][:, TAPS - 1:], ps_m[:], ACT.Copy).then_inc(item_free[k], 1)
                if k == 1:
                    act.wait_ge(item_free[0], now(i * ITEMS + ITEMS))
                    nc.scalar.activation(xnT[1][:, 0:TAPS - 1], xnT[0][:, UNIT:], ACT.Copy).then_inc(halo, 1)
            elif 3 <= n <= 6:
                if n == 3:
                    act.wait_ge(gated_ready[1 - k], now(i + k))
                act.wait_ge(item_done[k], now(i * ITEMS + n - 1))
                if n < 5:
                    nc.scalar.activation(pre[:, n - 3, :], ps_m[:], ACT.Identity, bias=conv_b[:, n - 3:n - 2]).then_inc(item_free[k], 1)
                else:
                    nc.scalar.activation(pre[:, n - 3, :], ps_m[:], ACT.Copy).then_inc(item_free[k], 1)
            elif n == 7:
                act.wait_ge(item_free[k], now(i * ITEMS + 5))
                act.wait_ge(yg_ready[k], now(i * 2))
                nc.scalar.activation(gated[k][:], pre[:], ACT.Silu).then_inc(gated_ready[k], 1)
            elif n == 8:
                act.wait_ge(item_done[k], now(i * ITEMS + 6))
                act.wait_ge(item_done[1 - k], now((i + k) * ITEMS))
                nc.scalar.activation(dr[:], ps_m[0:DT_RANK, :], ACT.Copy).then_inc(item_free[k], 1)
            elif n == 9:
                act.wait_ge(item_done[k], now(i * ITEMS + 7))
                act.wait_ge(c_done[k], now(i * STATES))
                nc.scalar.activation(stack[k][:], ps_m[0:PARTS * BC, :], ACT.Copy).then_inc(part1_ready[k], 1)
            elif n == 10:
                act.wait_ge(item_free[k], now(i * ITEMS + 7))
                act.wait_ge(part3_ready[1 - k], now(i + k))
                nc.scalar.activation(stack[k][BC:2 * BC, :], rest[BC:2 * BC, :], ACT.Copy).then_inc(part2_ready[k], 1)
                nc.scalar.activation(part2[2 * BC:3 * BC, :], rest[2 * BC:3 * BC, :], ACT.Copy).then_inc(part2_ready[k], 1)
            elif n == 12:
                act.wait_ge(item_free[k], now(i * ITEMS + ITEMS))
                act.wait_ge(delta_ready[1 - k], now(i + k))
                nc.scalar.activation(soft[:], dtx[:], ACT.Abs).then_inc(abs_ready[k], 1)
                act.wait_ge(abs_ready[k], now(i + 1))
                nc.scalar.activation(soft[:], soft[:], ACT.Exp, scale=-1.0).then_inc(exp_ready[k], 1)
            elif n == 13:
                act.wait_ge(exp_ready[k], now(i + 1))
                nc.scalar.activation(soft[:], soft[:], ACT.Ln, bias=1.0).then_inc(ln_ready[k], 1)

        def prepare_dve(dve, i, k, n):
            if n == 0:
                dve.wait_ge(x_loaded[k], now(i * 16 + 16))
                for j in range(UPT):
                    nc.vector.bn_stats(stats[:, j, :], x[k][:, j, :]).then_inc(stat[k], 1)
                dve.wait_ge(stat[k], now(i * UPT + UPT))
                dve.sem_inc(passed, 1)
                for j in range(UPT):
                    nc.vector.bn_aggr(mv[:, j, :], stats[:, j, :]).then_inc(mean[k], 1)
            elif n == 1:
                dve.wait_ge(rstd_ready[k], now(i + 1))
                dve.wait_ge(item_done[1 - k], now((i + k) * ITEMS))
                for j in range(UPT):
                    nc.vector.tensor_scalar(xn[:, j, :], x[k][:, j, :], mv[:, j, 0:1], rstd[:, j:j + 1],
                                            ALU.subtract, ALU.mult).then_inc(xn_ready[k], 1)
            elif n == 9:
                dve.wait_ge(part1_ready[k], now(i + 1))
                dve.wait_ge(part3_ready[1 - k], now(i + k))
                nc.vector.tensor_tensor(rest[:], ps_m[0:PARTS * BC, :], stack[k][:], ALU.subtract).then_inc(item_free[k], 1)
            elif n in (10, 11):
                ch = n - 10
                dve.wait_ge(item_done[k], now(i * ITEMS + n - 2))
                dve.wait_ge(delta_ready[1 - k], now(i + k))
                nc.vector.tensor_scalar(dtx[:, ch, :], ps_m[:], dt_b[:, ch:ch + 1], None, ALU.add).then_inc(item_free[k], 1)
            elif n == 12:
                dve.wait_ge(part2_ready[k], now(i * 2 + 2))
                nc.vector.tensor_tensor(stack[k][2 * BC:3 * BC, :], rest[2 * BC:3 * BC, :], part2[2 * BC:3 * BC, :],
                                        ALU.subtract).then_inc(part3_ready[k], 1)
            elif n == 14:
                dve.wait_ge(ln_ready[k], now(i + 1))
                dve.wait_ge(decay_ready[k], now(i * NS))
                dve.wait_ge(u_ready[k], now(i * 1))
                nc.vector.scalar_tensor_tensor(delta[k][:], dtx[:], 0.0, soft[:], ALU.max, ALU.add).then_inc(delta_ready[k], 1)
            elif n == 15:
                dve.wait_ge(delta_ready[k], now(i + 1))
                dve.wait_ge(gated_ready[k], now(i + 1))
                dve.wait_ge(dbx_done[k], now(i * NS))
                nc.vector.tensor_tensor(u[k][:], delta[k][:], gated[k][:, 0:CH, :], ALU.mult).then_inc(u_ready[k], 1)

        def prepare_pool(pool, i, k, n):
            if n == 1:
                pool.wait_ge(mean[k], now(i * UPT + UPT))
                pool.wait_ge(xn_ready[1 - k], now((i + k) * UPT))
                pool.sem_inc(passed, 1)
                nc.gpsimd.tensor_scalar(veps[:], mv[:, :, 1], EPS, 1.0, ALU.add, ALU.mult).then_inc(veps_ready[k], 1)
                pool.wait_ge(veps_ready[k], now(i + 1))
                nc.gpsimd.tensor_tensor(rstd[:], veps[:], power[:], ALU.pow).then_inc(rstd_ready[k], 1)

        def core_pe(i, k, n):
            if True:
                if n == 0:
                    nc.tensor.wait_ge(part3_ready[k], now(i + 1))
                    nc.tensor.wait_ge(part2_ready[k], now(i * 2 + 2))
                if n < 2:
                    nc.tensor.wait_ge(dbx_done[1 - k], now((i + k) * NS))
                else:
                    nc.tensor.wait_ge(dbx_done[k], now(i * NS + (n - 1) * CH))
                nc.tensor.matmul(ps_b[n % 2][:], pick[0:PARTS * BC, n, :], stack[k][:], start=True, stop=True).then_inc(b_done[k], 1)
                if n == 0:
                    nc.tensor.wait_ge(c_kept[1 - k], now((i + k) * STATES))
                else:
                    nc.tensor.wait_ge(c_kept[k], now(i * STATES + n))
                nc.tensor.matmul(ps_c[:], pick[0:PARTS * BC, STATES + n, :], stack[k][:], start=True, stop=True).then_inc(c_done[k], 1)
            if n >= LAG:
                sum_pe(i, k, n - LAG)

        def sum_pe(i, k, r):
            for ch in range(CH):
                if r == 0:
                    nc.tensor.wait_ge(yd_ready[1 - k], now((i + k) * 2))
                nc.tensor.wait_ge(hc_done[k], now(i * NS + r * CH + ch + 1))
                nc.tensor.matmul(ps_y[ch][:], c["ident"][:], hc[ch][r % 2][:], start=r == 0, stop=r == STATES - 1).then_inc(y_done[k], 1)

        def core_act(act, i, k, n):
            if n == 0:
                act.wait_ge(delta_ready[k], now(i + 1))
            for ch in range(CH):
                if n < 2:
                    act.wait_ge(scan_done[1 - k], now((i + k) * NS))
                else:
                    act.wait_ge(scan_done[k], now(i * NS + (n - 2) * CH + ch + 1))
                nc.scalar.activation(decay[ch][n % 2][:], delta[k][:, ch, :], ACT.Exp, scale=aneg[:, ch, n:n + 1]).then_inc(decay_ready[k], 1)
            act.wait_ge(c_done[k], now(i * STATES + n + 1))
            if n < 2:
                act.wait_ge(hc_done[1 - k], now((i + k) * NS))
            else:
                act.wait_ge(hc_done[k], now(i * NS + (n - 1) * CH))
            nc.scalar.activation(cb[n % 2][:], ps_c[:], ACT.Copy).then_inc(c_kept[k], 1)

        def core_dve(dve, i, k, n):
            if n == 0:
                dve.wait_ge(u_ready[k], now(i + 1))
                if k == 0:
                    dve.wait_ge(hc_done[0], now(i * NS))
                dve.wait_ge(scan_done[1 - k], now((i + k) * NS))
            dve.wait_ge(b_done[k], now(i * STATES + n + 1))
            for ch in range(CH):
                if n:
                    dve.wait_ge(scan_done[k], now(i * NS + (n - 1) * CH + ch + 1))
                nc.vector.tensor_tensor(ps_d[ch][:], u[k][:, ch, :], ps_b[n % 2][:], ALU.mult).then_inc(dbx_done[k], 1)
            for ch in range(CH):
                q = n * CH + ch + 1
                dve.wait_ge(dbx_done[k], now(i * NS + q))
                dve.wait_ge(decay_ready[k], now(i * NS + q))
                if k == 0:
                    state, start = h0[ch][:, n, :], 0.0
                else:
                    if n < 2:
                        dve.wait_ge(hc_done[1], now(i * NS))
                    else:
                        dve.wait_ge(hc_done[1], now(i * NS + (n - 2) * CH + ch + 1))
                    state, start = h1[ch][:, n % 2, :], h0[ch][:, n, UNIT - 1:UNIT]
                nc.vector.tensor_tensor_scan(state, decay[ch][n % 2][:], ps_d[ch][:], start, ALU.mult, ALU.add).then_inc(scan_done[k], 1)

        def core_pool(pool, i, k, n):
            pool.wait_ge(c_kept[k], now(i * STATES + n + 1))
            for ch in range(CH):
                pool.wait_ge(scan_done[k], now(i * NS + n * CH + ch + 1))
                if n < 2:
                    pool.wait_ge(y_done[1 - k], now((i + k) * NS))
                else:
                    pool.wait_ge(y_done[k], now(i * NS + (n - 2) * CH + ch + 1))
                state = h0[ch][:, n, :] if k == 0 else h1[ch][:, n % 2, :]
                nc.gpsimd.tensor_tensor(hc[ch][n % 2][:], state, cb[n % 2][:], ALU.mult).then_inc(hc_done[k], 1)

        def finish_dve(dve, i, k):
            for ch in range(CH):
                dve.wait_ge(y_done[k], now(i * NS + NS - CH + ch + 1))
                dve.wait_ge(yg_ready[1 - k], now((i + k) * 2))
                nc.vector.scalar_tensor_tensor(yd[:, ch, :], gated[k][:, ch, :], skip[:, ch:ch + 1], ps_y[ch][:],
                                               ALU.mult, ALU.add).then_inc(yd_ready[k], 1)
            for ch in range(CH):
                dve.wait_ge(yd_ready[k], now(i * 2 + ch + 1))
                dve.wait_ge(o_done[1 - k], now(i + k))
                nc.vector.tensor_tensor(yg[:, ch, :], yd[:, ch, :], gated[k][:, CH + ch, :], ALU.mult).then_inc(yg_ready[k], 1)

        def project_out(i, k, more):
            nc.tensor.wait_ge(yg_ready[k], now(i * 2 + 2))
            if more:
                nc.tensor.wait_ge(item_free[1 - k], now((i + k + 1) * ITEMS))
            nc.tensor.wait_ge(out_ready[1 - k], now(i + k))
            for j in range(UPT):
                for ch in range(CH):
                    done = nc.tensor.matmul(ps_m[:, j * P:(j + 1) * P], yg[:, ch, j * P:(j + 1) * P], wout[:, ch, :],
                                            start=ch == 0, stop=ch == CH - 1)
            done.then_inc(o_done[k], 1)

        def add_x(dve, i, k):
            dve.wait_ge(o_done[k], now(i + 1))
            dve.wait_ge(xr_loaded[k], now(i * 16 + 16))
            dve.wait_ge(out_stored[1 - k], now((i + k) * 16))
            nc.vector.tensor_tensor(out[:].rearrange("p j d -> p (j d)"), ps_m[:], xr[:].rearrange("p j d -> p (j d)"), ALU.add).then_inc(out_ready[k], 1)

        def unit_of(t, i, k):
            return t[ds(i * T + k * UNIT, UNIT), :].rearrange("(j p) d -> p j d", p=P)

        def pe_unit(i, k, first, more):
            (pi, pk), (ni, nk) = (i - 1, 1) if k == 0 else (i, 0), after(i, k)
            for n in range(STATES):
                core_pe(i, k, n)
                if not first and n < LAG:
                    sum_pe(pi, pk, STATES - LAG + n)
                if not first and n == OUT_AT:
                    project_out(pi, pk, True)
                if more:
                    for part in AT.get(n, []):
                        prepare_pe(ni, nk, part)

        def dve_unit(dve, i, k, first, more):
            (pi, pk), (ni, nk) = (i - 1, 1) if k == 0 else (i, 0), after(i, k)
            for n in range(STATES):
                if not first and n == FINISH_AT:
                    finish_dve(dve, pi, pk)
                core_dve(dve, i, k, n)
                if not first and n == OUT_AT:
                    add_x(dve, pi, pk)
                if more:
                    for part in AT.get(n, []):
                        prepare_dve(dve, ni, nk, part)

        def act_unit(act, i, k, more):
            for n in range(STATES):
                core_act(act, i, k, n)
                if more:
                    for part in AT.get(n, []):
                        prepare_act(act, *after(i, k), part)

        def pool_unit(pool, i, k, more):
            for n in range(STATES):
                core_pool(pool, i, k, n)
                if more and n == 0:
                    prepare_pool(pool, *after(i, k), 1)

        last = B - 1
        with nc.Block() as block:
            @block.sync
            def _(sp):
                sp.dma_start(x[0][:], src[0:UNIT, :].rearrange("(j p) d -> p j d", p=P)).then_inc(x_loaded[0], 16)
                sp.dma_start(x[1][:], src[UNIT:2 * UNIT, :].rearrange("(j p) d -> p j d", p=P)).then_inc(x_loaded[1], 16)
                loads = [(win[:], a["W_in"]), (taps[:], a["conv_w"].rearrange("n o t -> o n t").broadcast_to([P, INNER, TAPS])),
                         (alog[:], a["A_log"].rearrange("(c p) n -> p c n", p=P)),
                         (wdr[:], a["W_x"][:, 0:DT_RANK].rearrange("(c p) n -> p c n", p=P)), (wdt[:], a["W_dt"]),
                         (wout[:], a["W_out"].rearrange("(c p) n -> p c n", p=P))]
                loads += [(wbc[:, :, s, :], a["W_x"][:, DT_RANK:].rearrange("(c p) n -> p c n", p=P)) for s in range(PARTS)]
                for to, what in loads:
                    sp.dma_start(to, what).then_inc(w_loaded, 16)
                for to, what in ((conv_b, "conv_b"), (dt_b, "b_dt"), (skip, "D")):
                    sp.dma_start(to[:], a[what].rearrange("(c p) -> p c", p=P), allow_slow_non_contiguous=True).then_inc(w_loaded, 16)
                with sp.Fori(0, last) as i:
                    for k in range(2):
                        if k == 0:
                            sp.wait_ge(out_ready[1], i)
                        else:
                            sp.wait_ge(out_ready[0], i + 1)
                        sp.dma_start(xr[:], unit_of(src, i, k)).then_inc(xr_loaded[k], 16)
                        sp.wait_ge(xn_ready[k], i * UPT + UPT)
                        sp.dma_start(x[k][:], unit_of(src, i + 1, k)).then_inc(x_loaded[k], 16)
                        sp.wait_ge(out_ready[k], i + 1)
                        sp.dma_start(unit_of(dst, i, k), out[:]).then_inc(out_stored[k], 16)
                for k in range(2):
                    rows = slice(last * T + k * UNIT, last * T + (k + 1) * UNIT)
                    sp.wait_ge(out_ready[1 - k], last + k)
                    sp.dma_start(xr[:], src[rows, :].rearrange("(j p) d -> p j d", p=P)).then_inc(xr_loaded[k], 16)
                    sp.wait_ge(out_ready[k], last + 1)
                    sp.dma_start(dst[rows, :].rearrange("(j p) d -> p j d", p=P), out[:]).then_inc(out_stored[k], 16)
                for k in range(2):
                    sp.wait_ge(out_stored[k], B * 16)

            @block.tensor
            def _(pe):
                prepare_pe(0, 0, 2)
                pe.wait_ge(w_ready, TAPS)
                pe.wait_ge(w_loaded, 12 * 16)
                for part in range(3, 16):
                    prepare_pe(0, 0, part)
                pe.wait_ge(filled, 7)
                pe_unit(0, 0, True, True)
                turns = Turns(pe, "ssm_pe", SCAN_STRIDES)
                with pe.Fori(0, last) as turn:
                    i = Linear(turns, turn)
                    pe_unit(i, 1, False, True)
                    pe_unit(i + 1, 0, False, True)
                    turns.step()
                pe_unit(last, 1, False, False)
                for r in range(STATES - LAG, STATES):
                    sum_pe(last, 1, r)
                project_out(last, 1, False)

            @block.vector
            def _(dve):
                nc.vector.memset(xnT[0][:, 0:TAPS - 1], 0.0).then_inc(filled, 1)
                for part in (0, 1):
                    prepare_dve(dve, 0, 0, part)
                dve.wait_ge(w_loaded, 12 * 16)
                for tap in range(TAPS):
                    nc.vector.tensor_tensor(wconv[:, tap, :], win[:, 0:INNER], taps[:, :, tap], ALU.mult).then_inc(w_ready, 1)
                dve.wait_ge(a_ready, 1)
                nc.vector.tensor_scalar(aneg[:], aneg[:], -1.0, None, ALU.mult).then_inc(a_ready, 1)
                for part in range(2, 16):
                    prepare_dve(dve, 0, 0, part)
                dve_unit(dve, 0, 0, True, True)
                turns = Turns(dve, "ssm_dve", SCAN_STRIDES)
                with dve.Fori(0, last) as turn:
                    i = Linear(turns, turn)
                    dve_unit(dve, i, 1, False, True)
                    dve_unit(dve, i + 1, 0, False, True)
                    turns.step()
                dve_unit(dve, last, 1, False, False)
                finish_dve(dve, last, 1)
                add_x(dve, last, 1)

            @block.scalar
            def _(act):
                act.wait_ge(w_loaded, 12 * 16)
                nc.scalar.activation(aneg[:], alog[:], ACT.Exp).then_inc(a_ready, 1)
                act.wait_ge(a_ready, 2)
                for part in range(16):
                    prepare_act(act, 0, 0, part)
                act_unit(act, 0, 0, True)
                turns = Turns(act, "ssm_act", SCAN_STRIDES)
                with act.Fori(0, last) as turn:
                    i = Linear(turns, turn)
                    act_unit(act, i, 1, True)
                    act_unit(act, i + 1, 0, True)
                    turns.step()
                act_unit(act, last, 1, False)

            @block.gpsimd
            def _(pool):
                nc.gpsimd.memset(power[:], -0.5).then_inc(filled, 1)
                nc.gpsimd.memset(pick[:], 0.0).then_inc(filled, 1)
                pool.wait_ge(filled, 3)
                prepare_pool(pool, 0, 0, 1)
                for s in range(PARTS):
                    nc.gpsimd.affine_select(out=pick[:], in_=pick[:], compare_op=ALU.not_equal, fill=1.0, base=-BC * s,
                                            pattern=[[-1, BC], [0, P]], channel_multiplier=1).then_inc(filled, 1)
                    pool.wait_ge(filled, 4 + s)
                pool.sem_inc(filled, 1)
                pool_unit(pool, 0, 0, True)
                turns = Turns(pool, "ssm_pool", SCAN_STRIDES)
                with pool.Fori(0, last) as turn:
                    i = Linear(turns, turn)
                    pool_unit(pool, i, 1, True)
                    pool_unit(pool, i + 1, 0, True)
                    turns.step()
                pool_unit(pool, last, 1, False)
        m.clear()


def build(nc, x, w_attn, b_attn, w_k2, b_k2, w_proj, b_proj, W_in, conv_w, conv_b, W_x, W_dt, b_dt, A_log, D_skip, W_out,
          sw1, sw2, sw3, ew1, ew2, ew3, rw, rb, y):
    rows = x.rearrange("b t d -> (b t) d")

    def scratch(name, shape, dt=F32):
        return nc.dram_tensor(name, shape, dt).ap()

    dram = {"xn": scratch("xn_dram", (N + 1, D)), "vp": scratch("vp_dram", (N, HEADS * (HD + 1))),
            "fT": scratch("fT_dram", (2, P, N)), "parts": scratch("parts_dram", (4 * PARTS, B, P, T), BF16),
            "yar": scratch("yar_dram", (16, T, 32)), "x1": scratch("x1_dram", (N, D))}
    x2, x3 = scratch("x2_dram", (N, D)), scratch("x3_dram", (N, D))
    experts = {"sw1": sw1, "sw2": sw2, "sw3": sw3, "ew1": ew1, "ew2": ew2, "ew3": ew3, "rw": rw, "rb": rb}
    with ExitStack() as ctx:
        m = Mem(nc, ctx, "const")
        c = constants(nc, m, dram)
        routing_scratch(nc, m, dram, ("ffn1", "ffn2"))
        project(nc, dram, c, {"x": rows, "w_attn": w_attn, "b_attn": b_attn, "w_k2": w_k2, "b_k2": b_k2})
        attention(nc, dram, c)
        memory(nc, dram, c, {"x": rows, "w_proj": w_proj, "b_proj": b_proj})
        ffn(nc, dram, c, experts, "ffn1", dram["x1"], x2)
        scan(nc, dram, c, {"W_in": W_in, "conv_w": conv_w, "conv_b": conv_b, "W_x": W_x, "W_dt": W_dt, "b_dt": b_dt,
                           "A_log": A_log, "D": D_skip, "W_out": W_out}, x2, x3)
        ffn(nc, dram, c, experts, "ffn2", x3, y.rearrange("b t d -> (b t) d"))


_INS = ["L0_attn_a_x", "L0_attn_a_w_attn", "L0_attn_a_b_attn", "L0_attn_a_w_k2", "L0_attn_a_b_k2", "L0_attn_a_w_proj",
        "L0_attn_a_b_proj", "L0_attn_b_W_in", "L0_attn_b_conv_w", "L0_attn_b_conv_b", "L0_attn_b_W_x", "L0_attn_b_W_dt",
        "L0_attn_b_b_dt", "L0_attn_b_A_log", "L0_attn_b_D", "L0_attn_b_W_out", "L0_ffn_sw1", "L0_ffn_sw2", "L0_ffn_sw3",
        "L0_ffn_ew1", "L0_ffn_ew2", "L0_ffn_ew3", "L0_ffn_rw", "L0_ffn_rb"]
_OUTS = [((4, 1024, 128), "float32")]


def kernel(**inputs):
    import numpy as _np
    import concourse.bacc as _bacc
    from concourse import mybir as _mybir
    from concourse.bass_utils import run_bass_kernel_spmd as _run

    nc = _bacc.Bacc("TRN2", target_bir_lowering=False, num_devices=1)
    arrays, args = {}, []
    for name in _INS:
        a = _np.ascontiguousarray(inputs[name])
        arrays[f"in_{name}_dram"] = a
        args.append(nc.dram_tensor(f"in_{name}_dram", a.shape, _mybir.dt.from_np(a.dtype), kind="ExternalInput").ap())
    for i, (shape, dtype) in enumerate(_OUTS):
        dt = _mybir.dt.from_np(_np.dtype(dtype))
        args.append(nc.dram_tensor(f"out_{i}_dram", shape, dt, kind="ExternalOutput").ap())
    build(nc, *args)
    r = _run(nc, [arrays], core_ids=[0])
    return r.results[0]["out_0_dram"]
```
